# Optimizing a Trainium2 kernel written in Bass

```python
import numpy as np
import jax
import jax.numpy as jnp

def _softmax(x, axis=-1):
    return jax.nn.softmax(x, axis=axis)

def _gelu(x):
    return jax.nn.gelu(x, approximate=True)

def _silu(x):
    return jax.nn.silu(x)

def _sigmoid(x):
    return jax.nn.sigmoid(x)

def _layernorm(x, axis=-1, eps=1e-05):
    m = jnp.mean(x, axis=axis, keepdims=True)
    v = jnp.var(x, axis=axis, keepdims=True)
    return (x - m) / jnp.sqrt(v + eps)

def _scatter_add(tgt, idx, src, axis=0):
    return tgt.at[idx].add(src)

def _segment_sum(src, seg, n):
    return jax.ops.segment_sum(src, seg, n)
kernel_name = 'mk_perceiver_d1_seqx_r2_db2112'

def setup_inputs(seed: int=0):
    np.random.seed(seed)
    _w = jnp.asarray

    def _rec_inputs():
        import jax
        import jax.numpy as jnp
        _rk = jax.random.key(seed)
        x = -0.0002928 + 1 * jax.random.normal(jax.random.fold_in(_rk, 1), (8, 128, 512), jnp.float32)
        _lenS = 128 - jax.random.randint(jax.random.fold_in(_rk, 7), (8,), 0, max(1, 128 // 4) + 1, jnp.int32)
        _lenS2 = 2048 - jax.random.randint(jax.random.fold_in(_rk, 8), (8,), 0, max(1, 2048 // 4) + 1, jnp.int32)
        _ctx_1024P = jax.random.normal(jax.random.fold_in(_rk, 11), (8, 16, 512), jnp.float32)
        _ctx_1024c = jax.random.dirichlet(jax.random.fold_in(_rk, 511), 0.3 * jnp.ones((16,), jnp.float32), (8, 2048))
        _ctx_1024t = jnp.einsum('bsk,bkd->bsd', _ctx_1024c, _ctx_1024P)
        _ctx_1024t = _ctx_1024t * jax.lax.rsqrt(jnp.mean(jnp.square(_ctx_1024t)) + 1e-12) * 0.953939
        ctx_1024 = -1.39393e-06 + 0.999914 * (_ctx_1024t + 0.3 * jax.random.normal(jax.random.fold_in(_rk, 611), (8, 2048, 512), jnp.float32))
        return (x, ctx_1024)
    x, ctx_1024 = _rec_inputs()

    def _L0_xattn_setup():
        import jax, jax.numpy as jnp
        import numpy as np
        B, T, S, D, H, DK = (2, 1024, 1024, 512, 16, 64)
        key = jax.random.key(seed)
        ks = jax.random.split(key, 11)
        s = 1.0 / np.sqrt(D)
        return {'query': jax.random.normal(ks[0], (B, T, D), jnp.float32), 'value': jax.random.normal(ks[1], (B, S, D), jnp.float32), 'key': jax.random.normal(ks[2], (B, S, D), jnp.float32), 'Wq': jax.random.normal(ks[3], (D, H, DK), jnp.float32) * s, 'bq': jnp.zeros((H, DK), jnp.float32), 'Wk': jax.random.normal(ks[4], (D, H, DK), jnp.float32) * s, 'bk': jnp.zeros((H, DK), jnp.float32), 'Wv': jax.random.normal(ks[5], (D, H, DK), jnp.float32) * s, 'bv': jnp.zeros((H, DK), jnp.float32), 'Wo': jax.random.normal(ks[6], (H, DK, D), jnp.float32) * (1.0 / np.sqrt(H * DK)), 'bo': jnp.zeros((D,), jnp.float32)}
    _L0_xattn_all = _L0_xattn_setup()
    _L0_xattn_in = {k: v for k, v in _L0_xattn_all.items() if k in ('Wq', 'bq', 'Wk', 'bk', 'Wv', 'bv', 'Wo', 'bo')}
    del _L0_xattn_all

    def _L0_attn_setup():
        import jax, jax.numpy as jnp
        import numpy as np
        from jax.scipy.special import logsumexp
        B, L, E = (2, 512, 512)
        H, D = (8, 64)
        N_ITERS = 20
        key = jax.random.key(seed)
        ks = jax.random.split(key, 5)
        s_in = 1.0 / np.sqrt(E)
        s_out = 1.0 / np.sqrt(H * D)
        return {'x': jax.random.normal(ks[0], (B, L, E), jnp.float32), 'Wq': jax.random.normal(ks[1], (E, H * D), jnp.float32) * s_in, 'bq': jnp.zeros((H * D,), jnp.float32), 'Wk': jax.random.normal(ks[2], (E, H * D), jnp.float32) * s_in, 'bk': jnp.zeros((H * D,), jnp.float32), 'Wv': jax.random.normal(ks[3], (E, H * D), jnp.float32) * s_in, 'bv': jnp.zeros((H * D,), jnp.float32), 'Wo': jax.random.normal(ks[4], (H * D, E), jnp.float32) * s_out, 'bo': jnp.zeros((E,), jnp.float32)}
    _L0_attn_all = _L0_attn_setup()
    _L0_attn_in = {k: v for k, v in _L0_attn_all.items() if k in ('Wq', 'bq', 'Wk', 'bk', 'Wv', 'bv', 'Wo', 'bo')}
    del _L0_attn_all

    def _L0_ffn_setup():
        import jax, jax.numpy as jnp
        import numpy as np
        CAPACITY_FACTOR = 1.25
        key = jax.random.key(seed)
        k1, k2, k3, k4 = jax.random.split(key, 4)
        B, T, D, F, E = (4, 2048, 512, 2048, 8)
        s = 0.02
        return {'x': jax.random.normal(k1, (B, T, D), dtype=jnp.float32), 'wg': jax.random.normal(k2, (D, E), dtype=jnp.float32) * s, 'W1': jax.random.normal(k3, (E, D, F), dtype=jnp.float32) * s, 'b1': jnp.zeros((E, F), dtype=jnp.float32), 'W2': jax.random.normal(k4, (E, F, D), dtype=jnp.float32) * s, 'b2': jnp.zeros((E, D), dtype=jnp.float32)}
    _L0_ffn_all = _L0_ffn_setup()
    _L0_ffn_in = {k: v for k, v in _L0_ffn_all.items() if k in ('wg', 'W1', 'b1', 'W2', 'b2')}
    del _L0_ffn_all
    return {'x': x, 'ctx_1024': ctx_1024, 'L0_xattn_Wq': _L0_xattn_in['Wq'], 'L0_xattn_bq': _L0_xattn_in['bq'], 'L0_xattn_Wk': _L0_xattn_in['Wk'], 'L0_xattn_bk': _L0_xattn_in['bk'], 'L0_xattn_Wv': _L0_xattn_in['Wv'], 'L0_xattn_bv': _L0_xattn_in['bv'], 'L0_xattn_Wo': _L0_xattn_in['Wo'], 'L0_xattn_bo': _L0_xattn_in['bo'], 'L0_attn_Wq': _L0_attn_in['Wq'], 'L0_attn_bq': _L0_attn_in['bq'], 'L0_attn_Wk': _L0_attn_in['Wk'], 'L0_attn_bk': _L0_attn_in['bk'], 'L0_attn_Wv': _L0_attn_in['Wv'], 'L0_attn_bv': _L0_attn_in['bv'], 'L0_attn_Wo': _L0_attn_in['Wo'], 'L0_attn_bo': _L0_attn_in['bo'], 'L0_ffn_wg': _L0_ffn_in['wg'], 'L0_ffn_W1': _L0_ffn_in['W1'], 'L0_ffn_b1': _L0_ffn_in['b1'], 'L0_ffn_W2': _L0_ffn_in['W2'], 'L0_ffn_b2': _L0_ffn_in['b2']}

def reference(x, ctx_1024, L0_xattn_Wq, L0_xattn_bq, L0_xattn_Wk, L0_xattn_bk, L0_xattn_Wv, L0_xattn_bv, L0_xattn_Wo, L0_xattn_bo, L0_attn_Wq, L0_attn_bq, L0_attn_Wk, L0_attn_bk, L0_attn_Wv, L0_attn_bv, L0_attn_Wo, L0_attn_bo, L0_ffn_wg, L0_ffn_W1, L0_ffn_b1, L0_ffn_W2, L0_ffn_b2):
    import jax
    import jax.numpy as jnp

    def _L0_xattn_ref(query, value, key, Wq, bq, Wk, bk, Wv, bv, Wo, bo):
        import jax, jax.numpy as jnp
        import numpy as np
        B, T, S, D, H, DK = (2, 1024, 1024, 512, 16, 64)
        q = jnp.einsum('btd,dhk->bthk', query, Wq) + bq
        k = jnp.einsum('bsd,dhk->bshk', key, Wk) + bk
        v = jnp.einsum('bsd,dhk->bshk', value, Wv) + bv
        q = q * (1.0 / np.sqrt(DK)).astype(np.float32)
        scores = jnp.einsum('bshk,bthk->bhts', k, q)
        probs = jax.nn.softmax(scores, axis=-1)
        attn = jnp.einsum('bhts,bshk->bthk', probs, v)
        out = jnp.einsum('bthk,hkd->btd', attn, Wo) + bo
        return out

    def _L0_attn_ref(x, Wq, bq, Wk, bk, Wv, bv, Wo, bo):
        import jax, jax.numpy as jnp
        import numpy as np
        from jax.scipy.special import logsumexp
        B, L, E = (2, 512, 512)
        H, D = (8, 64)
        N_ITERS = 20
        b, l, e = x.shape

        def proj(W, bias):
            return (x @ W + bias).reshape(b, l, H, D).transpose(0, 2, 1, 3)
        q, k, v = (proj(Wq, bq), proj(Wk, bk), proj(Wv, bv))
        logits = jnp.einsum('bhqd,bhkd->bhqk', q, k) / jnp.sqrt(jnp.float32(D))

        def body(_, la):
            la = la - logsumexp(la, axis=-1, keepdims=True)
            la = la - logsumexp(la, axis=-2, keepdims=True)
            return la
        log_alpha = jax.lax.fori_loop(0, N_ITERS, body, logits)
        attn = jnp.exp(log_alpha)
        out = jnp.einsum('bhqk,bhkd->bhqd', attn, v)
        out = out.transpose(0, 2, 1, 3).reshape(b, l, H * D)
        return out @ Wo + bo

    def _L0_ffn_ref(x, wg, W1, b1, W2, b2):
        import jax, jax.numpy as jnp
        import numpy as np
        CAPACITY_FACTOR = 1.25
        B, T, D = x.shape
        E = wg.shape[1]
        N = B * T
        capacity = int(N / E * CAPACITY_FACTOR) + 1
        xf = x.reshape(N, D)
        logits = xf @ wg
        scores = jax.nn.softmax(logits, axis=-1)
        top1 = jnp.argmax(scores, axis=-1)
        combine_w = jnp.take_along_axis(scores, top1[:, None], axis=1)[:, 0]
        oh = jax.nn.one_hot(top1, E, dtype=jnp.int32)
        rank = jnp.take_along_axis(jnp.cumsum(oh, axis=0), top1[:, None], axis=1)[:, 0] - 1
        valid = rank < capacity
        trash = E * capacity
        slot = jnp.where(valid, top1 * capacity + rank, trash)
        buf = jnp.zeros((E * capacity + 1, D), dtype=x.dtype).at[slot].set(xf)
        eb = buf[:E * capacity].reshape(E, capacity, D)
        h = jax.nn.gelu(jnp.einsum('ecd,edf->ecf', eb, W1) + b1[:, None, :], approximate=False)
        y = jnp.einsum('ecf,efd->ecd', h, W2) + b2[:, None, :]
        yf = y.reshape(E * capacity, D)
        gathered = yf[jnp.minimum(slot, E * capacity - 1)]
        out_flat = jnp.where(valid[:, None], gathered, 0.0) * combine_w[:, None]
        return out_flat.reshape(B, T, D)
    x = x + _L0_xattn_ref(_layernorm(x, axis=-1), ctx_1024, ctx_1024, L0_xattn_Wq, L0_xattn_bq, L0_xattn_Wk, L0_xattn_bk, L0_xattn_Wv, L0_xattn_bv, L0_xattn_Wo, L0_xattn_bo)
    x = x + _L0_attn_ref(_layernorm(x, axis=-1), L0_attn_Wq, L0_attn_bq, L0_attn_Wk, L0_attn_bk, L0_attn_Wv, L0_attn_bv, L0_attn_Wo, L0_attn_bo)
    x = x + _L0_ffn_ref(_layernorm(x, axis=-1), L0_ffn_wg, L0_ffn_W1, L0_ffn_b1, L0_ffn_W2, L0_ffn_b2)
    return x

_drawn_inputs = setup_inputs


def setup_inputs(seed=0):
    import zlib

    import numpy as np

    out = dict(_drawn_inputs(seed))
    spreads = {'L0_xattn_bq': (0.0, 0.328),
     'L0_xattn_bk': (0.0, 0.8),
     'L0_xattn_bv': (0.0, 0.1),
     'L0_xattn_bo': (0.0, 0.1),
     'L0_attn_bq': (0.0, 0.8),
     'L0_attn_bk': (0.0, 0.8),
     'L0_attn_bv': (0.0, 0.1),
     'L0_attn_bo': (0.0, 0.1),
     'L0_ffn_b1': (0.0, 0.8),
     'L0_ffn_b2': (0.0, 0.432)}
    factors = {}
    for name, (base, spread) in spreads.items():
        noise = np.random.default_rng([zlib.crc32(name.encode()), seed]).standard_normal(out[name].shape)
        drawn = base * np.exp(spread * noise) if base else spread * noise
        out[name] = jnp.asarray(drawn.astype(out[name].dtype))
    for name, factor in factors.items():
        out[name] = (out[name] * factor).astype(out[name].dtype)
    return out
```

```python
import concourse.bass as bass
from concourse import mybir
from contextlib import ExitStack

F32 = mybir.dt.float32
F32R = mybir.dt.float32r
I32 = mybir.dt.int32
U32 = mybir.dt.uint32
ALU = mybir.AluOpType
ACT = mybir.ActivationFunctionType
AX = mybir.AxisListType

P = 128
B = 8
D = 512
DT = D // P
TOK = B * P
S = 2048
ST = S // P
XH, DK = 16, 64
XG = 4
NCH = S // 512
EPS = 1e-5


def new_semaphore(nc, name, used):
    used.append(nc.alloc_semaphore(name))
    return used[-1]


def cross_attention(nc, ctx, wk_split, wv_split, q_split, bk, ident, o_parts, row_scale, used, batches=B):
    NS = 4
    PIECES = 16 * XG
    FIRST_CTX = 47
    PRO = ST + 16
    PER = PIECES + ST

    def fill_no(m, last=False):
        return m if last else m + 2 * min(max(m - FIRST_CTX + 1, 0), ST // 2)

    def ctx_no(u):
        return FIRST_CTX + 3 * (u // 2) + u % 2

    es = ExitStack()
    with es:
        sb = lambda n, s, d: es.enter_context(nc.sbuf_tensor(n, s, d))
        ps = lambda n, s, d: es.enter_context(nc.psum_tensor(n, s, d))
        sem = lambda n: new_semaphore(nc, n, used)
        stage = sb("ctx_stage", [P, NS, D], F32)
        ctx_hi = sb("ctxT_hi", [P, DT, S], F32R)
        ctx_lo = sb("ctxT_lo", [P, DT, S], F32R)
        wk = sb("wk_pairs", [P, 2, 2, DT, P], F32R)
        wv = sb("wv_group", [P, 2, DT, 256], F32R)
        keys = sb("keys", [P, XG, S], F32R)
        values = sb("values", [P, 2, ST, 4, 2 * DK], F32R)
        q = sb("q", [P, 4, 2, P], F32R)
        probs = sb("probs", [P, S], F32)
        probsT = sb("probsT", [P, 2, 4, 2, P], F32R)
        bk_sb = sb("bk", [DK, XH], F32)
        neg_max = sb("neg_max", [P, 2], F32)
        sums = sb("sums", [P, XH, NCH], F32)
        total = sb("total", [P, XH], F32)
        scale = sb("scale", [P, XH], F32)
        o_copy = sb("o_copy", [P, 2 * P], F32)
        o_half = sb("o_half", [P, 2, P], F32)
        pS = ps("scores", [P, S], F32)
        pJ = ps("fills", [P, 2, 512], F32)
        pT = ps("probsT_ps", [P, 4, P], F32)
        pO = ps("o_ps", [P, 512], F32)

        bias_in = sem("bias_in")
        ctx_in = [sem(f"ctx_in{n}") for n in range(NS)]
        wk_in = [sem("wk_in0"), sem("wk_in1")]
        wv_in = sem("wv_in")
        q_in = [sem(f"q_in{i}") for i in range(4)]
        o_out = [sem("o_out0"), sem("o_out1")]
        scale_out = sem("scale_out")
        filled = sem("filled")
        fill_hi = sem("fill_hi")
        fill_lo = sem("fill_lo")
        scored = sem("scored")
        maxed = sem("maxed")
        exped = sem("exped")
        transposed = sem("transposed")
        pt_hi = sem("pt_hi")
        pt_lo = sem("pt_lo")
        weighed = sem("weighed")
        o_copied = sem("o_copied")
        o_added = sem("o_added")
        totalled = sem("totalled")
        scaled = sem("scaled")

        block = es.enter_context(nc.Block())

        def q_load(sp, b, g, i):
            for u in range(2):
                sp.dma_start(q[64 * u:64 * u + 64, i, :, :].bitcast(F32),
                             q_split[bass.ds((4 * g + i) * DK, DK), b, :, :]).then_inc(q_in[i], 16)

        def wv_load(sp, g):
            for n in range(2):
                sp.dma_start(wv[:, n, :, :].bitcast(F32), wv_split[n, :, :, 256 * g:256 * g + 256]).then_inc(wv_in, 16)

        def wk_load(sp, g, p):
            c = 256 * g + 128 * p
            for n in range(2):
                sp.dma_start(wk[:, p, n, :, :].bitcast(F32), wk_split[n, :, :, c:c + P]).then_inc(wk_in[p], 16)

        def ctx_load(sp, b, u):
            sp.dma_start(stage[:, u % NS, :], ctx[b, P * u:P * u + P, :]).then_inc(ctx_in[u % NS], 16)

        @block.sync
        def _(sp):
            def batch(b, last):
                if not last:
                    for u in range(NS):
                        ctx_load(sp, b + 1, u)
                for g in range(XG):
                    more = not (last and g == XG - 1)
                    for i in range(4):
                        h = 4 * g + i
                        for j in range(4):
                            k = 16 * g + 4 * i + j - FIRST_CTX
                            if not last and 0 <= k < (ST - NS) // 2:
                                sp.wait_ge(filled, PRO + PER * b + ctx_no(2 * k + 1) + 1)
                                ctx_load(sp, b + 1, 2 * k + NS)
                                ctx_load(sp, b + 1, 2 * k + NS + 1)
                            if j == 1 and h > 0:
                                o_store(b, h - 1)
                            if j == 1 and more:
                                sp.wait_ge(scored, 16 * b + h + 1)
                                q_load(sp, b + 1 if g == 3 else b, (g + 1) % XG, i)
                        if i and not (last and g >= 2):
                            sp.wait_ge(filled, PRO + PER * b + fill_no(16 * g + 4 * i + 3) + 1)
                            if i == 1:
                                wv_load(sp, (g + 2) % XG)
                            else:
                                wk_load(sp, (g + 2) % XG, i - 2)
                o_store(b, XH - 1)
                sp.wait_ge(scaled, 16 * b + 16)
                with nc.allow_non_contiguous_dma(reason="one number per token and head"):
                    sp.dma_start(row_scale[b, :, :], scale[:, :]).then_inc(scale_out, 16)

            def o_store(b, h):
                sp.wait_ge(o_added, 16 * b + h + 2)
                sp.dma_start(o_parts[b, h, :, :], o_half[:, h % 2, :]).then_inc(o_out[h % 2], 16)

            with nc.allow_non_contiguous_dma(reason="the bias, once"):
                sp.dma_start(bk_sb[:, :], bk.rearrange("h k -> k h")).then_inc(bias_in, 16)
            for u in range(NS):
                ctx_load(sp, 0, u)
            wv_load(sp, 0)
            wk_load(sp, 0, 0)
            wk_load(sp, 0, 1)
            for i in range(4):
                q_load(sp, 0, 0, i)
            for u in range(NS, ST):
                sp.wait_ge(filled, u - NS + 1)
                ctx_load(sp, 0, u)
            sp.wait_ge(filled, ST + 8)
            wv_load(sp, 1)
            sp.wait_ge(filled, ST + 12)
            wk_load(sp, 1, 0)
            sp.wait_ge(filled, ST + 16)
            wk_load(sp, 1, 1)
            if batches > 1:
                with sp.Fori(0, batches - 1) as b:
                    batch(b, False)
            batch(batches - 1, True)
            for n in range(2):
                sp.wait_ge(o_out[n], 16 * 8 * batches + 16)
            sp.wait_ge(scale_out, 16 * batches + 16)

        @block.tensor
        def _(pe):
            def ctx_fill(no, b, u):
                pe.wait_ge(ctx_in[u % NS], 16 * (ST // NS * b + u // NS + 1))
                pe.wait_ge(fill_lo, no - 1)
                for t in range(DT):
                    last = nc.tensor.transpose(pJ[:, bank[0], P * t:P * t + P],
                                               stage[:, u % NS, P * t:P * t + P], ident[:, :])
                last.then_inc(filled, 1)

            def v_fill(seq, j, i):
                for k in range(2):
                    s = P * (2 * (4 * i + j) + k)
                    for t in range(DT):
                        for n, (c, w) in enumerate(((ctx_hi, 0), (ctx_lo, 0), (ctx_hi, 1))):
                            last = nc.tensor.matmul(pJ[:, bank[0], 256 * k:256 * k + 256], c[:, t, s:s + P],
                                                    wv[:, w, t, :], start=t + n == 0, stop=t == DT - 1 and n == 2)
                last.then_inc(filled, 1)

            def k_fill(p, j):
                for t in range(DT):
                    for n, (w, c) in enumerate(((0, ctx_hi), (0, ctx_lo), (1, ctx_hi))):
                        last = nc.tensor.matmul(pJ[:, bank[0], :], wk[:, p, w, t, :], c[:, t, 512 * j:512 * j + 512],
                                                start=t + n == 0, stop=t == DT - 1 and n == 2)
                last.then_inc(filled, 1)

            bank = [0]

            def fill(no, seq, i, j):
                if j == 0 and i == 0:
                    pe.wait_ge(wv_in, 32 * seq + 32)
                if j == 0 and i >= 2:
                    pe.wait_ge(wk_in[i - 2], 32 * seq + 32)
                pe.wait_ge(fill_lo, no - 1)
                if i < 2:
                    v_fill(seq, j, i)
                else:
                    k_fill(i - 2, j)

            def score(b, h, last=False):
                g, i = h // 4, h % 4
                pe.wait_ge(q_in[i], 128 * b + 32 * (g + 1))
                pe.wait_ge(fill_lo, PER * b + (28 + 4 * (i // 2) if g == 0 else
                                               PRO + fill_no(16 * g - 16 + 11 + 4 * (i // 2), last) + 1))
                if h or not first[0]:
                    pe.wait_ge(exped, 64 * b + 4 * h)
                for c in range(NCH):
                    for n in range(2):
                        last = nc.tensor.matmul(pS[:, 512 * c:512 * c + 512], q[:, i, n, :],
                                                keys[:, i, 512 * c:512 * c + 512], start=n == 0, stop=n == 1)
                last.then_inc(scored, 1)

            def transpose(b, h, j):
                pe.wait_ge(exped, 64 * b + 4 * h + j + 1)
                if h or j:
                    pe.wait_ge(pt_lo, 64 * b + 4 * h + j)
                for k in range(4):
                    last = nc.tensor.transpose(pT[:, k, :], probs[:, P * (4 * j + k):P * (4 * j + k) + P], ident[:, :])
                last.then_inc(transposed, 1)

            def weigh(b, h, j):
                g, i = h // 4, h % 4
                pe.wait_ge(pt_lo, 64 * b + 4 * h + j + 1)
                if j == 0:
                    pe.wait_ge(o_copied, 16 * b + h + 1)
                    pe.wait_ge(fill_lo, PER * b + (24 if g == 0 else PRO + fill_no(16 * g - 16 + 7) + 1))
                for k in range(4):
                    s = 4 * j + k
                    last = nc.tensor.matmul(pO[:, 0:2 * P], values[:, g % 2, s, i, :],
                                            probsT[:, j % 2, k, :, :].rearrange("p n t -> p (n t)"),
                                            start=s == 0, stop=s == ST - 1)
                last.then_inc(weighed, 1)

            first = [True]

            def batch(b, last):
                for g in range(XG):
                    more = not (last and g == XG - 1)
                    for i in range(4):
                        h = 4 * g + i
                        for j in range(4):
                            m = 16 * g + 4 * i + j
                            k = m - FIRST_CTX
                            turn = not last and 0 <= k < ST // 2
                            if turn:
                                bank[0] = ctx_no(2 * k) % 2
                                ctx_fill(PRO + PER * b + ctx_no(2 * k), b + 1, 2 * k)
                            if j:
                                weigh(b, h, j - 1)
                            elif h:
                                weigh(b, h - 1, 3)
                            transpose(b, h, j)
                            if j == 1 and (more or i < 3):
                                score(b, h + 1, last)
                            if turn:
                                bank[0] = ctx_no(2 * k + 1) % 2
                                ctx_fill(PRO + PER * b + ctx_no(2 * k + 1), b + 1, 2 * k + 1)
                            if more:
                                bank[0] = fill_no(m) % 2
                                fill(PRO + PER * b + fill_no(m, last), 4 * b + g + 1, i, j)
                weigh(b, XH - 1, 3)

            for u in range(ST):
                bank[0] = u % 2
                if u >= 2:
                    ctx_fill(u, 0, u)
                else:
                    pe.wait_ge(ctx_in[u], 16)
                    for t in range(DT):
                        last = nc.tensor.transpose(pJ[:, u, P * t:P * t + P], stage[:, u, P * t:P * t + P], ident[:, :])
                    last.then_inc(filled, 1)
            for m in range(16):
                bank[0] = m % 2
                fill(ST + m, 0, m // 4, m % 4)
            score(0, 0)
            first[0] = False
            if batches > 1:
                with pe.Fori(0, batches - 1) as b:
                    batch(b, False)
            batch(batches - 1, True)

        @block.scalar
        def _(act):
            def fill_hi_ctx(no, bk_, u):
                act.wait_ge(filled, no + 1)
                nc.scalar.copy(ctx_hi[:, :, P * u:P * u + P],
                               pJ[:, bk_, :].rearrange("p (t s) -> p t s", t=DT)).then_inc(fill_hi, 1)

            def fill_hi_vk(no, bk_, g, i, j):
                act.wait_ge(filled, no + 1)
                if i < 2:
                    n = 2 * (4 * i + j)
                    nc.scalar.copy(values[:, g % 2, n:n + 2, :, 0:DK],
                                   pJ[:, bk_, :].rearrange("p (s h k) -> p s h k", s=2, h=4)).then_inc(fill_hi, 1)
                    return
                for a in range(2):
                    x = 2 * (i - 2) + a
                    last = nc.scalar.activation(keys[0:DK, x, 512 * j:512 * j + 512], pJ[DK * a:DK * a + DK, bk_, :],
                                                ACT.Identity, bias=bk_sb[:, 4 * g + x:4 * g + x + 1])
                last.then_inc(fill_hi, 1)

            def exp(b, h, c):
                act.wait_ge(maxed, 16 * b + h + 1)
                if h:
                    act.wait_ge(transposed, 64 * b + 4 * (h - 1) + c + 1)
                nc.scalar.activation(probs[:, 512 * c:512 * c + 512], pS[:, 512 * c:512 * c + 512], ACT.Exp,
                                     bias=neg_max[:, h % 2:h % 2 + 1],
                                     accum_out=sums[:, h % XH, c:c + 1]).then_inc(exped, 1)

            def copy_o(b, h):
                act.wait_ge(weighed, 64 * b + 4 * h + 4)
                act.wait_ge(o_added, 16 * b + h + 1)
                nc.scalar.copy(o_copy[:, :], pO[:, 0:2 * P]).then_inc(o_copied, 1)

            def batch(b, last):
                for g in range(XG):
                    more = not (last and g == XG - 1)
                    for i in range(4):
                        h = 4 * g + i
                        for j in range(4):
                            m = 16 * g + 4 * i + j
                            k = m - FIRST_CTX
                            turn = not last and 0 <= k < ST // 2
                            if turn:
                                fill_hi_ctx(PRO + PER * b + ctx_no(2 * k), ctx_no(2 * k) % 2, 2 * k)
                            act.wait_ge(transposed, 64 * b + 4 * h + j + 1)
                            if h or j > 1:
                                act.wait_ge(weighed, 64 * b + 4 * h + j - 1)
                            nc.scalar.copy(probsT[:, j % 2, :, 0, :], pT[:, :, :]).then_inc(pt_hi, 1)
                            if j == 0 and h:
                                copy_o(b, h - 1)
                            if turn:
                                fill_hi_ctx(PRO + PER * b + ctx_no(2 * k + 1), ctx_no(2 * k + 1) % 2, 2 * k + 1)
                            if j >= 2 and (more or i < 3):
                                exp(b, h + 1, 2 * j - 4)
                                exp(b, h + 1, 2 * j - 3)
                            if more:
                                if g and i < 2 and j == 0:
                                    act.wait_ge(weighed, 64 * b + 16 * g)
                                if i >= 2 and j == 0:
                                    act.wait_ge(scored, 16 * b + 4 * g + 2 * (i - 2) + 2)
                                fill_hi_vk(PRO + PER * b + fill_no(m, last), fill_no(m) % 2, (g + 1) % XG, i, j)
                copy_o(b, XH - 1)

            act.sem_inc(o_copied, 1)
            act.wait_ge(bias_in, 16)
            for u in range(ST):
                fill_hi_ctx(u, u % 2, u)
            for m in range(16):
                fill_hi_vk(ST + m, m % 2, 0, m // 4, m % 4)
            for c in range(NCH):
                exp(0, 0, c)
            if batches > 1:
                with act.Fori(0, batches - 1) as b:
                    batch(b, False)
            batch(batches - 1, True)

        @block.vector
        def _(dve):
            def fill_lo_ctx(no, bk_, u):
                dve.wait_ge(fill_hi, no + 1)
                nc.vector.tensor_tensor(ctx_lo[:, :, P * u:P * u + P],
                                        pJ[:, bk_, :].rearrange("p (t s) -> p t s", t=DT),
                                        ctx_hi[:, :, P * u:P * u + P].bitcast(F32), ALU.subtract).then_inc(fill_lo, 1)

            def fill_lo_vk(no, bk_, g, i, j):
                dve.wait_ge(fill_hi, no + 1)
                if i < 2:
                    n = 2 * (4 * i + j)
                    nc.vector.tensor_tensor(values[:, g % 2, n:n + 2, :, DK:2 * DK],
                                            pJ[:, bk_, :].rearrange("p (s h k) -> p s h k", s=2, h=4),
                                            values[:, g % 2, n:n + 2, :, 0:DK].bitcast(F32),
                                            ALU.subtract).then_inc(fill_lo, 1)
                    return
                for a in range(2):
                    x = 2 * (i - 2) + a
                    last = nc.vector.scalar_tensor_tensor(
                        out=keys[DK:P, x, 512 * j:512 * j + 512], in0=pJ[DK * a:DK * a + DK, bk_, :],
                        scalar=bk_sb[:, 4 * g + x:4 * g + x + 1],
                        in1=keys[0:DK, x, 512 * j:512 * j + 512].bitcast(F32), op0=ALU.add, op1=ALU.subtract)
                last.then_inc(fill_lo, 1)

            def maxima(b, h):
                dve.wait_ge(scored, 16 * b + h + 1)
                nc.vector.tensor_reduce(neg_max[:, h % 2:h % 2 + 1], pS[:, :], AX.X, ALU.max,
                                        negate=True).then_inc(maxed, 1)

            def add_o(b, h):
                dve.wait_ge(o_copied, 16 * b + h + 2)
                dve.wait_ge(o_out[h % 2], 128 * b + 16 * (h // 2) + 16)
                nc.vector.tensor_tensor(o_half[:, h % 2, :], o_copy[:, 0:P], o_copy[:, P:2 * P],
                                        ALU.add).then_inc(o_added, 1)

            def row_sum(b, h):
                dve.wait_ge(exped, 64 * b + 4 * h + 4)
                nc.vector.tensor_reduce(total[:, h:h + 1], sums[:, h, :], AX.X, ALU.add).then_inc(totalled, 1)
                dve.wait_ge(totalled, 16 * b + h + 1)
                if h == 0:
                    dve.wait_ge(scale_out, 16 * b + 16)
                nc.vector.reciprocal(scale[:, h:h + 1], total[:, h:h + 1]).then_inc(scaled, 1)

            def batch(b, last):
                for g in range(XG):
                    more = not (last and g == XG - 1)
                    for i in range(4):
                        h = 4 * g + i
                        for j in range(4):
                            m = 16 * g + 4 * i + j
                            k = m - FIRST_CTX
                            turn = not last and 0 <= k < ST // 2
                            if turn:
                                fill_lo_ctx(PRO + PER * b + ctx_no(2 * k), ctx_no(2 * k) % 2, 2 * k)
                            dve.wait_ge(pt_hi, 64 * b + 4 * h + j + 1)
                            nc.vector.tensor_tensor(probsT[:, j % 2, :, 1, :], pT[:, :, :],
                                                    probsT[:, j % 2, :, 0, :].bitcast(F32),
                                                    ALU.subtract).then_inc(pt_lo, 1)
                            if turn:
                                fill_lo_ctx(PRO + PER * b + ctx_no(2 * k + 1), ctx_no(2 * k + 1) % 2, 2 * k + 1)
                            if j == 0 and h:
                                add_o(b, h - 1)
                            if j == 0:
                                row_sum(b, h)
                            if j == 1 and (more or i < 3):
                                maxima(b, h + 1)
                            if more:
                                fill_lo_vk(PRO + PER * b + fill_no(m, last), fill_no(m) % 2, (g + 1) % XG, i, j)
                add_o(b, XH - 1)

            dve.sem_inc(o_added, 1)
            dve.sem_inc(o_out[0], 16)
            dve.sem_inc(o_out[1], 16)
            dve.sem_inc(scale_out, 16)
            dve.wait_ge(bias_in, 16)
            for u in range(ST):
                fill_lo_ctx(u, u % 2, u)
            for m in range(16):
                fill_lo_vk(ST + m, m % 2, 0, m // 4, m % 4)
            maxima(0, 0)
            if batches > 1:
                with dve.Fori(0, batches - 1) as b:
                    batch(b, False)
            batch(batches - 1, True)


def chain(eng, done):
    count = [0]

    def step(ins):
        count[0] += 1
        ins.then_inc(done, 1)
        eng.wait_ge(done, count[0])
    return step


def norm_steps(nc, dve, step, x, stats, mv, t):
    step(nc.vector.bn_stats(stats[:, t, :], x[:, t, :]))
    step(nc.vector.bn_aggr(mv[:, t, :], stats[:, t, :]))


def prepare(nc, x, wq, bq, wk, wv, ident, wk_split, wv_split, q_split, used):
    es = ExitStack()
    with es:
        sb = lambda n, s, d: es.enter_context(nc.sbuf_tensor(n, s, d))
        ps = lambda n, s, d: es.enter_context(nc.psum_tensor(n, s, d))
        sem = lambda n: new_semaphore(nc, n, used)
        xs = sb("p_x", [P, B, D], F32)
        xn = sb("p_xn", [P, B, D], F32)
        xT = sb("p_xT", [P, DT, TOK], F32)
        wq_sb = sb("p_wq", [P, DT, XH * DK], F32)
        w_sb = sb("p_w", [P, 2, DT, XH * DK], F32)
        w_part = sb("p_wpart", [P, 2, DT, XH * DK], F32R)
        bq_sb = sb("p_bq", [P, XH // 2], F32)
        bq8 = sb("p_bq8", [P, XH // 2], F32)
        stats = sb("p_stats", [P, B, 6], F32)
        mv = sb("p_mv", [P, B, 2], F32)
        veps = sb("p_veps", [P, B], F32)
        std = sb("p_std", [P, B], F32)
        rstd = sb("p_rstd", [P, B], F32)
        q32 = sb("p_q32", [P, 2, 512], F32)
        qb = sb("p_qb", [P, 2, 4, 2, P], F32R)
        pt = ps("p_pt", [P, 2, 512], F32)
        pq = ps("p_pq", [P, 4, 512], F32)

        x_in, wq_in, bq_in = sem("p_x_in"), sem("p_wq_in"), sem("p_bq_in")
        w_in = [sem("p_w_in0"), sem("p_w_in1")]
        w_out = sem("p_w_out")
        q_out = [sem("p_q_out0"), sem("p_q_out1")]
        made = sem("p_made")
        step_done = sem("p_step")
        var_ready, std_ready = sem("p_var"), sem("p_std_ready")
        normed = sem("p_normed")
        turned = sem("p_turned")
        turned_out = sem("p_turned_out")
        bias_ready = sem("p_bias8")
        q_done = sem("p_qdone")
        q_copied = sem("p_qcopied")
        q_hi, q_parts = sem("p_qhi"), sem("p_qparts")
        w_hi, w_lo = sem("p_whi"), sem("p_wlo")
        block = es.enter_context(nc.Block())

        @block.sync
        def _(sp):
            sp.dma_start(xs[:, :, :], x.rearrange("b p d -> p b d")).then_inc(x_in, 16)
            with nc.allow_non_contiguous_dma(reason="the bias, once"):
                sp.dma_start(bq_sb[:, :], bq.rearrange("(a u) k -> (u k) a", u=2)).then_inc(bq_in, 16)
            sp.dma_start(wq_sb[:, :, :], wq.rearrange("(t p) h k -> p t (h k)", p=P)).then_inc(wq_in, 16)
            for n, w in enumerate((wk, wv)):
                sp.dma_start(w_sb[:, n, :, :], w.rearrange("(t p) h k -> p t (h k)", p=P)).then_inc(w_in[n], 16)
            for n, out in enumerate((wk_split, wv_split)):
                sp.wait_ge(w_lo, n + 1)
                sp.dma_start(out[0], w_part[:, 0, :, :].bitcast(F32)).then_inc(w_out, 16)
                sp.dma_start(out[1], w_part[:, 1, :, :].bitcast(F32)).then_inc(w_out, 16)
                if n == 0:
                    continue
            for n in range(16):
                pair, half = n // 2, n % 2
                sp.wait_ge(q_parts, n + 1)
                sp.dma_start(q_split[P * pair:P * pair + P, 4 * half:4 * half + 4, :, :],
                             qb[:, n % 2, :, :, :].bitcast(F32)).then_inc(q_out[n % 2], 16)
            sp.wait_ge(w_out, 64)
            for n in range(2):
                sp.wait_ge(q_out[n], 16 * 8)

        @block.gpsimd
        def _(pool):
            nc.gpsimd.memset(ident[:, :], 0.0).then_inc(made, 1)
            pool.wait_ge(made, 1)
            nc.gpsimd.affine_select(out=ident[:, :], in_=ident[:, :], compare_op=ALU.not_equal, fill=1.0,
                                    base=0, pattern=[[-1, P]], channel_multiplier=1).then_inc(made, 1)

        @block.vector
        def _(dve):
            step = chain(dve, step_done)
            dve.wait_ge(x_in, 16)
            for t in range(B):
                norm_steps(nc, dve, step, xs, stats, mv, t)
            nc.vector.tensor_scalar_add(veps[:, :], mv[:, :, 1], EPS).then_inc(var_ready, 1)
            dve.wait_ge(std_ready, 1)
            step(nc.vector.reciprocal(rstd[:, :], std[:, :]))
            for t in range(B):
                nc.vector.tensor_scalar(xn[:, t, :], xs[:, t, :], mv[:, t, 0:1], rstd[:, t:t + 1],
                                        ALU.subtract, ALU.mult).then_inc(normed, 1)
            dve.wait_ge(bq_in, 16)
            nc.vector.tensor_scalar(bq8[:, :], bq_sb[:, :], DK ** -0.5, None, ALU.mult).then_inc(bias_ready, 1)
            for n in range(2):
                dve.wait_ge(w_hi, n + 1)
                nc.vector.tensor_tensor(w_part[:, 1, :, :], w_sb[:, n, :, :], w_part[:, 0, :, :].bitcast(F32),
                                        ALU.subtract).then_inc(w_lo, 1)
            for n in range(16):
                dve.wait_ge(q_copied, n + 1)
                if n >= 2:
                    dve.wait_ge(q_out[n % 2], 16 * (n // 2))
                q4 = q32[:, n % 2, :].rearrange("p (b t) -> p b t", b=4)
                nc.vector.tensor_copy(qb[:, n % 2, :, 0, :], q4).then_inc(q_hi, 1)
                dve.wait_ge(q_hi, n + 1)
                nc.vector.tensor_tensor(qb[:, n % 2, :, 1, :], q4, qb[:, n % 2, :, 0, :].bitcast(F32),
                                        ALU.subtract).then_inc(q_parts, 1)

        @block.scalar
        def _(act):
            act.wait_ge(var_ready, 1)
            nc.scalar.activation(std[:, :], veps[:, :], ACT.Sqrt).then_inc(std_ready, 1)
            for t in range(B):
                act.wait_ge(turned, t + 1)
                nc.scalar.copy(xT[:, :, P * t:P * t + P],
                               pt[:, t % 2, :].rearrange("p (c s) -> p c s", c=DT)).then_inc(turned_out, 1)
            act.wait_ge(w_in[0], 16)
            nc.scalar.copy(w_part[:, 0, :, :], w_sb[:, 0, :, :]).then_inc(w_hi, 1)
            act.wait_ge(w_in[1], 16)
            act.wait_ge(w_out, 32)
            nc.scalar.copy(w_part[:, 0, :, :], w_sb[:, 1, :, :]).then_inc(w_hi, 1)
            act.wait_ge(bias_ready, 1)
            for n in range(16):
                act.wait_ge(q_done, n + 1)
                if n >= 2:
                    act.wait_ge(q_parts, n - 1)
                nc.scalar.activation(q32[:, n % 2, :], pq[:, n % 4, :], ACT.Identity,
                                     bias=bq8[:, n // 2:n // 2 + 1], scale=DK ** -0.5).then_inc(q_copied, 1)

        @block.tensor
        def _(pe):
            pe.wait_ge(made, 2)
            for t in range(B):
                pe.wait_ge(normed, t + 1)
                if t >= 2:
                    pe.wait_ge(turned_out, t - 1)
                for c in range(DT):
                    last = nc.tensor.transpose(pt[:, t % 2, P * c:P * c + P], xn[:, t, P * c:P * c + P], ident[:, :])
                last.then_inc(turned, 1)
            pe.wait_ge(wq_in, 16)
            pe.wait_ge(turned_out, B)
            for n in range(16):
                pair, half = n // 2, n % 2
                if n >= 4:
                    pe.wait_ge(q_copied, n - 3)
                for t in range(DT):
                    last = nc.tensor.matmul(pq[:, n % 4, :], wq_sb[:, t, P * pair:P * pair + P],
                                            xT[:, t, 512 * half:512 * half + 512], start=t == 0, stop=t == DT - 1)
                last.then_inc(q_done, 1)

SH = 8
NM = B * SH
ITERS = 20


def self_attention(nc, x, xo, x_bv, x_bo, o_parts, row_scale, wq, bq, wk, bk, wv, bv, wo, bo, ident, x1, used):
    es = ExitStack()
    with es:
        sb = lambda n, s, d, e=es: e.enter_context(nc.sbuf_tensor(n, s, d))
        ps = lambda n, s, d, e=es: e.enter_context(nc.psum_tensor(n, s, d))
        sem = lambda n: new_semaphore(nc, n, used)
        BF16 = mybir.dt.bfloat16
        v_sb = sb("s_v", [P, B, D], F32)
        bo_sb = sb("s_bo", [P, D], F32)
        wo_sb = sb("s_wo", [P, DT, D], F32)
        AT = sb("s_AT", [P, NM, P], F32)
        half = ExitStack()
        q_sb = sb("s_q", [P, DT, TOK], F32, half)
        k_sb = sb("s_k", [P, DT, TOK], F32, half)
        wo_in = sem("s_wo_in")
        with half:
            with ExitStack() as s1:
                xn = sb("a_xn", [P, 2, D], F32, s1)
                xT = sb("a_xT", [P, DT, TOK], F32, s1)
                xo_sb = sb("a_xo", [P, XH // 2, D], F32, s1)
                ua = sb("a_ua", [P, 2, 2, XH // 2, P], F32, s1)
                us = sb("a_us", [P, XH // 2, P], F32, s1)
                ub = sb("a_ub", [P, XH // 2, P], F32, s1)
                oT = sb("a_oT", [P, 2, XH // 2, P], F32, s1)
                rs = sb("a_rs", [P, B, XH], F32, s1)
                xbo = sb("a_xbo", [P, D], F32, s1)
                xbv = sb("a_xbv", [P, XH // 2], F32, s1)
                bqk = sb("a_bqk", [P, 2, DT], F32, s1)
                bq8 = sb("a_bq8", [P, DT], F32, s1)
                bvb = sb("a_bv", [P, D], F32, s1)
                w = sb("a_w", [P, 3, DT, D], F32, s1)
                stats = sb("a_stats", [P, B, 6], F32, s1)
                mv = sb("a_mv", [P, B, 2], F32, s1)
                veps = sb("a_veps", [P, B], F32, s1)
                std = sb("a_std", [P, B], F32, s1)
                rstd = sb("a_rstd", [P, B], F32, s1)
                pR = ps("a_pR", [P, 2, 4, P], F32, s1)
                pY = ps("a_pY", [P, 2, D], F32, s1)
                pt = ps("a_pt", [P, 2, DT, P], F32, s1)
                pw = ps("a_pw", [P, 2, 512], F32, s1)
                xs_in, xo_in, rs_in, c_in = (sem(n) for n in ("a_xs_in", "a_xo_in", "a_rs_in", "a_c_in"))
                w_in = sem("a_w_in")
                u_in = [sem("a_u_in0"), sem("a_u_in1")]
                spread, added, merged = sem("a_spread"), sem("a_added"), sem("a_merged")
                projected, xb_done = sem("a_projected"), sem("a_xb")
                step_done, var_ready, std_ready = sem("a_step"), sem("a_var"), sem("a_std")
                normed, turned, turned_out = sem("a_normed"), sem("a_turned"), sem("a_turned_out")
                x1_done, made, b8 = sem("a_x1"), sem("a_made"), sem("a_b8")
                qk_out, v_out = sem("a_qk_out"), sem("a_v_out")
                block = s1.enter_context(nc.Block())

                def residual(dve, step, b):
                    dve.wait_ge(projected, b + 1)
                    dve.wait_ge(xb_done, b + 1)
                    nc.vector.tensor_tensor(x1[:, b, :], pY[:, b % 2, :], x1[:, b, :], ALU.add).then_inc(x1_done, 1)
                    dve.wait_ge(x1_done, b + 1)
                    norm_steps(nc, dve, step, x1, stats, mv, b)

                @block.sync
                def _(sp):
                    def u_load(b):
                        for n in range(2):
                            for u in range(2):
                                sp.dma_start(ua[DK * u:DK * u + DK, b % 2, n, :, :],
                                             o_parts[b].rearrange("(a u) k t -> u k a t", u=2)[u, DK * n:DK * n + DK, :, :]
                                             ).then_inc(u_in[b % 2], 16)
                    sp.dma_start(rs[:, :, :], row_scale.rearrange("b t h -> t b h")).then_inc(rs_in, 16)
                    u_load(0)
                    sp.dma_start(xo_sb[:, :, :], xo.rearrange("(a u) k d -> (u k) a d", u=2)).then_inc(xo_in, 16)
                    with nc.allow_non_contiguous_dma(reason="biases, once"):
                        sp.dma_start(xbv[:, :], x_bv.rearrange("(a u) k -> (u k) a", u=2)).then_inc(c_in, 16)
                        sp.dma_start(bqk[:, 0, :], bq.rearrange("(t p) -> p t", p=P)).then_inc(c_in, 16)
                        sp.dma_start(bqk[:, 1, :], bk.rearrange("(t p) -> p t", p=P)).then_inc(c_in, 16)
                    for out, src in ((xbo, x_bo), (bvb, bv), (bo_sb, bo)):
                        sp.dma_start(out[:, :], src.rearrange("(a d) -> a d", a=1).to_broadcast([P, D])).then_inc(c_in, 16)
                    sp.dma_start(x1[:, :, :], x.rearrange("b p d -> p b d")).then_inc(xs_in, 16)
                    u_load(1)
                    for n, src in enumerate((wq, wk, wv)):
                        sp.dma_start(w[:, n, :, :], src.rearrange("(t p) d -> p t d", p=P)).then_inc(w_in, 16)
                    sp.dma_start(wo_sb[:, :, :], wo.rearrange("(t p) d -> p t d", p=P)).then_inc(wo_in, 16)
                    for b in range(2, B):
                        sp.wait_ge(added, b - 1)
                        u_load(b)
                    sp.wait_ge(wo_in, 16)

                @block.tensor
                def _(pe):
                    pe.wait_ge(rs_in, 16)

                    def spread_scales(b):
                        if b:
                            pe.wait_ge(merged, b)
                        for a in range(XH // 2):
                            for u in range(2):
                                h = 2 * a + u
                                last = nc.tensor.matmul(pR[DK * u:DK * u + DK, a // 4, a % 4, :],
                                                        rs[:, b, h:h + 1].to_broadcast([P, DK]),
                                                        ident[:, :], start=True, stop=True)
                        last.then_inc(spread, 1)
                    spread_scales(0)
                    pe.wait_ge(xo_in, 16)
                    for b in range(B):
                        if b + 1 < B:
                            spread_scales(b + 1)
                        pe.wait_ge(merged, b + 1)
                        if b >= 2:
                            pe.wait_ge(x1_done, b - 1)
                        for a in range(XH // 2):
                            last = nc.tensor.matmul(pY[:, b % 2, :], oT[:, b % 2, a, :], xo_sb[:, a, :],
                                                    start=a == 0, stop=a == XH // 2 - 1)
                        last.then_inc(projected, 1)
                    for t in range(B):
                        pe.wait_ge(normed, t + 1)
                        if t >= 2:
                            pe.wait_ge(turned_out, t - 1)
                        for c in range(DT):
                            last = nc.tensor.transpose(pt[:, t % 2, c, :], xn[:, t % 2, P * c:P * c + P], ident[:, :])
                        last.then_inc(turned, 1)
                    pe.wait_ge(turned_out, B)
                    pe.wait_ge(w_in, 48)
                    for n in range(16):
                        if n >= 2:
                            pe.wait_ge(qk_out, n - 1)
                        s, a, hf = n // 8, n // 2 % 4, n % 2
                        for t in range(DT):
                            last = nc.tensor.matmul(pw[:, n % 2, :], w[:, s, t, P * a:P * a + P],
                                                    xT[:, t, 512 * hf:512 * hf + 512], start=t == 0, stop=t == DT - 1)
                        last.then_inc(made, 1)
                    pe.wait_ge(qk_out, 16)
                    for b in range(B):
                        if b >= 2:
                            pe.wait_ge(v_out, b - 1)
                        for t in range(DT):
                            last = nc.tensor.matmul(pw[:, b % 2, :], xT[:, t, P * b:P * b + P], w[:, 2, t, :],
                                                    start=t == 0, stop=t == DT - 1)
                        last.then_inc(made, 1)

                @block.gpsimd
                def _(pool):
                    pool.wait_ge(c_in, 96)
                    pool.wait_ge(xs_in, 16)
                    for b in range(B):
                        nc.gpsimd.tensor_tensor(x1[:, b, :], x1[:, b, :], xbo[:, :], ALU.add).then_inc(xb_done, 1)

                @block.vector
                def _(dve):
                    step = chain(dve, step_done)
                    dve.wait_ge(c_in, 96)
                    for b in range(B):
                        dve.wait_ge(u_in[b % 2], 64 * (b // 2 + 1))
                        nc.vector.tensor_tensor(us[:, :, :], ua[:, b % 2, 0, :, :], ua[:, b % 2, 1, :, :],
                                                ALU.add).then_inc(added, 1)
                        dve.wait_ge(added, b + 1)
                        dve.wait_ge(spread, b + 1)
                        step(nc.vector.tensor_tensor(ub[:, :, :], us[:, :, :], pR[:, :, :, :].rearrange("p a b t -> p (a b) t"),
                                                     ALU.mult))
                        if b >= 2:
                            dve.wait_ge(projected, b - 1)
                        nc.vector.tensor_tensor(oT[:, b % 2, :, :], ub[:, :, :],
                                                xbv[:, :].unsqueeze(2).to_broadcast([P, XH // 2, P]), ALU.add).then_inc(merged, 1)
                        if b:
                            residual(dve, step, b - 1)
                    residual(dve, step, B - 1)
                    nc.vector.tensor_scalar_add(veps[:, :], mv[:, :, 1], EPS).then_inc(var_ready, 1)
                    dve.wait_ge(std_ready, 1)
                    step(nc.vector.reciprocal(rstd[:, :], std[:, :]))
                    nc.vector.tensor_scalar(bq8[:, :], bqk[:, 0, :], DK ** -0.5, None, ALU.mult).then_inc(b8, 1)
                    for t in range(B):
                        if t >= 2:
                            dve.wait_ge(turned, t - 1)
                        nc.vector.tensor_scalar(xn[:, t % 2, :], x1[:, t, :], mv[:, t, 0:1], rstd[:, t:t + 1],
                                                ALU.subtract, ALU.mult).then_inc(normed, 1)
                    for b in range(B):
                        dve.wait_ge(made, 16 + b + 1)
                        nc.vector.tensor_tensor(v_sb[:, b, :], pw[:, b % 2, :], bvb[:, :], ALU.add).then_inc(v_out, 1)

                @block.scalar
                def _(act):
                    act.wait_ge(var_ready, 1)
                    nc.scalar.activation(std[:, :], veps[:, :], ACT.Sqrt).then_inc(std_ready, 1)
                    for t in range(B):
                        act.wait_ge(turned, t + 1)
                        nc.scalar.copy(xT[:, :, P * t:P * t + P], pt[:, t % 2, :, :]).then_inc(turned_out, 1)
                    act.wait_ge(b8, 1)
                    for n in range(16):
                        act.wait_ge(made, n + 1)
                        s, a, hf = n // 8, n // 2 % 4, n % 2
                        nc.scalar.activation((q_sb, k_sb)[s][:, a, 512 * hf:512 * hf + 512], pw[:, n % 2, :], ACT.Identity,
                                             bias=bq8[:, a:a + 1] if s == 0 else bqk[:, 1, a:a + 1],
                                             scale=DK ** -0.5 if s == 0 else 1.0).then_inc(qk_out, 1)

            with ExitStack() as s2:
                NQ = NM // 4
                lm = sb("b_lm", [P, 2, 4, P], F32, s2)
                ex = sb("b_ex", [P, 2, 4, P], F32, s2)
                la = sb("b_la", [P, 2, 4, P], F32, s2)
                lt = sb("b_lt", [P, 2, 4, P], F32, s2)
                et = sb("b_et", [P, 2, 4, P], F32, s2)
                nm = sb("b_nm", [P, NM], F32, s2)
                s_ = sb("b_s", [P, NM], F32, s2)
                ls = sb("b_ls", [P, NM], F32, s2)
                nm2 = sb("b_nm2", [P, NM], F32, s2)
                s2_ = sb("b_s2", [P, NM], F32, s2)
                r2 = sb("b_r2", [P, NM], F32, s2)
                pL = ps("b_pL", [P, 2, 4, P], F32, s2)
                pLT = ps("b_pLT", [P, 2, 4, P], F32, s2)
                logits, shifted, exped, summed = (sem(n) for n in ("b_logits", "b_shifted", "b_exped", "b_summed"))
                logged, normed1, turned = (sem(n) for n in ("b_logged", "b_normed", "b_turned"))
                shifted2, exped2, done2 = (sem(n) for n in ("b_shifted2", "b_exped2", "b_done2"))
                step_done = sem("b_step")
                block = s2.enter_context(nc.Block())

                @block.tensor
                def _(pe):
                    def turn(n):
                        pe.wait_ge(normed1, n + 1)
                        if n >= 2:
                            pe.wait_ge(shifted2, n - 1)
                        for k in range(4):
                            last = nc.tensor.transpose(pLT[:, n % 2, k, :], la[:, n % 2, k, :], ident[:, :])
                        last.then_inc(turned, 1)
                    for n in range(NQ):
                        b = n // 2
                        if n >= 2:
                            pe.wait_ge(shifted, n - 1)
                        for k in range(4):
                            h = 2 * k + n % 2
                            r = slice(DK * (h % 2), DK * (h % 2) + DK)
                            last = nc.tensor.matmul(pL[:, n % 2, k, :], q_sb[r, h // 2, P * b:P * b + P],
                                                    k_sb[r, h // 2, P * b:P * b + P], start=True, stop=True)
                        last.then_inc(logits, 1)
                        if n:
                            turn(n - 1)
                    turn(NQ - 1)

                def over(t, n):
                    return t[:, 4 * n:4 * n + 4].unsqueeze(2).to_broadcast([P, 4, P])

                @block.scalar
                def _(act):
                    def second(n):
                        act.wait_ge(shifted2, n + 1)
                        nc.scalar.activation(et[:, n % 2, :, :], lt[:, n % 2, :, :], ACT.Exp).then_inc(exped2, 1)
                    for n in range(NQ):
                        act.wait_ge(shifted, n + 1)
                        nc.scalar.activation(ex[:, n % 2, :, :], lm[:, n % 2, :, :], ACT.Exp).then_inc(exped, 1)
                        act.wait_ge(summed, n + 1)
                        nc.scalar.activation(ls[:, 4 * n:4 * n + 4], s_[:, 4 * n:4 * n + 4], ACT.Ln).then_inc(logged, 1)
                        if n:
                            second(n - 1)
                    second(NQ - 1)

                @block.vector
                def _(dve):
                    step = chain(dve, step_done)

                    def first(n):
                        dve.wait_ge(logits, n + 1)
                        step(nc.vector.tensor_reduce(nm[:, 4 * n:4 * n + 4], pL[:, n % 2, :, :], AX.X, ALU.max, negate=True))
                        nc.vector.tensor_tensor(lm[:, n % 2, :, :], pL[:, n % 2, :, :], over(nm, n), ALU.add).then_inc(shifted, 1)

                    def sums(n):
                        dve.wait_ge(exped, n + 1)
                        nc.vector.tensor_reduce(s_[:, 4 * n:4 * n + 4], ex[:, n % 2, :, :], AX.X, ALU.add).then_inc(summed, 1)

                    def rows(n):
                        dve.wait_ge(logged, n + 1)
                        nc.vector.tensor_tensor(la[:, n % 2, :, :], lm[:, n % 2, :, :], over(ls, n), ALU.subtract).then_inc(normed1, 1)

                    def columns(n):
                        dve.wait_ge(turned, n + 1)
                        step(nc.vector.tensor_reduce(nm2[:, 4 * n:4 * n + 4], pLT[:, n % 2, :, :], AX.X, ALU.max, negate=True))
                        nc.vector.tensor_tensor(lt[:, n % 2, :, :], pLT[:, n % 2, :, :], over(nm2, n), ALU.add).then_inc(shifted2, 1)

                    def close(n):
                        dve.wait_ge(exped2, n + 1)
                        step(nc.vector.tensor_reduce(s2_[:, 4 * n:4 * n + 4], et[:, n % 2, :, :], AX.X, ALU.add))
                        step(nc.vector.reciprocal(r2[:, 4 * n:4 * n + 4], s2_[:, 4 * n:4 * n + 4]))
                        nc.vector.tensor_tensor(AT[:, 4 * n:4 * n + 4, :], et[:, n % 2, :, :], over(r2, n), ALU.mult).then_inc(done2, 1)
                    first(0)
                    for n in range(NQ):
                        sums(n)
                        if n + 1 < NQ:
                            first(n + 1)
                        if n >= 1:
                            columns(n - 1)
                        rows(n)
                        if n >= 1:
                            close(n - 1)
                    columns(NQ - 1)
                    close(NQ - 1)

        r32 = sb("s_r32", [P, NM], F32)
        c32 = sb("s_c32", [P, NM], F32)
        with ExitStack() as s3:
            NQ = NM // 4
            at_p = sb("c_atp", [P, 3, NM, P], BF16, s3)
            a_p = sb("c_ap", [P, 3, NM, P], BF16, s3)
            rest = sb("c_rest", [P, 2, 4, P], F32, s3)
            r_p = sb("c_rp", [P, NM, 3], BF16, s3)
            c_p = sb("c_cp", [P, NM, 3], BF16, s3)
            tot = sb("c_tot", [P, NM], F32, s3)
            left = sb("c_left", [P, NM], F32, s3)
            pA = ps("c_pA", [P, 2, 4, P], F32, s3)
            with ExitStack() as s4:
                turned, part1, rest1, part2, part3 = (sem(n) for n in ("c_turned", "c_part1", "c_rest1", "c_part2", "c_part3"))
                block = s4.enter_context(nc.Block())

                def source(n):
                    m = n // 2
                    return (AT[:, 4 * m:4 * m + 4, :], at_p) if n % 2 == 0 else (pA[:, m % 2, :, :], a_p)

                @block.tensor
                def _(pe):
                    for m in range(NQ):
                        if m >= 2:
                            pe.wait_ge(rest1, 2 * m - 2)
                        for k in range(4):
                            last = nc.tensor.transpose(pA[:, m % 2, k, :], AT[:, 4 * m + k, :], ident[:, :])
                        last.then_inc(turned, 1)

                @block.scalar
                def _(act):
                    for n in range(2 * NQ + 1):
                        m = n // 2
                        if n < 2 * NQ:
                            src, parts = source(n)
                            if n % 2:
                                act.wait_ge(turned, m + 1)
                            nc.scalar.copy(parts[:, 0, 4 * m:4 * m + 4, :], src).then_inc(part1, 1)
                        if n:
                            src, parts = source(n - 1)
                            m = (n - 1) // 2
                            act.wait_ge(rest1, n)
                            nc.scalar.copy(parts[:, 1, 4 * m:4 * m + 4, :], rest[:, (n - 1) % 2, :, :]).then_inc(part2, 1)

                @block.vector
                def _(dve):
                    for n in range(2 * NQ + 1):
                        m = n // 2
                        if n < 2 * NQ:
                            src, parts = source(n)
                            dve.wait_ge(part1, n + 1)
                            if n >= 2:
                                dve.wait_ge(part3, n - 1)
                            nc.vector.tensor_tensor(rest[:, n % 2, :, :], src, parts[:, 0, 4 * m:4 * m + 4, :],
                                                    ALU.subtract).then_inc(rest1, 1)
                        if n:
                            src, parts = source(n - 1)
                            m = (n - 1) // 2
                            dve.wait_ge(part2, n)
                            nc.vector.tensor_tensor(parts[:, 2, 4 * m:4 * m + 4, :], rest[:, (n - 1) % 2, :, :],
                                                    parts[:, 1, 4 * m:4 * m + 4, :], ALU.subtract).then_inc(part3, 1)
            with ExitStack() as s5:
                NG, GM = 4, NM // 4
                pV = ps("c_pV", [P, 4, 512], F32, s5)
                r_sums, r_ready = sem("c_r_sums"), sem("c_r_ready")
                c_sums, c_ready = sem("c_c_sums"), sem("c_c_ready")
                step_done = sem("c_step")
                STEPS = 5 * 2 * NG
                block = s5.enter_context(nc.Block())

                @block.tensor
                def _(pe):
                    def products(g, mats, vec, done):
                        for k in range(GM):
                            m = GM * g + k
                            for n in range(3):
                                last = nc.tensor.matmul(pV[:, g, 4 * k:4 * k + 3], mats[:, n, m, :], vec[:, m, :],
                                                        start=n == 0, stop=n == 2)
                        last.then_inc(done, 1)
                    with pe.Fori(0, ITERS - 1) as it:
                        for g in range(NG):
                            pe.wait_ge(c_ready, NG * it + g + 1)
                            products(g, at_p, c_p, r_sums)
                        for g in range(NG):
                            pe.wait_ge(r_ready, NG * it + g + 1)
                            products(g, a_p, r_p, c_sums)

                @block.vector
                def _(dve):
                    def invert(it, no, g, sums, v32, v_p, ready):
                        s = slice(GM * g, GM * g + GM)
                        base = STEPS * it + 5 * no
                        dve.wait_ge(sums, NG * it + g + 1)
                        nc.vector.tensor_reduce(tot[:, s], pV[:, g, 0:4 * GM].rearrange("p (m n) -> p m n", n=4)[:, :, 0:3],
                                                AX.X, ALU.add).then_inc(step_done, 1)
                        dve.wait_ge(step_done, base + 1)
                        nc.vector.reciprocal(v32[:, s], tot[:, s]).then_inc(step_done, 1)
                        dve.wait_ge(step_done, base + 2)
                        nc.vector.tensor_copy(v_p[:, s, 0], v32[:, s]).then_inc(step_done, 1)
                        dve.wait_ge(step_done, base + 3)
                        nc.vector.tensor_tensor(left[:, s], v32[:, s], v_p[:, s, 0], ALU.subtract).then_inc(step_done, 1)
                        dve.wait_ge(step_done, base + 4)
                        nc.vector.tensor_copy(v_p[:, s, 1], left[:, s]).then_inc(step_done, 1)
                        dve.wait_ge(step_done, base + 5)
                        nc.vector.tensor_tensor(v_p[:, s, 2], left[:, s], v_p[:, s, 1], ALU.subtract).then_inc(ready, 1)
                    nc.vector.memset(c_p[:, :, 1:3], 0.0)
                    for g in range(NG):
                        nc.vector.memset(c_p[:, GM * g:GM * g + GM, 0:1], 1.0).then_inc(c_ready, 1)
                    with dve.Fori(0, ITERS - 1) as it:
                        for g in range(NG):
                            invert(it, g, g, r_sums, r32, r_p, r_ready)
                        for g in range(NG):
                            invert(it, NG + g, g, c_sums, c32, c_p, c_ready)

        with ExitStack() as s6:
            cv = sb("d_cv", [P, 2, D], F32, s6)
            o = sb("d_o", [P, 2, D], F32, s6)
            oT = sb("d_oT", [P, 2, DT, P], F32, s6)
            pO = ps("d_pO", [P, 2, D], F32, s6)
            pt = ps("d_pt", [P, 2, DT, P], F32, s6)
            pY = ps("d_pY", [P, 2, D], F32, s6)
            weighted, summed, scaled, turned = (sem(n) for n in ("d_weighted", "d_summed", "d_scaled", "d_turned"))
            turned_out, projected, added, biased = (sem(n) for n in ("d_tout", "d_proj", "d_added", "d_biased"))
            block = s6.enter_context(nc.Block())

            def by_parity(rows):
                return rows.rearrange("p (a u k) -> p u a k", a=SH // 2, u=2)

            def spread(scales, b):
                return scales[:, SH * b:SH * b + SH].rearrange("p (u a) -> p u a", u=2).unsqueeze(3).to_broadcast(
                    [P, 2, SH // 2, DK])

            @block.gpsimd
            def _(pool):
                for b in range(B):
                    nc.gpsimd.tensor_tensor(x1[:, b, :], x1[:, b, :], bo_sb[:, :], ALU.add).then_inc(biased, 1)

            @block.vector
            def _(dve):
                def weight(b):
                    if b >= 2:
                        dve.wait_ge(summed, b - 1)
                    nc.vector.tensor_tensor(by_parity(cv[:, b % 2, :]), by_parity(v_sb[:, b, :]), spread(c32, b),
                                            ALU.mult).then_inc(weighted, 1)

                def add(b):
                    dve.wait_ge(projected, b + 1)
                    dve.wait_ge(biased, b + 1)
                    nc.vector.tensor_tensor(x1[:, b, :], pY[:, b % 2, :], x1[:, b, :], ALU.add).then_inc(added, 1)
                weight(0)
                for b in range(B):
                    if b + 1 < B:
                        weight(b + 1)
                    dve.wait_ge(summed, b + 1)
                    if b >= 2:
                        dve.wait_ge(turned, b - 1)
                    nc.vector.tensor_tensor(by_parity(o[:, b % 2, :]), by_parity(pO[:, b % 2, :]), spread(r32, b),
                                            ALU.mult).then_inc(scaled, 1)
                    if b:
                        add(b - 1)
                add(B - 1)

            @block.tensor
            def _(pe):
                def attend(b):
                    pe.wait_ge(weighted, b + 1)
                    if b >= 2:
                        pe.wait_ge(scaled, b - 1)
                    for h in range(SH):
                        last = nc.tensor.matmul(pO[:, b % 2, DK * h:DK * h + DK], AT[:, SH * b + 4 * (h % 2) + h // 2, :],
                                                cv[:, b % 2, DK * h:DK * h + DK], start=True, stop=True)
                    last.then_inc(summed, 1)
                attend(0)
                pe.wait_ge(wo_in, 16)
                for b in range(B):
                    if b + 1 < B:
                        attend(b + 1)
                    pe.wait_ge(scaled, b + 1)
                    if b >= 2:
                        pe.wait_ge(turned_out, b - 1)
                    for c in range(DT):
                        last = nc.tensor.transpose(pt[:, b % 2, c, :], o[:, b % 2, P * c:P * c + P], ident[:, :])
                    last.then_inc(turned, 1)
                    pe.wait_ge(turned_out, b + 1)
                    if b >= 2:
                        pe.wait_ge(added, b - 1)
                    for c in range(DT):
                        last = nc.tensor.matmul(pY[:, b % 2, :], oT[:, b % 2, c, :], wo_sb[:, c, :],
                                                start=c == 0, stop=c == DT - 1)
                    last.then_inc(projected, 1)

            @block.scalar
            def _(act):
                for b in range(B):
                    act.wait_ge(turned, b + 1)
                    if b >= 2:
                        act.wait_ge(projected, b - 1)
                    nc.scalar.copy(oT[:, b % 2, :, :], pt[:, b % 2, :, :]).then_inc(turned_out, 1)

E = 8
F = 2048
CAP = 161
CAPP = 162
OVER = CAP - P
FC = 4


def experts(nc, x2, wg, w1, b1, w2, b2, ident, buf, ybuf, out, used):
    es = ExitStack()
    with es:
        sb = lambda n, s, d, e=es: e.enter_context(nc.sbuf_tensor(n, s, d))
        ps = lambda n, s, d, e=es: e.enter_context(nc.psum_tensor(n, s, d))
        sem = lambda n: new_semaphore(nc, n, used)
        raw1 = sb("e_raw1", [P, 2, DT, 512], F32)
        raw2 = sb("e_raw2", [P, 2, 4, D], F32)
        w_in = [[sem(f"e_w{a}_in{n}") for n in range(2)] for a in (1, 2)]
        backs = [sem(f"h_back{t}") for t in range(B)]
        b1T = sb("e_b1T", [P, E * F // P], F32)
        b2T = sb("e_b2T", [P, E * DT], F32)
        slot = sb("e_slot", [P, B], U32)
        yslot = sb("e_yslot", [P, B], U32)
        weight = sb("e_weight", [P, B], F32)

        def w1_load(eng, e, c):
            eng.dma_start(raw1[:, c % 2, :, :], w1[e].rearrange("(t p) f -> p t f", p=P)[:, :, 512 * c:512 * c + 512]
                          ).then_inc(w_in[0][c % 2], 16)

        def w2_load(eng, e, c):
            eng.dma_start(raw2[:, c % 2, :, :], w2[e].rearrange("(c t p) d -> p c t d", p=P, c=FC)[:, c, :, :]
                          ).then_inc(w_in[1][c % 2], 16)

        with ExitStack() as s1:
            xn = sb("g_xn", [P, B, D], F32, s1)
            xT = sb("g_xT", [P, 2, DT, P], F32, s1)
            zero = sb("g_zero", [P, D], F32, s1)
            wg_sb = sb("g_wg", [P, DT, E], F32, s1)
            b1r = sb("g_b1", [P, P], F32, s1)
            b2r = sb("g_b2", [E * DT, P], F32, s1)
            stats = sb("g_stats", [P, B, 6], F32, s1)
            mv = sb("g_mv", [P, B, 2], F32, s1)
            veps = sb("g_veps", [P, B], F32, s1)
            std = sb("g_std", [P, B], F32, s1)
            rstd = sb("g_rstd", [P, B], F32, s1)
            before = sb("g_before", [P, P], F32, s1)
            ones = sb("g_ones", [P, P], F32, s1)
            e_no = sb("g_eno", [P, E], F32, s1)
            token = sb("g_token", [P, B], F32, s1)
            mx = sb("g_mx", [P, B], F32, s1)
            lm = sb("g_lm", [P, B, E], F32, s1)
            ex = sb("g_ex", [P, B, E], F32, s1)
            s_ = sb("g_s", [P, B], F32, s1)
            prob = sb("g_prob", [P, B], F32, s1)
            cand = sb("g_cand", [P, B, E], F32, s1)
            top = sb("g_top", [P, B], F32, s1)
            oh = sb("g_oh", [P, B, E], F32, s1)
            carry = sb("g_carry", [P, B, E], F32, s1)
            rk = sb("g_rk", [P, B, E], F32, s1)
            ro = sb("g_ro", [P, B, E], F32, s1)
            rank = sb("g_rank", [P, B], F32, s1)
            valid = sb("g_valid", [P, B], F32, s1)
            sl = sb("g_sl", [P, 4, B], F32, s1)
            pt = ps("g_pt", [P, 2, DT, P], F32, s1)
            pg = ps("g_pg", [P, B, E], F32, s1)
            pr = ps("g_pr", [P, B, E], F32, s1)
            pc = ps("g_pc", [P, B, E], F32, s1)
            pb = ps("g_pb", [P, P + E * DT], F32, s1)
            c_in, zeroed, zero_out = sem("g_c_in"), sem("g_zeroed"), sem("g_zero_out")
            step_done, var_ready, std_ready = sem("g_step"), sem("g_var"), sem("g_std")
            normed, turned, turned_out, gated = (sem(n) for n in ("g_normed", "g_turned", "g_tout", "g_gated"))
            shifted, exped, hot, counted = (sem(n) for n in ("g_shifted", "g_exped", "g_hot", "g_counted"))
            placed, sent, consts, b1_turned = (sem(n) for n in ("g_placed", "g_sent", "g_consts", "g_b1t"))
            pool_step = sem("g_pool")
            block = s1.enter_context(nc.Block())

            @block.sync
            def _(sp):
                sp.dma_start(b1r[:, :], b1.rearrange("e (t p) -> (e t) p", p=P)).then_inc(c_in, 16)
                sp.dma_start(b2r[:, :], b2.rearrange("e (t p) -> (e t) p", p=P)).then_inc(c_in, 16)
                sp.dma_start(wg_sb[:, :, :], wg.rearrange("(t p) e -> p t e", p=P)).then_inc(c_in, 16)
                sp.wait_ge(zeroed, 1)
                rows = E * CAP
                for r in range(0, rows, P):
                    n = min(P, rows - r)
                    sp.dma_start(buf[r:r + n, :], zero[0:n, :]).then_inc(zero_out, 16)
                for c in range(2):
                    w1_load(sp, 0, c)
                for c in range(2):
                    w2_load(sp, 0, c)
                sp.wait_ge(zero_out, 16 * -(-rows // P))
                sp.wait_ge(c_in, 48)

            @block.gpsimd
            def _(pool):
                step = chain(pool, pool_step)
                nc.gpsimd.memset(ones[:, :], 1.0).then_inc(consts, 1)
                pool.wait_ge(consts, 1)
                nc.gpsimd.affine_select(out=before[:, :], in_=ones[:, :], compare_op=ALU.is_gt, fill=0.0, base=0,
                                        pattern=[[1, P]], channel_multiplier=-1).then_inc(consts, 1)
                nc.gpsimd.iota(e_no[:, :], pattern=[[1, E]], base=-E, channel_multiplier=0,
                               allow_small_or_imprecise_dtypes=True).then_inc(consts, 1)
                nc.gpsimd.iota(token[:, :], pattern=[[P, B]], base=E * CAP, channel_multiplier=1,
                               allow_small_or_imprecise_dtypes=True).then_inc(consts, 1)
                pool.wait_ge(placed, 1)
                pool.wait_ge(zero_out, 16 * -(-(E * CAP) // P))
                for t in range(B):
                    nc.gpsimd.indirect_dma_start(buf[:, :], bass.IndirectOffsetOnAxis(ap=slot[:, t:t + 1], axis=0),
                                                 xn[:, t, :], None).then_inc(sent, 16)
                pool.wait_ge(sent, 16 * B)

            @block.vector
            def _(dve):
                step = chain(dve, step_done)
                nc.vector.memset(zero[:, :], 0.0).then_inc(zeroed, 1)
                for t in range(B):
                    norm_steps(nc, dve, step, x2, stats, mv, t)
                nc.vector.tensor_scalar_add(veps[:, :], mv[:, :, 1], EPS).then_inc(var_ready, 1)
                dve.wait_ge(std_ready, 1)
                step(nc.vector.reciprocal(rstd[:, :], std[:, :]))
                for t in range(B):
                    nc.vector.tensor_scalar(xn[:, t, :], x2[:, t, :], mv[:, t, 0:1], rstd[:, t:t + 1],
                                            ALU.subtract, ALU.mult).then_inc(normed, 1)
                over = lambda a: a[:, :].unsqueeze(2).to_broadcast([P, B, E])
                dve.wait_ge(gated, B)
                dve.wait_ge(consts, 4)
                step(nc.vector.tensor_reduce(mx[:, :], pg[:, :, :], AX.X, ALU.max))
                nc.vector.tensor_tensor(lm[:, :, :], pg[:, :, :], over(mx), ALU.subtract).then_inc(shifted, 1)
                dve.wait_ge(shifted, 1)
                step(nc.vector.tensor_scalar(cand[:, :, :], lm[:, :, :], 0.0, None, ALU.is_lt))
                step(nc.vector.scalar_tensor_tensor(out=cand[:, :, :], in0=cand[:, :, :], scalar=float(E),
                                                    in1=e_no[:, :].unsqueeze(1).to_broadcast([P, B, E]),
                                                    op0=ALU.mult, op1=ALU.add))
                step(nc.vector.tensor_reduce(top[:, :], cand[:, :, :], AX.X, ALU.min))
                nc.vector.tensor_tensor(oh[:, :, :], e_no[:, :].unsqueeze(1).to_broadcast([P, B, E]), over(top),
                                        ALU.is_equal).then_inc(hot, 1)
                dve.wait_ge(exped, 1)
                step(nc.vector.tensor_reduce(s_[:, :], ex[:, :, :], AX.X, ALU.add))
                step(nc.vector.reciprocal(prob[:, :], s_[:, :]))
                dve.wait_ge(counted, 1)
                step(nc.vector.memset(carry[:, 0, :], 0.0))
                for t in range(1, B):
                    step(nc.vector.tensor_tensor(carry[:, t, :], pc[:, t - 1, :], carry[:, t - 1, :], ALU.add))
                step(nc.vector.tensor_tensor(rk[:, :, :], pr[:, :, :], carry[:, :, :], ALU.add))
                step(nc.vector.tensor_tensor(ro[:, :, :], rk[:, :, :], oh[:, :, :], ALU.mult))
                step(nc.vector.tensor_reduce(rank[:, :], ro[:, :, :], AX.X, ALU.add))
                step(nc.vector.tensor_scalar(valid[:, :], rank[:, :], float(CAP), None, ALU.is_lt))
                step(nc.vector.tensor_scalar(sl[:, 0, :], top[:, :], float(E), float(CAP), ALU.add, ALU.mult))
                step(nc.vector.tensor_tensor(sl[:, 1, :], sl[:, 0, :], rank[:, :], ALU.add))
                step(nc.vector.tensor_tensor(sl[:, 2, :], sl[:, 1, :], token[:, :], ALU.subtract))
                step(nc.vector.tensor_tensor(sl[:, 3, :], sl[:, 2, :], valid[:, :], ALU.mult))
                step(nc.vector.tensor_tensor(sl[:, 0, :], sl[:, 3, :], token[:, :], ALU.add))
                step(nc.vector.tensor_copy(slot[:, :], sl[:, 0, :]))
                step(nc.vector.tensor_scalar(sl[:, 1, :], sl[:, 0, :], float(E * CAP - 1), None, ALU.min))
                step(nc.vector.tensor_copy(yslot[:, :], sl[:, 1, :]))
                nc.vector.tensor_tensor(weight[:, :], prob[:, :], valid[:, :], ALU.mult).then_inc(placed, 1)

            @block.scalar
            def _(act):
                act.wait_ge(var_ready, 1)
                nc.scalar.activation(std[:, :], veps[:, :], ACT.Sqrt).then_inc(std_ready, 1)
                for t in range(B):
                    act.wait_ge(turned, t + 1)
                    if t >= 2:
                        act.wait_ge(gated, t - 1)
                    nc.scalar.copy(xT[:, t % 2, :, :], pt[:, t % 2, :, :]).then_inc(turned_out, 1)
                act.wait_ge(b1_turned, 1)
                nc.scalar.copy(b1T[:, :], pb[:, 0:P]).then_inc(turned_out, 1)
                nc.scalar.copy(b2T[:, :], pb[:, P:P + E * DT]).then_inc(turned_out, 1)
                act.wait_ge(shifted, 1)
                nc.scalar.activation(ex[:, :, :], lm[:, :, :], ACT.Exp).then_inc(exped, 1)

            @block.tensor
            def _(pe):
                pe.wait_ge(c_in, 48)

                def gate(t):
                    pe.wait_ge(turned_out, t + 1)
                    for c in range(DT):
                        last = nc.tensor.matmul(pg[:, t, :], xT[:, t % 2, c, :], wg_sb[:, c, :],
                                                start=c == 0, stop=c == DT - 1)
                    last.then_inc(gated, 1)
                for t in range(B):
                    pe.wait_ge(normed, t + 1)
                    if t >= 2:
                        pe.wait_ge(turned_out, t - 1)
                    for c in range(DT):
                        last = nc.tensor.transpose(pt[:, t % 2, c, :], xn[:, t, P * c:P * c + P], ident[:, :])
                    last.then_inc(turned, 1)
                    if t:
                        gate(t - 1)
                gate(B - 1)
                nc.tensor.transpose(pb[:, 0:P], b1r[:, :], ident[:, :])
                nc.tensor.transpose(pb[:, P:P + E * DT], b2r[:, :], ident[0:E * DT, 0:E * DT]).then_inc(b1_turned, 1)
                pe.wait_ge(hot, 1)
                pe.wait_ge(consts, 2)
                flat = oh[:, :, :].rearrange("p b e -> p (b e)")
                nc.tensor.matmul(pr[:, :, :].rearrange("p b e -> p (b e)"), before[:, :], flat, start=True, stop=True)
                nc.tensor.matmul(pc[:, :, :].rearrange("p b e -> p (b e)"), ones[:, :], flat,
                                 start=True, stop=True).then_inc(counted, 1)

        with ExitStack() as s2:
            NF = F // P
            PAIRS = NF // 2
            eb = sb("f_eb", [P, 2, D], F32, s2)
            xe = sb("f_xe", [P, DT, 2, CAPP], F32R, s2)
            w1p = sb("f_w1", [P, 2, 2, DT, 512], F32R, s2)
            w2p = sb("f_w2", [P, FC, 2, 4, D], F32R, s2)
            mixed = sb("f_mixed", [P, 2, 2, CAPP], F32, s2)
            pre = sb("f_pre", [P, 2, 2, CAPP], F32, s2)
            h32 = sb("f_h32", [P, 2, 2, CAPP], F32, s2)
            hp = sb("f_h", [P, NF, 2, CAPP], F32R, s2)
            ymix = sb("f_ymix", [P, DT, CAPP], F32, s2)
            yT = sb("f_yT", [P, DT, CAPP], F32, s2)
            y = sb("f_y", [P, 2, D], F32, s2)
            ph = ps("f_ph", [P, 4, 512], F32, s2)
            py = ps("f_py", [P, DT, 512], F32, s2)
            eb_in, y_out = sem("f_eb_in"), sem("f_y_out")
            w_hi = [sem("f_w1_hi"), sem("f_w2_hi")]
            w_lo = [sem("f_w1_lo"), sem("f_w2_lo")]
            xt, x_hi, x_lo = sem("f_xt"), sem("f_x_hi"), sem("f_x_lo")
            up, up_mixed, up_sum = sem("f_up"), sem("f_up_mixed"), sem("f_up_sum")
            gelus, h_hi, h_lo = sem("f_gelus"), sem("f_h_hi"), sem("f_h_lo")
            down, y_mixed, y_sum = sem("f_down"), sem("f_y_mixed"), sem("f_y_sum")
            y_back, y_first, y_second = sem("f_y_back"), sem("f_y_first"), sem("f_y_second")
            padded = sem("f_padded")
            block = s2.enter_context(nc.Block())

            @block.sync
            def _(sp):
                def rows_load(e):
                    sp.dma_start(eb[:, 0, :], buf[bass.ds(e * CAP, P), :]).then_inc(eb_in, 16)
                    sp.dma_start(eb[0:OVER, 1, :], buf[bass.ds(e * CAP + P, OVER), :]).then_inc(eb_in, 16)

                def body(e, last):
                    if not last:
                        sp.wait_ge(xt, e + 1)
                        rows_load(e + 1)
                        sp.wait_ge(w_lo[1], FC * e + 3)
                        w2_load(sp, e + 1, 0)
                        sp.wait_ge(w_lo[1], FC * e + 4)
                        w2_load(sp, e + 1, 1)
                        for c in range(2):
                            sp.wait_ge(w_lo[0], FC * e + c + 3)
                            w1_load(sp, e + 1, c)
                        for c in range(2):
                            sp.wait_ge(w_lo[0], FC * e + FC + c + 1)
                            w1_load(sp, e + 1, c + 2)
                        for c in range(2):
                            sp.wait_ge(w_lo[1], FC * e + FC + c + 1)
                            w2_load(sp, e + 1, c + 2)
                    sp.wait_ge(y_first, e + 2)
                    sp.dma_start(ybuf[bass.ds(e * CAP, P), :], y[:, 0, :]).then_inc(y_out, 16)
                    sp.wait_ge(y_second, e + 2)
                    sp.dma_start(ybuf[bass.ds(e * CAP + P, OVER), :], y[0:OVER, 1, :]).then_inc(y_out, 16)
                rows_load(0)
                for c in range(2):
                    sp.wait_ge(w_lo[0], c + 1)
                    w1_load(sp, 0, c + 2)
                for c in range(2):
                    sp.wait_ge(w_lo[1], c + 1)
                    w2_load(sp, 0, c + 2)
                with sp.Fori(0, E - 1) as e:
                    body(e, False)
                body(E - 1, True)
                sp.wait_ge(y_out, 32 * E + 32)

            @block.tensor
            def _(pe):
                def product(out, hi, lo, rows, first, last):
                    nc.tensor.matmul(out[:, 0:2 * CAPP], hi, rows.rearrange("p n s -> p (n s)"), start=first, stop=False)
                    return nc.tensor.matmul(out[:, CAPP:2 * CAPP], lo, rows[:, 0, :], start=False, stop=last)

                def rows_turn(e):
                    pe.wait_ge(eb_in, 32 * e + 32)
                    for c in range(DT):
                        nc.tensor.transpose(ph[:, c, 0:P], eb[:, 0, P * c:P * c + P], ident[:, :])
                        last = nc.tensor.transpose(ph[:, c, P:CAP], eb[0:OVER, 1, P * c:P * c + P], ident[0:OVER, 0:OVER])
                    last.then_inc(xt, 1)

                def body(e, final):
                    pe.wait_ge(x_lo, e + 1)
                    for n in range(PAIRS):
                        if n % 2 == 0:
                            pe.wait_ge(w_lo[0], FC * e + n // 2 + 1)
                        if n >= 2:
                            pe.wait_ge(up_sum, PAIRS * e + n - 1)
                        for t in range(2):
                            f = 2 * n + t
                            for k in range(DT):
                                cols = slice(P * (f % 4), P * (f % 4) + P)
                                last = product(ph[:, f % 4, :], w1p[:, n // 2 % 2, 0, k, cols], w1p[:, n // 2 % 2, 1, k, cols],
                                               xe[:, k, :, :], k == 0, k == DT - 1)
                        last.then_inc(up, 1)
                    if not final:
                        pe.wait_ge(up_sum, PAIRS * e + PAIRS)
                        rows_turn(e + 1)
                    pe.wait_ge(y_first, e + 1)
                    pe.wait_ge(y_second, e + 1)
                    for c in range(FC):
                        pe.wait_ge(w_lo[1], FC * e + c + 1)
                        pe.wait_ge(h_lo, PAIRS * e + 2 * c + 4)
                        for d in range(DT):
                            for k in range(4):
                                cols = slice(P * d, P * d + P)
                                last = product(py[:, d, :], w2p[:, c, 0, k, cols], w2p[:, c, 1, k, cols],
                                               hp[:, 4 * c + k, :, :], c + k == 0, c == FC - 1 and k == 3)
                        last.then_inc(down, 1)
                    pe.wait_ge(y_sum, 2 * e + 2)
                    for c in range(DT):
                        nc.tensor.transpose(py[:, 0, P * c:P * c + P], yT[:, c, 0:P], ident[:, :])
                        last = nc.tensor.transpose(py[0:OVER, 1, P * c:P * c + P], yT[:, c, P:CAP], ident[:, :])
                    last.then_inc(y_back, 1)
                rows_turn(0)
                pe.wait_ge(padded, 1)
                with pe.Fori(0, E - 1) as e:
                    body(e, False)
                body(E - 1, True)

            @block.scalar
            def _(act):
                def split1(e, c, used):
                    act.wait_ge(w_in[0][c % 2], 16 * (2 * e + c // 2 + 1))
                    if used is not None:
                        act.wait_ge(up, used)
                    nc.scalar.copy(w1p[:, c % 2, 0, :, :], raw1[:, c % 2, :, :]).then_inc(w_hi[0], 1)

                def split2(e, c, used):
                    act.wait_ge(w_in[1][c % 2], 16 * (2 * e + c // 2 + 1))
                    if used is not None:
                        act.wait_ge(down, used)
                    nc.scalar.copy(w2p[:, c, 0, :, :], raw2[:, c % 2, :, :]).then_inc(w_hi[1], 1)

                def rows_hi(e):
                    act.wait_ge(xt, e + 1)
                    nc.scalar.copy(xe[:, :, 0, 0:CAP], ph[:, :, 0:CAP]).then_inc(x_hi, 1)

                def body(e, final):
                    for n in range(PAIRS):
                        b = 2 * (n % 2)
                        act.wait_ge(up, PAIRS * e + n + 1)
                        nc.scalar.copy(mixed[:, n % 2, :, :], ph[:, b:b + 2, CAPP:2 * CAPP]).then_inc(up_mixed, 1)
                        if n == 0:
                            split2(e, 3, None)
                        if n in (2, 4):
                            split1(e, n // 2 + 1, PAIRS * e + n)
                        act.wait_ge(up_sum, PAIRS * e + n + 1)
                        act.wait_ge(h_lo, PAIRS * e + n + 1)
                        for t in range(2):
                            last = nc.scalar.activation(h32[:, n % 2, t, :], pre[:, n % 2, t, :], ACT.Gelu,
                                                        bias=b1T[:, bass.ds(e * NF + 2 * n + t, 1)])
                        last.then_inc(gelus, 1)
                    if not final:
                        rows_hi(e + 1)
                        for c in range(2):
                            split1(e + 1, c, PAIRS * e + 2 * c + 6)
                        for c in range(3):
                            split2(e + 1, c, FC * e + c + 1)
                    act.wait_ge(down, FC * e + FC)
                    for d in range(DT):
                        last = nc.scalar.activation(ymix[:, d, :], py[:, d, CAPP:2 * CAPP], ACT.Identity,
                                                    bias=b2T[:, bass.ds(e * DT + d, 1)])
                        if d % 2:
                            last.then_inc(y_mixed, 1)
                    act.wait_ge(y_back, e + 1)
                    act.wait_ge(y_out, 32 * e + 32)
                    nc.scalar.copy(y[:, 0, :], py[:, 0, :]).then_inc(y_first, 1)
                act.sem_inc(y_first, 1)
                rows_hi(0)
                for c in range(2):
                    split1(0, c, None)
                for c in range(3):
                    split2(0, c, None)
                with act.Fori(0, E - 1) as e:
                    body(e, False)
                body(E - 1, True)

            @block.vector
            def _(dve):
                def split1(e, c):
                    dve.wait_ge(w_hi[0], FC * e + c + 1)
                    nc.vector.tensor_tensor(w1p[:, c % 2, 1, :, :], raw1[:, c % 2, :, :], w1p[:, c % 2, 0, :, :].bitcast(F32),
                                            ALU.subtract).then_inc(w_lo[0], 1)

                def split2(e, c):
                    dve.wait_ge(w_hi[1], FC * e + c + 1)
                    nc.vector.tensor_tensor(w2p[:, c, 1, :, :], raw2[:, c % 2, :, :], w2p[:, c, 0, :, :].bitcast(F32),
                                            ALU.subtract).then_inc(w_lo[1], 1)

                def rows_lo(e):
                    dve.wait_ge(x_hi, e + 1)
                    nc.vector.tensor_tensor(xe[:, :, 1, 0:CAP], ph[:, :, 0:CAP], xe[:, :, 0, 0:CAP].bitcast(F32),
                                            ALU.subtract).then_inc(x_lo, 1)

                def body(e, final):
                    for n in range(PAIRS):
                        b = 2 * (n % 2)
                        dve.wait_ge(up_mixed, PAIRS * e + n + 1)
                        nc.vector.tensor_tensor(pre[:, n % 2, :, :], ph[:, b:b + 2, 0:CAPP], mixed[:, n % 2, :, :],
                                                ALU.add).then_inc(up_sum, 1)
                        if n == 0:
                            split2(e, 3)
                        if n in (2, 4):
                            split1(e, n // 2 + 1)
                        dve.wait_ge(gelus, PAIRS * e + n + 1)
                        nc.vector.tensor_copy(hp[:, 2 * n:2 * n + 2, 0, :], h32[:, n % 2, :, :]).then_inc(h_hi, 1)
                        dve.wait_ge(h_hi, PAIRS * e + n + 1)
                        nc.vector.tensor_tensor(hp[:, 2 * n:2 * n + 2, 1, :], h32[:, n % 2, :, :],
                                                hp[:, 2 * n:2 * n + 2, 0, :].bitcast(F32), ALU.subtract).then_inc(h_lo, 1)
                    if not final:
                        rows_lo(e + 1)
                        for c in range(2):
                            split1(e + 1, c)
                        for c in range(3):
                            split2(e + 1, c)
                    for a in range(2):
                        dve.wait_ge(y_mixed, 2 * e + a + 1)
                        nc.vector.tensor_tensor(yT[:, 2 * a:2 * a + 2, :], py[:, 2 * a:2 * a + 2, 0:CAPP],
                                                ymix[:, 2 * a:2 * a + 2, :], ALU.add).then_inc(y_sum, 1)
                    dve.wait_ge(y_back, e + 1)
                    dve.wait_ge(y_out, 32 * e + 32)
                    nc.vector.tensor_copy(y[0:OVER, 1, :], py[0:OVER, 1, :]).then_inc(y_second, 1)
                dve.sem_inc(y_second, 1)
                dve.sem_inc(y_out, 32)
                dve.sem_inc(h_lo, 2)
                nc.vector.memset(xe[:, :, :, CAP:CAPP].bitcast(F32), 0.0).then_inc(padded, 1)
                rows_lo(0)
                for c in range(2):
                    split1(0, c)
                for c in range(3):
                    split2(0, c)
                with dve.Fori(0, E - 1) as e:
                    body(e, False)
                body(E - 1, True)

        with ExitStack() as s3:
            yg = sb("h_y", [P, B, D], F32, s3)
            o = sb("h_o", [P, B, D], F32, s3)
            done, out_done = sem("h_done"), sem("h_out")
            block = s3.enter_context(nc.Block())

            @block.gpsimd
            def _(pool):
                for t in range(B):
                    nc.gpsimd.indirect_dma_start(yg[:, t, :], None, ybuf[:, :],
                                                 bass.IndirectOffsetOnAxis(ap=yslot[:, t:t + 1], axis=0)).then_inc(backs[t], 16)
                for t in range(B):
                    pool.wait_ge(backs[t], 16)

            @block.vector
            def _(dve):
                for t in range(B):
                    dve.wait_ge(backs[t], 16)
                    nc.vector.scalar_tensor_tensor(out=o[:, t, :], in0=yg[:, t, :], scalar=weight[:, t:t + 1],
                                                   in1=x2[:, t, :], op0=ALU.mult, op1=ALU.add).then_inc(done, 1)

            @block.sync
            def _(sp):
                for t in range(B):
                    sp.wait_ge(done, t + 1)
                    sp.dma_start(out[t, :, :], o[:, t, :]).then_inc(out_done, 16)
                sp.wait_ge(out_done, 16 * B)


def perceiver(nc, x, ctx_1024, xWq, xbq, xWk, xbk, xWv, xbv, xWo, xbo, aWq, abq, aWk, abk, aWv, abv, aWo, abo,
              wg, W1, b1, W2, b2, out):
    scratch = lambda name, shape: nc.dram_tensor(name, shape, F32, kind="Internal").ap()
    wk_split = scratch("wk_split", [2, P, DT, XH * DK])
    wv_split = scratch("wv_split", [2, P, DT, XH * DK])
    q_split = scratch("q_split", [XH * DK, B, 2, P])
    o_parts = scratch("o_parts", [B, XH, P, P])
    row_scale = scratch("row_scale", [B, P, XH])
    buf = scratch("expert_rows", [E * CAP + TOK, D])
    ybuf = scratch("expert_results", [E * CAP, D])
    used = []
    with nc.sbuf_tensor("ident", [P, P], F32) as ident:
        prepare(nc, x, xWq, xbq, xWk, xWv, ident, wk_split, wv_split, q_split, used)
        cross_attention(nc, ctx_1024, wk_split, wv_split, q_split, xbk, ident, o_parts, row_scale, used)
        with nc.sbuf_tensor("x12", [P, B, D], F32) as x12:
            self_attention(nc, x, xWo, xbv, xbo, o_parts, row_scale, aWq, abq, aWk, abk, aWv, abv, aWo, abo, ident, x12, used)
            nc.clear_and_free_semaphores(used)
            nc.all_engine_barrier()
            used = []
            experts(nc, x12, wg, W1, b1, W2, b2, ident, buf, ybuf, out, used)


_INS = ["x", "ctx_1024", "L0_xattn_Wq", "L0_xattn_bq", "L0_xattn_Wk", "L0_xattn_bk", "L0_xattn_Wv", "L0_xattn_bv",
        "L0_xattn_Wo", "L0_xattn_bo", "L0_attn_Wq", "L0_attn_bq", "L0_attn_Wk", "L0_attn_bk", "L0_attn_Wv",
        "L0_attn_bv", "L0_attn_Wo", "L0_attn_bo", "L0_ffn_wg", "L0_ffn_W1", "L0_ffn_b1", "L0_ffn_W2", "L0_ffn_b2"]


def kernel(**inputs):
    import numpy as np
    import concourse.bacc as bacc
    from concourse.bass_utils import run_bass_kernel_spmd

    nc = bacc.Bacc("TRN2", target_bir_lowering=False, num_devices=1)
    arrays, args = {}, []
    for name in _INS:
        a = np.ascontiguousarray(inputs[name])
        arrays[f"in_{name}"] = a
        args.append(nc.dram_tensor(f"in_{name}", a.shape, mybir.dt.from_np(a.dtype), kind="ExternalInput").ap())
    out = nc.dram_tensor("out_0", (B, P, D), F32, kind="ExternalOutput").ap()
    perceiver(nc, *args, out)
    r = run_bass_kernel_spmd(nc, [arrays], core_ids=[0])
    return r.results[0]["out_0"]
```

```python
import concourse.bass as bass
from concourse import mybir
from contextlib import ExitStack

F32 = mybir.dt.float32
F32R = mybir.dt.float32r
I32 = mybir.dt.int32
U32 = mybir.dt.uint32
ALU = mybir.AluOpType
ACT = mybir.ActivationFunctionType
AX = mybir.AxisListType

P = 128
B = 8
D = 512
DT = D // P
TOK = B * P
S = 2048
ST = S // P
XH, DK = 16, 64
XG = 4
NCH = S // 512
EPS = 1e-5


def new_semaphore(nc, name, used):
    used.append(nc.alloc_semaphore(name))
    return used[-1]


def cross_attention(nc, ctx, wk_split, wv_split, q_split, bk, ident, o_parts, row_scale, used, batches=B):
    NS = 4
    PIECES = 16 * XG
    FIRST_CTX = 47
    PRO = ST + 16
    PER = PIECES + ST

    def fill_no(m, last=False):
        return m if last else m + 2 * min(max(m - FIRST_CTX + 1, 0), ST // 2)

    def ctx_no(u):
        return FIRST_CTX + 3 * (u // 2) + u % 2

    es = ExitStack()
    with es:
        sb = lambda n, s, d: es.enter_context(nc.sbuf_tensor(n, s, d))
        ps = lambda n, s, d: es.enter_context(nc.psum_tensor(n, s, d))
        sem = lambda n: new_semaphore(nc, n, used)
        stage = sb("ctx_stage", [P, NS, D], F32)
        ctx_hi = sb("ctxT_hi", [P, DT, S], F32R)
        ctx_lo = sb("ctxT_lo", [P, DT, S], F32R)
        wk = sb("wk_pairs", [P, 2, 2, DT, P], F32R)
        wv = sb("wv_group", [P, 2, DT, 256], F32R)
        keys = sb("keys", [P, XG, S], F32R)
        values = sb("values", [P, 2, ST, 4, 2 * DK], F32R)
        q = sb("q", [P, 4, 2, P], F32R)
        probs = sb("probs", [P, S], F32)
        probsT = sb("probsT", [P, 2, 4, 2, P], F32R)
        bk_sb = sb("bk", [DK, XH], F32)
        neg_max = sb("neg_max", [P, 2], F32)
        sums = sb("sums", [P, XH, NCH], F32)
        total = sb("total", [P, XH], F32)
        scale = sb("scale", [P, XH], F32)
        o_copy = sb("o_copy", [P, 2 * P], F32)
        o_half = sb("o_half", [P, 2, P], F32)
        pS = ps("scores", [P, S], F32)
        pJ = ps("fills", [P, 2, 512], F32)
        pT = ps("probsT_ps", [P, 4, P], F32)
        pO = ps("o_ps", [P, 512], F32)

        bias_in = sem("bias_in")
        ctx_in = [sem(f"ctx_in{n}") for n in range(NS)]
        wk_in = [sem("wk_in0"), sem("wk_in1")]
        wv_in = sem("wv_in")
        q_in = [sem(f"q_in{i}") for i in range(4)]
        o_out = [sem("o_out0"), sem("o_out1")]
        scale_out = sem("scale_out")
        filled = sem("filled")
        fill_hi = sem("fill_hi")
        fill_lo = sem("fill_lo")
        scored = sem("scored")
        maxed = sem("maxed")
        exped = sem("exped")
        transposed = sem("transposed")
        pt_hi = sem("pt_hi")
        pt_lo = sem("pt_lo")
        weighed = sem("weighed")
        o_copied = sem("o_copied")
        o_added = sem("o_added")
        totalled = sem("totalled")
        scaled = sem("scaled")

        block = es.enter_context(nc.Block())

        def q_load(sp, b, g, i):
            for u in range(2):
                sp.dma_start(q[64 * u:64 * u + 64, i, :, :].bitcast(F32),
                             q_split[bass.ds((4 * g + i) * DK, DK), b, :, :]).then_inc(q_in[i], 16)

        def wv_load(sp, g):
            for n in range(2):
                sp.dma_start(wv[:, n, :, :].bitcast(F32), wv_split[n, :, :, 256 * g:256 * g + 256]).then_inc(wv_in, 16)

        def wk_load(sp, g, p):
            c = 256 * g + 128 * p
            for n in range(2):
                sp.dma_start(wk[:, p, n, :, :].bitcast(F32), wk_split[n, :, :, c:c + P]).then_inc(wk_in[p], 16)

        def ctx_load(sp, b, u):
            sp.dma_start(stage[:, u % NS, :], ctx[b, P * u:P * u + P, :]).then_inc(ctx_in[u % NS], 16)

        @block.sync
        def _(sp):
            def batch(b, last):
                if not last:
                    for u in range(NS):
                        ctx_load(sp, b + 1, u)
                for g in range(XG):
                    more = not (last and g == XG - 1)
                    for i in range(4):
                        h = 4 * g + i
                        for j in range(4):
                            k = 16 * g + 4 * i + j - FIRST_CTX
                            if not last and 0 <= k < (ST - NS) // 2:
                                sp.wait_ge(filled, PRO + PER * b + ctx_no(2 * k + 1) + 1)
                                ctx_load(sp, b + 1, 2 * k + NS)
                                ctx_load(sp, b + 1, 2 * k + NS + 1)
                            if j == 1 and h > 0:
                                o_store(b, h - 1)
                            if j == 1 and more:
                                sp.wait_ge(scored, 16 * b + h + 1)
                                q_load(sp, b + 1 if g == 3 else b, (g + 1) % XG, i)
                        if i and not (last and g >= 2):
                            sp.wait_ge(filled, PRO + PER * b + fill_no(16 * g + 4 * i + 3) + 1)
                            if i == 1:
                                wv_load(sp, (g + 2) % XG)
                            else:
                                wk_load(sp, (g + 2) % XG, i - 2)
                o_store(b, XH - 1)
                sp.wait_ge(scaled, 16 * b + 16)
                with nc.allow_non_contiguous_dma(reason="one number per token and head"):
                    sp.dma_start(row_scale[b, :, :], scale[:, :]).then_inc(scale_out, 16)

            def o_store(b, h):
                sp.wait_ge(o_added, 16 * b + h + 2)
                sp.dma_start(o_parts[b, h, :, :], o_half[:, h % 2, :]).then_inc(o_out[h % 2], 16)

            with nc.allow_non_contiguous_dma(reason="the bias, once"):
                sp.dma_start(bk_sb[:, :], bk.rearrange("h k -> k h")).then_inc(bias_in, 16)
            for u in range(NS):
                ctx_load(sp, 0, u)
            wv_load(sp, 0)
            wk_load(sp, 0, 0)
            wk_load(sp, 0, 1)
            for i in range(4):
                q_load(sp, 0, 0, i)
            for u in range(NS, ST):
                sp.wait_ge(filled, u - NS + 1)
                ctx_load(sp, 0, u)
            sp.wait_ge(filled, ST + 8)
            wv_load(sp, 1)
            sp.wait_ge(filled, ST + 12)
            wk_load(sp, 1, 0)
            sp.wait_ge(filled, ST + 16)
            wk_load(sp, 1, 1)
            if batches > 1:
                with sp.Fori(0, batches - 1) as b:
                    batch(b, False)
            batch(batches - 1, True)
            for n in range(2):
                sp.wait_ge(o_out[n], 16 * 8 * batches + 16)
            sp.wait_ge(scale_out, 16 * batches + 16)

        @block.tensor
        def _(pe):
            def ctx_fill(no, b, u):
                pe.wait_ge(ctx_in[u % NS], 16 * (ST // NS * b + u // NS + 1))
                pe.wait_ge(fill_lo, no - 1)
                for t in range(DT):
                    last = nc.tensor.transpose(pJ[:, bank[0], P * t:P * t + P],
                                               stage[:, u % NS, P * t:P * t + P], ident[:, :])
                last.then_inc(filled, 1)

            def v_fill(seq, j, i):
                for k in range(2):
                    s = P * (2 * (4 * i + j) + k)
                    for t in range(DT):
                        for n, (c, w) in enumerate(((ctx_hi, 0), (ctx_lo, 0), (ctx_hi, 1))):
                            last = nc.tensor.matmul(pJ[:, bank[0], 256 * k:256 * k + 256], c[:, t, s:s + P],
                                                    wv[:, w, t, :], start=t + n == 0, stop=t == DT - 1 and n == 2)
                last.then_inc(filled, 1)

            def k_fill(p, j):
                for t in range(DT):
                    for n, (w, c) in enumerate(((0, ctx_hi), (0, ctx_lo), (1, ctx_hi))):
                        last = nc.tensor.matmul(pJ[:, bank[0], :], wk[:, p, w, t, :], c[:, t, 512 * j:512 * j + 512],
                                                start=t + n == 0, stop=t == DT - 1 and n == 2)
                last.then_inc(filled, 1)

            bank = [0]

            def fill(no, seq, i, j):
                if j == 0 and i == 0:
                    pe.wait_ge(wv_in, 32 * seq + 32)
                if j == 0 and i >= 2:
                    pe.wait_ge(wk_in[i - 2], 32 * seq + 32)
                pe.wait_ge(fill_lo, no - 1)
                if i < 2:
                    v_fill(seq, j, i)
                else:
                    k_fill(i - 2, j)

            def score(b, h, last=False):
                g, i = h // 4, h % 4
                pe.wait_ge(q_in[i], 128 * b + 32 * (g + 1))
                pe.wait_ge(fill_lo, PER * b + (28 + 4 * (i // 2) if g == 0 else
                                               PRO + fill_no(16 * g - 16 + 11 + 4 * (i // 2), last) + 1))
                if h or not first[0]:
                    pe.wait_ge(exped, 64 * b + 4 * h)
                for c in range(NCH):
                    for n in range(2):
                        last = nc.tensor.matmul(pS[:, 512 * c:512 * c + 512], q[:, i, n, :],
                                                keys[:, i, 512 * c:512 * c + 512], start=n == 0, stop=n == 1)
                last.then_inc(scored, 1)

            def transpose(b, h, j):
                pe.wait_ge(exped, 64 * b + 4 * h + j + 1)
                if h or j:
                    pe.wait_ge(pt_lo, 64 * b + 4 * h + j)
                for k in range(4):
                    last = nc.tensor.transpose(pT[:, k, :], probs[:, P * (4 * j + k):P * (4 * j + k) + P], ident[:, :])
                last.then_inc(transposed, 1)

            def weigh(b, h, j):
                g, i = h // 4, h % 4
                pe.wait_ge(pt_lo, 64 * b + 4 * h + j + 1)
                if j == 0:
                    pe.wait_ge(o_copied, 16 * b + h + 1)
                    pe.wait_ge(fill_lo, PER * b + (24 if g == 0 else PRO + fill_no(16 * g - 16 + 7) + 1))
                for k in range(4):
                    s = 4 * j + k
                    last = nc.tensor.matmul(pO[:, 0:2 * P], values[:, g % 2, s, i, :],
                                            probsT[:, j % 2, k, :, :].rearrange("p n t -> p (n t)"),
                                            start=s == 0, stop=s == ST - 1)
                last.then_inc(weighed, 1)

            first = [True]

            def batch(b, last):
                for g in range(XG):
                    more = not (last and g == XG - 1)
                    for i in range(4):
                        h = 4 * g + i
                        for j in range(4):
                            m = 16 * g + 4 * i + j
                            k = m - FIRST_CTX
                            turn = not last and 0 <= k < ST // 2
                            if turn:
                                bank[0] = ctx_no(2 * k) % 2
                                ctx_fill(PRO + PER * b + ctx_no(2 * k), b + 1, 2 * k)
                            if j:
                                weigh(b, h, j - 1)
                            elif h:
                                weigh(b, h - 1, 3)
                            transpose(b, h, j)
                            if j == 1 and (more or i < 3):
                                score(b, h + 1, last)
                            if turn:
                                bank[0] = ctx_no(2 * k + 1) % 2
                                ctx_fill(PRO + PER * b + ctx_no(2 * k + 1), b + 1, 2 * k + 1)
                            if more:
                                bank[0] = fill_no(m) % 2
                                fill(PRO + PER * b + fill_no(m, last), 4 * b + g + 1, i, j)
                weigh(b, XH - 1, 3)

            for u in range(ST):
                bank[0] = u % 2
                if u >= 2:
                    ctx_fill(u, 0, u)
                else:
                    pe.wait_ge(ctx_in[u], 16)
                    for t in range(DT):
                        last = nc.tensor.transpose(pJ[:, u, P * t:P * t + P], stage[:, u, P * t:P * t + P], ident[:, :])
                    last.then_inc(filled, 1)
            for m in range(16):
                bank[0] = m % 2
                fill(ST + m, 0, m // 4, m % 4)
            score(0, 0)
            first[0] = False
            if batches > 1:
                with pe.Fori(0, batches - 1) as b:
                    batch(b, False)
            batch(batches - 1, True)

        @block.scalar
        def _(act):
            def fill_hi_ctx(no, bk_, u):
                act.wait_ge(filled, no + 1)
                nc.scalar.copy(ctx_hi[:, :, P * u:P * u + P],
                               pJ[:, bk_, :].rearrange("p (t s) -> p t s", t=DT)).then_inc(fill_hi, 1)

            def fill_hi_vk(no, bk_, g, i, j):
                act.wait_ge(filled, no + 1)
                if i < 2:
                    n = 2 * (4 * i + j)
                    nc.scalar.copy(values[:, g % 2, n:n + 2, :, 0:DK],
                                   pJ[:, bk_, :].rearrange("p (s h k) -> p s h k", s=2, h=4)).then_inc(fill_hi, 1)
                    return
                for a in range(2):
                    x = 2 * (i - 2) + a
                    last = nc.scalar.activation(keys[0:DK, x, 512 * j:512 * j + 512], pJ[DK * a:DK * a + DK, bk_, :],
                                                ACT.Identity, bias=bk_sb[:, 4 * g + x:4 * g + x + 1])
                last.then_inc(fill_hi, 1)

            def exp(b, h, c):
                act.wait_ge(maxed, 16 * b + h + 1)
                if h:
                    act.wait_ge(transposed, 64 * b + 4 * (h - 1) + c + 1)
                nc.scalar.activation(probs[:, 512 * c:512 * c + 512], pS[:, 512 * c:512 * c + 512], ACT.Exp,
                                     bias=neg_max[:, h % 2:h % 2 + 1],
                                     accum_out=sums[:, h % XH, c:c + 1]).then_inc(exped, 1)

            def copy_o(b, h):
                act.wait_ge(weighed, 64 * b + 4 * h + 4)
                act.wait_ge(o_added, 16 * b + h + 1)
                nc.scalar.copy(o_copy[:, :], pO[:, 0:2 * P]).then_inc(o_copied, 1)

            def batch(b, last):
                for g in range(XG):
                    more = not (last and g == XG - 1)
                    for i in range(4):
                        h = 4 * g + i
                        for j in range(4):
                            m = 16 * g + 4 * i + j
                            k = m - FIRST_CTX
                            turn = not last and 0 <= k < ST // 2
                            if turn:
                                fill_hi_ctx(PRO + PER * b + ctx_no(2 * k), ctx_no(2 * k) % 2, 2 * k)
                            act.wait_ge(transposed, 64 * b + 4 * h + j + 1)
                            if h or j > 1:
                                act.wait_ge(weighed, 64 * b + 4 * h + j - 1)
                            nc.scalar.copy(probsT[:, j % 2, :, 0, :], pT[:, :, :]).then_inc(pt_hi, 1)
                            if j == 0 and h:
                                copy_o(b, h - 1)
                            if turn:
                                fill_hi_ctx(PRO + PER * b + ctx_no(2 * k + 1), ctx_no(2 * k + 1) % 2, 2 * k + 1)
                            if j >= 2 and (more or i < 3):
                                exp(b, h + 1, 2 * j - 4)
                                exp(b, h + 1, 2 * j - 3)
                            if more:
                                if g and i < 2 and j == 0:
                                    act.wait_ge(weighed, 64 * b + 16 * g)
                                if i >= 2 and j == 0:
                                    act.wait_ge(scored, 16 * b + 4 * g + 2 * (i - 2) + 2)
                                fill_hi_vk(PRO + PER * b + fill_no(m, last), fill_no(m) % 2, (g + 1) % XG, i, j)
                copy_o(b, XH - 1)

            act.sem_inc(o_copied, 1)
            act.wait_ge(bias_in, 16)
            for u in range(ST):
                fill_hi_ctx(u, u % 2, u)
            for m in range(16):
                fill_hi_vk(ST + m, m % 2, 0, m // 4, m % 4)
            for c in range(NCH):
                exp(0, 0, c)
            if batches > 1:
                with act.Fori(0, batches - 1) as b:
                    batch(b, False)
            batch(batches - 1, True)

        @block.vector
        def _(dve):
            def fill_lo_ctx(no, bk_, u):
                dve.wait_ge(fill_hi, no + 1)
                nc.vector.tensor_tensor(ctx_lo[:, :, P * u:P * u + P],
                                        pJ[:, bk_, :].rearrange("p (t s) -> p t s", t=DT),
                                        ctx_hi[:, :, P * u:P * u + P].bitcast(F32), ALU.subtract).then_inc(fill_lo, 1)

            def fill_lo_vk(no, bk_, g, i, j):
                dve.wait_ge(fill_hi, no + 1)
                if i < 2:
                    n = 2 * (4 * i + j)
                    nc.vector.tensor_tensor(values[:, g % 2, n:n + 2, :, DK:2 * DK],
                                            pJ[:, bk_, :].rearrange("p (s h k) -> p s h k", s=2, h=4),
                                            values[:, g % 2, n:n + 2, :, 0:DK].bitcast(F32),
                                            ALU.subtract).then_inc(fill_lo, 1)
                    return
                for a in range(2):
                    x = 2 * (i - 2) + a
                    last = nc.vector.scalar_tensor_tensor(
                        out=keys[DK:P, x, 512 * j:512 * j + 512], in0=pJ[DK * a:DK * a + DK, bk_, :],
                        scalar=bk_sb[:, 4 * g + x:4 * g + x + 1],
                        in1=keys[0:DK, x, 512 * j:512 * j + 512].bitcast(F32), op0=ALU.add, op1=ALU.subtract)
                last.then_inc(fill_lo, 1)

            def maxima(b, h):
                dve.wait_ge(scored, 16 * b + h + 1)
                nc.vector.tensor_reduce(neg_max[:, h % 2:h % 2 + 1], pS[:, :], AX.X, ALU.max,
                                        negate=True).then_inc(maxed, 1)

            def add_o(b, h):
                dve.wait_ge(o_copied, 16 * b + h + 2)
                dve.wait_ge(o_out[h % 2], 128 * b + 16 * (h // 2) + 16)
                nc.vector.tensor_tensor(o_half[:, h % 2, :], o_copy[:, 0:P], o_copy[:, P:2 * P],
                                        ALU.add).then_inc(o_added, 1)

            def row_sum(b, h):
                dve.wait_ge(exped, 64 * b + 4 * h + 4)
                nc.vector.tensor_reduce(total[:, h:h + 1], sums[:, h, :], AX.X, ALU.add).then_inc(totalled, 1)
                dve.wait_ge(totalled, 16 * b + h + 1)
                if h == 0:
                    dve.wait_ge(scale_out, 16 * b + 16)
                nc.vector.reciprocal(scale[:, h:h + 1], total[:, h:h + 1]).then_inc(scaled, 1)

            def batch(b, last):
                for g in range(XG):
                    more = not (last and g == XG - 1)
                    for i in range(4):
                        h = 4 * g + i
                        for j in range(4):
                            m = 16 * g + 4 * i + j
                            k = m - FIRST_CTX
                            turn = not last and 0 <= k < ST // 2
                            if turn:
                                fill_lo_ctx(PRO + PER * b + ctx_no(2 * k), ctx_no(2 * k) % 2, 2 * k)
                            dve.wait_ge(pt_hi, 64 * b + 4 * h + j + 1)
                            nc.vector.tensor_tensor(probsT[:, j % 2, :, 1, :], pT[:, :, :],
                                                    probsT[:, j % 2, :, 0, :].bitcast(F32),
                                                    ALU.subtract).then_inc(pt_lo, 1)
                            if turn:
                                fill_lo_ctx(PRO + PER * b + ctx_no(2 * k + 1), ctx_no(2 * k + 1) % 2, 2 * k + 1)
                            if j == 0 and h:
                                add_o(b, h - 1)
                            if j == 0:
                                row_sum(b, h)
                            if j == 1 and (more or i < 3):
                                maxima(b, h + 1)
                            if more:
                                fill_lo_vk(PRO + PER * b + fill_no(m, last), fill_no(m) % 2, (g + 1) % XG, i, j)
                add_o(b, XH - 1)

            dve.sem_inc(o_added, 1)
            dve.sem_inc(o_out[0], 16)
            dve.sem_inc(o_out[1], 16)
            dve.sem_inc(scale_out, 16)
            dve.wait_ge(bias_in, 16)
            for u in range(ST):
                fill_lo_ctx(u, u % 2, u)
            for m in range(16):
                fill_lo_vk(ST + m, m % 2, 0, m // 4, m % 4)
            maxima(0, 0)
            if batches > 1:
                with dve.Fori(0, batches - 1) as b:
                    batch(b, False)
            batch(batches - 1, True)


def chain(eng, done):
    count = [0]

    def step(ins):
        count[0] += 1
        ins.then_inc(done, 1)
        eng.wait_ge(done, count[0])
    return step


def norm_steps(nc, dve, step, x, stats, mv, t):
    step(nc.vector.bn_stats(stats[:, t, :], x[:, t, :]))
    step(nc.vector.bn_aggr(mv[:, t, :], stats[:, t, :]))


def prepare(nc, x, wq, bq, wk, wv, ident, wk_split, wv_split, q_split, used):
    es = ExitStack()
    with es:
        sb = lambda n, s, d: es.enter_context(nc.sbuf_tensor(n, s, d))
        ps = lambda n, s, d: es.enter_context(nc.psum_tensor(n, s, d))
        sem = lambda n: new_semaphore(nc, n, used)
        xs = sb("p_x", [P, B, D], F32)
        xn = sb("p_xn", [P, B, D], F32)
        xT = sb("p_xT", [P, DT, TOK], F32)
        wq_sb = sb("p_wq", [P, DT, XH * DK], F32)
        w_sb = sb("p_w", [P, 2, DT, XH * DK], F32)
        w_part = sb("p_wpart", [P, 2, DT, XH * DK], F32R)
        bq_sb = sb("p_bq", [P, XH // 2], F32)
        bq8 = sb("p_bq8", [P, XH // 2], F32)
        stats = sb("p_stats", [P, B, 6], F32)
        mv = sb("p_mv", [P, B, 2], F32)
        veps = sb("p_veps", [P, B], F32)
        std = sb("p_std", [P, B], F32)
        rstd = sb("p_rstd", [P, B], F32)
        q32 = sb("p_q32", [P, 2, 512], F32)
        qb = sb("p_qb", [P, 2, 4, 2, P], F32R)
        pt = ps("p_pt", [P, 2, 512], F32)
        pq = ps("p_pq", [P, 4, 512], F32)

        x_in, wq_in, bq_in = sem("p_x_in"), sem("p_wq_in"), sem("p_bq_in")
        w_in = [sem("p_w_in0"), sem("p_w_in1")]
        w_out = sem("p_w_out")
        q_out = [sem("p_q_out0"), sem("p_q_out1")]
        made = sem("p_made")
        step_done = sem("p_step")
        var_ready, std_ready = sem("p_var"), sem("p_std_ready")
        normed = sem("p_normed")
        turned = sem("p_turned")
        turned_out = sem("p_turned_out")
        bias_ready = sem("p_bias8")
        q_done = sem("p_qdone")
        q_copied = sem("p_qcopied")
        q_hi, q_parts = sem("p_qhi"), sem("p_qparts")
        w_hi, w_lo = sem("p_whi"), sem("p_wlo")
        block = es.enter_context(nc.Block())

        @block.sync
        def _(sp):
            sp.dma_start(xs[:, :, :], x.rearrange("b p d -> p b d")).then_inc(x_in, 16)
            with nc.allow_non_contiguous_dma(reason="the bias, once"):
                sp.dma_start(bq_sb[:, :], bq.rearrange("(a u) k -> (u k) a", u=2)).then_inc(bq_in, 16)
            sp.dma_start(wq_sb[:, :, :], wq.rearrange("(t p) h k -> p t (h k)", p=P)).then_inc(wq_in, 16)
            for n, w in enumerate((wk, wv)):
                sp.dma_start(w_sb[:, n, :, :], w.rearrange("(t p) h k -> p t (h k)", p=P)).then_inc(w_in[n], 16)
            for n, out in enumerate((wk_split, wv_split)):
                sp.wait_ge(w_lo, n + 1)
                sp.dma_start(out[0], w_part[:, 0, :, :].bitcast(F32)).then_inc(w_out, 16)
                sp.dma_start(out[1], w_part[:, 1, :, :].bitcast(F32)).then_inc(w_out, 16)
                if n == 0:
                    continue
            for n in range(16):
                pair, half = n // 2, n % 2
                sp.wait_ge(q_parts, n + 1)
                sp.dma_start(q_split[P * pair:P * pair + P, 4 * half:4 * half + 4, :, :],
                             qb[:, n % 2, :, :, :].bitcast(F32)).then_inc(q_out[n % 2], 16)
            sp.wait_ge(w_out, 64)
            for n in range(2):
                sp.wait_ge(q_out[n], 16 * 8)

        @block.gpsimd
        def _(pool):
            nc.gpsimd.memset(ident[:, :], 0.0).then_inc(made, 1)
            pool.wait_ge(made, 1)
            nc.gpsimd.affine_select(out=ident[:, :], in_=ident[:, :], compare_op=ALU.not_equal, fill=1.0,
                                    base=0, pattern=[[-1, P]], channel_multiplier=1).then_inc(made, 1)

        @block.vector
        def _(dve):
            step = chain(dve, step_done)
            dve.wait_ge(x_in, 16)
            for t in range(B):
                norm_steps(nc, dve, step, xs, stats, mv, t)
            nc.vector.tensor_scalar_add(veps[:, :], mv[:, :, 1], EPS).then_inc(var_ready, 1)
            dve.wait_ge(std_ready, 1)
            step(nc.vector.reciprocal(rstd[:, :], std[:, :]))
            for t in range(B):
                nc.vector.tensor_scalar(xn[:, t, :], xs[:, t, :], mv[:, t, 0:1], rstd[:, t:t + 1],
                                        ALU.subtract, ALU.mult).then_inc(normed, 1)
            dve.wait_ge(bq_in, 16)
            nc.vector.tensor_scalar(bq8[:, :], bq_sb[:, :], DK ** -0.5, None, ALU.mult).then_inc(bias_ready, 1)
            for n in range(2):
                dve.wait_ge(w_hi, n + 1)
                nc.vector.tensor_tensor(w_part[:, 1, :, :], w_sb[:, n, :, :], w_part[:, 0, :, :].bitcast(F32),
                                        ALU.subtract).then_inc(w_lo, 1)
            for n in range(16):
                dve.wait_ge(q_copied, n + 1)
                if n >= 2:
                    dve.wait_ge(q_out[n % 2], 16 * (n // 2))
                q4 = q32[:, n % 2, :].rearrange("p (b t) -> p b t", b=4)
                nc.vector.tensor_copy(qb[:, n % 2, :, 0, :], q4).then_inc(q_hi, 1)
                dve.wait_ge(q_hi, n + 1)
                nc.vector.tensor_tensor(qb[:, n % 2, :, 1, :], q4, qb[:, n % 2, :, 0, :].bitcast(F32),
                                        ALU.subtract).then_inc(q_parts, 1)

        @block.scalar
        def _(act):
            act.wait_ge(var_ready, 1)
            nc.scalar.activation(std[:, :], veps[:, :], ACT.Sqrt).then_inc(std_ready, 1)
            for t in range(B):
                act.wait_ge(turned, t + 1)
                nc.scalar.copy(xT[:, :, P * t:P * t + P],
                               pt[:, t % 2, :].rearrange("p (c s) -> p c s", c=DT)).then_inc(turned_out, 1)
            act.wait_ge(w_in[0], 16)
            nc.scalar.copy(w_part[:, 0, :, :], w_sb[:, 0, :, :]).then_inc(w_hi, 1)
            act.wait_ge(w_in[1], 16)
            act.wait_ge(w_out, 32)
            nc.scalar.copy(w_part[:, 0, :, :], w_sb[:, 1, :, :]).then_inc(w_hi, 1)
            act.wait_ge(bias_ready, 1)
            for n in range(16):
                act.wait_ge(q_done, n + 1)
                if n >= 2:
                    act.wait_ge(q_parts, n - 1)
                nc.scalar.activation(q32[:, n % 2, :], pq[:, n % 4, :], ACT.Identity,
                                     bias=bq8[:, n // 2:n // 2 + 1], scale=DK ** -0.5).then_inc(q_copied, 1)

        @block.tensor
        def _(pe):
            pe.wait_ge(made, 2)
            for t in range(B):
                pe.wait_ge(normed, t + 1)
                if t >= 2:
                    pe.wait_ge(turned_out, t - 1)
                for c in range(DT):
                    last = nc.tensor.transpose(pt[:, t % 2, P * c:P * c + P], xn[:, t, P * c:P * c + P], ident[:, :])
                last.then_inc(turned, 1)
            pe.wait_ge(wq_in, 16)
            pe.wait_ge(turned_out, B)
            for n in range(16):
                pair, half = n // 2, n % 2
                if n >= 4:
                    pe.wait_ge(q_copied, n - 3)
                for t in range(DT):
                    last = nc.tensor.matmul(pq[:, n % 4, :], wq_sb[:, t, P * pair:P * pair + P],
                                            xT[:, t, 512 * half:512 * half + 512], start=t == 0, stop=t == DT - 1)
                last.then_inc(q_done, 1)

SH = 8
NM = B * SH
ITERS = 20


def self_attention(nc, x, xo, x_bv, x_bo, o_parts, row_scale, wq, bq, wk, bk, wv, bv, wo, bo, ident, x1, used):
    es = ExitStack()
    with es:
        sb = lambda n, s, d, e=es: e.enter_context(nc.sbuf_tensor(n, s, d))
        ps = lambda n, s, d, e=es: e.enter_context(nc.psum_tensor(n, s, d))
        sem = lambda n: new_semaphore(nc, n, used)
        BF16 = mybir.dt.bfloat16
        v_sb = sb("s_v", [P, B, D], F32)
        AT = sb("s_AT", [P, NM, P], F32)
        s_ = sb("s_rowsum", [P, NM], F32)
        ls = sb("s_ls", [P, NM], F32)
        NQ = NM // 4

        def four(n):
            return slice(4 * n, 4 * n + 4)

        def over(t, n):
            return t[:, four(n)].unsqueeze(2).to_broadcast([P, 4, P])
        half = ExitStack()
        w_p = sb("s_wp", [P, 3, 2, DT, D], F32R, half)
        q_sb = sb("s_q", [P, DT, TOK], F32, half)
        k_sb = sb("s_k", [P, DT, TOK], F32, half)
        bqk = sb("s_bqk", [P, 2, DT], F32, half)
        bq8 = sb("s_bq8", [P, DT], F32, half)
        bvb = sb("s_bv", [P, D], F32, half)
        mv = sb("s_mv", [P, B, 2], F32, half)
        rstd = sb("s_rstd", [P, B], F32, half)
        with half:
            with ExitStack() as s1:
                xo_sb = sb("a_xo", [P, XH // 2, D], F32, s1)
                ua = sb("a_ua", [P, 2, 2, XH // 2, P], F32, s1)
                us = sb("a_us", [P, XH // 2, P], F32, s1)
                oT = sb("a_oT", [P, 2, XH // 2, P], F32, s1)
                rs = sb("a_rs", [P, B, XH], F32, s1)
                rsx = sb("a_rsx", [P, XH // 2, P], F32, s1)
                xbo = sb("a_xbo", [P, D], F32, s1)
                xbv = sb("a_xbv", [P, XH // 2], F32, s1)
                w_raw = sb("a_w", [P, DT, D], F32, s1)
                stats = sb("a_stats", [P, B, 6], F32, s1)
                veps = sb("a_veps", [P, B], F32, s1)
                std = sb("a_std", [P, B], F32, s1)
                pR = ps("a_pR", [P, 2, 2, 4, P], F32, s1)
                pY = ps("a_pY", [P, 2, D], F32, s1)
                pB = ps("a_pB", [P, D], F32, s1)
                xs_in, xo_in, rs_in, c_in = (sem(n) for n in ("a_xs_in", "a_xo_in", "a_rs_in", "a_c_in"))
                w_in, w_hi, w_lo = sem("a_w_in"), sem("a_w_hi"), sem("a_w_lo")
                u_in = [sem("a_u_in0"), sem("a_u_in1")]
                widened, spread, added, merged = sem("a_widened"), sem("a_spread"), sem("a_added"), sem("a_merged")
                bias_made, bias_ready = sem("a_bias_made"), sem("a_bias_ready")
                projected, xb_done = sem("a_projected"), sem("a_xb")
                step_done, var_ready, std_ready = sem("a_step"), sem("a_var"), sem("a_std")
                x1_done = sem("a_x1")
                block = s1.enter_context(nc.Block())

                @block.sync
                def _(sp):
                    def u_load(b):
                        for n in range(2):
                            for u in range(2):
                                sp.dma_start(ua[DK * u:DK * u + DK, b % 2, n, :, :],
                                             o_parts[b].rearrange("(a u) k t -> u k a t", u=2)[u, DK * n:DK * n + DK, :, :]
                                             ).then_inc(u_in[b % 2], 16)
                    sp.dma_start(rs[:, :, :], row_scale.rearrange("b t h -> t b h")).then_inc(rs_in, 16)
                    u_load(0)
                    sp.dma_start(xo_sb[:, :, :], xo.rearrange("(a u) k d -> (u k) a d", u=2)).then_inc(xo_in, 16)
                    with nc.allow_non_contiguous_dma(reason="biases, once"):
                        sp.dma_start(xbv[:, :], x_bv.rearrange("(a u) k -> (u k) a", u=2)).then_inc(xo_in, 16)
                        sp.dma_start(bqk[:, 0, :], bq.rearrange("(t p) -> p t", p=P)).then_inc(c_in, 16)
                        sp.dma_start(bqk[:, 1, :], bk.rearrange("(t p) -> p t", p=P)).then_inc(c_in, 16)
                    for out, src in ((xbo, x_bo), (bvb, bv)):
                        sp.dma_start(out[:, :], src.rearrange("(a d) -> a d", a=1).to_broadcast([P, D])).then_inc(c_in, 16)
                    u_load(1)
                    sp.dma_start(x1[:, :, :], x.rearrange("b p d -> p b d")).then_inc(xs_in, 16)
                    for b in range(2, B):
                        sp.wait_ge(added, b - 1)
                        u_load(b)
                        if b % 2 == 0:
                            n = b // 2 - 1
                            if n:
                                sp.wait_ge(w_lo, n)
                            sp.dma_start(w_raw[:, :, :], (wq, wk, wv)[n].rearrange("(t p) d -> p t d", p=P)).then_inc(w_in, 16)
                    sp.wait_ge(w_in, 48)

                @block.tensor
                def _(pe):
                    def spread_scales(b):
                        pe.wait_ge(widened, b + 1)
                        if b >= 2:
                            pe.wait_ge(merged, b - 1)
                        for a in range(XH // 2):
                            last = nc.tensor.transpose(pR[:, b % 2, a // 4, a % 4, :], rsx[:, a, :], ident[:, :])
                        last.then_inc(spread, 1)
                    spread_scales(0)
                    pe.wait_ge(xo_in, 32)
                    for a in range(XH // 2):
                        last = nc.tensor.matmul(pB[:, :], xbv[:, a:a + 1].to_broadcast([P, P]), xo_sb[:, a, :],
                                                start=a == 0, stop=a == XH // 2 - 1)
                    last.then_inc(bias_made, 1)
                    for b in range(B):
                        if b + 1 < B:
                            spread_scales(b + 1)
                        pe.wait_ge(merged, b + 1)
                        if b >= 2:
                            pe.wait_ge(x1_done, b - 1)
                        for a in range(XH // 2):
                            last = nc.tensor.matmul(pY[:, b % 2, :], oT[:, b % 2, a, :], xo_sb[:, a, :],
                                                    start=a == 0, stop=a == XH // 2 - 1)
                        last.then_inc(projected, 1)

                @block.gpsimd
                def _(pool):
                    for b in range(B):
                        pool.wait_ge(u_in[b % 2], 64 * (b // 2 + 1))
                        if b:
                            pool.wait_ge(merged, b)
                        nc.gpsimd.tensor_tensor(us[:, :, :], ua[:, b % 2, 0, :, :], ua[:, b % 2, 1, :, :],
                                                ALU.add).then_inc(added, 1)
                        if b == 0:
                            pool.wait_ge(bias_ready, 1)
                            pool.wait_ge(xs_in, 16)
                        nc.gpsimd.tensor_tensor(x1[:, b, :], x1[:, b, :], xbo[:, :], ALU.add).then_inc(xb_done, 1)
                        if b in (3, 5, 7):
                            n = b // 2 - 1
                            pool.wait_ge(w_hi, n + 1)
                            nc.gpsimd.tensor_tensor(w_p[:, n, 1, :, :], w_raw[:, :, :], w_p[:, n, 0, :, :].bitcast(F32),
                                                    ALU.subtract).then_inc(w_lo, 1)

                @block.vector
                def _(dve):
                    step = chain(dve, step_done)

                    def residual(b):
                        dve.wait_ge(projected, b + 1)
                        dve.wait_ge(xb_done, b + 1)
                        nc.vector.tensor_tensor(x1[:, b, :], pY[:, b % 2, :], x1[:, b, :], ALU.add).then_inc(x1_done, 1)
                        dve.wait_ge(x1_done, b + 1)
                        norm_steps(nc, dve, step, x1, stats, mv, b)
                    for b in range(B):
                        dve.wait_ge(added, b + 1)
                        dve.wait_ge(spread, b + 1)
                        if b >= 2:
                            dve.wait_ge(projected, b - 1)
                        nc.vector.tensor_tensor(oT[:, b % 2, :, :], us[:, :, :],
                                                pR[:, b % 2, :, :, :].rearrange("p a b t -> p (a b) t"), ALU.mult).then_inc(merged, 1)
                        if b == 0:
                            dve.wait_ge(c_in, 64)
                            dve.wait_ge(bias_made, 1)
                            nc.vector.tensor_tensor(xbo[:, :], pB[:, :], xbo[:, :], ALU.add).then_inc(bias_ready, 1)
                        else:
                            residual(b - 1)
                    residual(B - 1)
                    nc.vector.tensor_scalar_add(veps[:, :], mv[:, :, 1], EPS).then_inc(var_ready, 1)
                    step(nc.vector.tensor_scalar(bq8[:, :], bqk[:, 0, :], DK ** -0.5, None, ALU.mult))
                    dve.wait_ge(std_ready, 1)
                    step(nc.vector.reciprocal(rstd[:, :], std[:, :]))

                @block.scalar
                def _(act):
                    act.wait_ge(rs_in, 16)
                    for b in range(B):
                        if b:
                            act.wait_ge(spread, b)
                        nc.scalar.copy(rsx[:, :, :].rearrange("p a (u k) -> p (a u) k", u=2),
                                       rs[:, b, :].unsqueeze(2).to_broadcast([P, XH, DK])).then_inc(widened, 1)
                        if b in (3, 5, 7):
                            n = b // 2 - 1
                            act.wait_ge(w_in, 16 * n + 16)
                            nc.scalar.copy(w_p[:, n, 0, :, :], w_raw[:, :, :]).then_inc(w_hi, 1)
                    act.wait_ge(var_ready, 1)
                    nc.scalar.activation(std[:, :], veps[:, :], ACT.Sqrt).then_inc(std_ready, 1)

            with ExitStack() as s2:
                lm = AT
                xn = sb("b_xn", [P, 2, D], F32, s2)
                xT = sb("b_xT", [P, 2, DT, TOK], F32R, s2)
                ex = sb("b_ex", [P, 2, 4, P], F32, s2)
                nm = sb("b_nm", [P, NM], F32, s2)
                pt = ps("b_pt", [P, 2, DT, P], F32, s2)
                pw = ps("b_pw", [P, 2, 512], F32, s2)
                pL = ps("b_pL", [P, 2, 4, P], F32, s2)
                normed, x_turned, x_hi, x_lo = (sem(n) for n in ("b_normed_x", "b_x_turned", "b_x_hi", "b_x_lo"))
                made, qk_out, v_out = sem("b_made"), sem("b_qk_out"), sem("b_v_out")
                logits, shifted, exped, summed = (sem(n) for n in ("b_logits", "b_shifted", "b_exped", "b_summed"))
                logged = sem("b_logged")
                step_done = sem("b_step")
                block = s2.enter_context(nc.Block())

                @block.tensor
                def _(pe):
                    def x_turn(t):
                        pe.wait_ge(normed, t + 1)
                        if t >= 2:
                            pe.wait_ge(x_lo, t - 1)
                        for c in range(DT):
                            last = nc.tensor.transpose(pt[:, t % 2, c, :], xn[:, t % 2, P * c:P * c + P], ident[:, :])
                        last.then_inc(x_turned, 1)

                    def queries_keys(n):
                        hf, s, a = n // 8, n // 4 % 2, n % 4
                        pe.wait_ge(x_lo, 4 * hf + 4)
                        if n >= 2:
                            pe.wait_ge(qk_out, n - 1)
                        for t in range(DT):
                            for k, (w, c) in enumerate(((0, 0), (0, 1), (1, 0))):
                                last = nc.tensor.matmul(pw[:, n % 2, :], w_p[:, s, w, t, P * a:P * a + P],
                                                        xT[:, c, t, 512 * hf:512 * hf + 512],
                                                        start=t + k == 0, stop=t == DT - 1 and k == 2)
                        last.then_inc(made, 1)

                    def values(b):
                        if b >= 2:
                            pe.wait_ge(v_out, b - 1)
                        else:
                            pe.wait_ge(qk_out, 15 + b)
                        for t in range(DT):
                            for k, (c, w) in enumerate(((0, 0), (1, 0), (0, 1))):
                                last = nc.tensor.matmul(pw[:, b % 2, :], xT[:, c, t, P * b:P * b + P], w_p[:, 2, w, t, :],
                                                        start=t + k == 0, stop=t == DT - 1 and k == 2)
                        last.then_inc(made, 1)

                    def score(n):
                        b = n // 2
                        pe.wait_ge(qk_out, 8 * (b // 4) + 8)
                        if n >= 2:
                            pe.wait_ge(shifted, n - 1)
                        for k in range(4):
                            h = 2 * k + n % 2
                            r = slice(DK * (h % 2), DK * (h % 2) + DK)
                            last = nc.tensor.matmul(pL[:, n % 2, k, :], q_sb[r, h // 2, P * b:P * b + P],
                                                    k_sb[r, h // 2, P * b:P * b + P], start=True, stop=True)
                        last.then_inc(logits, 1)

                    for t in range(4):
                        x_turn(t)
                    for n in range(8):
                        queries_keys(n)
                        if n < 4:
                            x_turn(4 + n)
                    for n in range(8):
                        queries_keys(8 + n)
                        score(n)
                    for n in range(8):
                        values(n)
                        score(8 + n)
                @block.scalar
                def _(act):
                    def hi(t):
                        act.wait_ge(x_turned, t + 1)
                        nc.scalar.copy(xT[:, 0, :, P * t:P * t + P], pt[:, t % 2, :, :]).then_inc(x_hi, 1)

                    def queries_keys(n):
                        hf, s, a = n // 8, n // 4 % 2, n % 4
                        act.wait_ge(made, n + 1)
                        nc.scalar.activation((q_sb, k_sb)[s][:, a, 512 * hf:512 * hf + 512], pw[:, n % 2, :], ACT.Identity,
                                             bias=bq8[:, a:a + 1] if s == 0 else bqk[:, 1, a:a + 1],
                                             scale=DK ** -0.5 if s == 0 else 1.0).then_inc(qk_out, 1)

                    def exp(n):
                        act.wait_ge(shifted, n + 1)
                        if n >= 2:
                            act.wait_ge(summed, n - 1)
                        nc.scalar.activation(ex[:, n % 2, :, :], lm[:, four(n), :], ACT.Exp).then_inc(exped, 1)
                    for t in range(4):
                        hi(t)
                    for n in range(8):
                        queries_keys(n)
                        if n < 4:
                            hi(4 + n)
                    for n in range(8):
                        queries_keys(8 + n)
                        if n:
                            exp(n - 1)
                    for n in range(7, NQ):
                        exp(n)
                    act.wait_ge(summed, NQ)
                    nc.scalar.activation(ls[:, :], s_[:, :], ACT.Ln).then_inc(logged, 1)

                @block.vector
                def _(dve):
                    step = chain(dve, step_done)

                    def first(n):
                        dve.wait_ge(logits, n + 1)
                        step(nc.vector.tensor_reduce(nm[:, four(n)], pL[:, n % 2, :, :], AX.X, ALU.max, negate=True))
                        nc.vector.tensor_tensor(lm[:, four(n), :], pL[:, n % 2, :, :], over(nm, n), ALU.add).then_inc(shifted, 1)

                    def sums(n):
                        dve.wait_ge(exped, n + 1)
                        nc.vector.tensor_reduce(s_[:, four(n)], ex[:, n % 2, :, :], AX.X, ALU.add).then_inc(summed, 1)

                    def normalise(t):
                        if t >= 2:
                            dve.wait_ge(x_turned, t - 1)
                        nc.vector.tensor_scalar(xn[:, t % 2, :], x1[:, t, :], mv[:, t, 0:1], rstd[:, t:t + 1],
                                                ALU.subtract, ALU.mult).then_inc(normed, 1)

                    def lo(t):
                        dve.wait_ge(x_hi, t + 1)
                        nc.vector.tensor_tensor(xT[:, 1, :, P * t:P * t + P], pt[:, t % 2, :, :],
                                                xT[:, 0, :, P * t:P * t + P].bitcast(F32), ALU.subtract).then_inc(x_lo, 1)

                    def values(b):
                        dve.wait_ge(made, 16 + b + 1)
                        nc.vector.tensor_tensor(v_sb[:, b, :], pw[:, b % 2, :], bvb[:, :], ALU.add).then_inc(v_out, 1)
                    normalise(0)
                    normalise(1)
                    for t in range(B):
                        if t + 2 < B:
                            normalise(t + 2)
                        lo(t)
                    for n in range(NQ):
                        if n >= 8:
                            values(n - 8)
                        first(n)
                        if n:
                            sums(n - 1)
                    sums(NQ - 1)

        bo_sb = sb("s_bo", [P, D], F32)
        wo_sb = sb("s_wo", [P, DT, D], F32)
        wo_in = sem("s_wo_in")
        r32 = sb("s_r32", [P, NM], F32)
        c32 = sb("s_c32", [P, NM], F32)
        with ExitStack() as s3:
            at_p = sb("c_atp", [P, 3, NM, P], BF16, s3)
            a_p = sb("c_ap", [P, 3, NM, P], BF16, s3)
            r_p = sb("c_rp", [P, NM, 3], BF16, s3)
            c_p = sb("c_cp", [P, NM, 3], BF16, s3)
            tot = sb("c_tot", [P, NM], F32, s3)
            left = sb("c_left", [P, NM], F32, s3)
            with ExitStack() as s4:
                la = sb("c_la", [P, 2, 4, P], F32, s4)
                rest_t = sb("c_rest_t", [P, 2, 4, P], F32, s4)
                rest_a = sb("c_rest_a", [P, 2, 4, P], F32, s4)
                nm2 = sb("c_nm2", [P, NM], F32, s4)
                pLT = ps("c_pLT", [P, 2, 4, P], F32, s4)
                pA = ps("c_pA", [P, 2, 4, P], F32, s4)
                normed, turned, maxed, exped = (sem(n) for n in ("c_normed", "c_turned", "c_maxed", "c_exped"))
                t_part1, t_rest, t_part2, t_part3 = (sem(n) for n in ("c_t_part1", "c_t_rest", "c_t_part2", "c_t_part3"))
                a_turned, a_part1, a_rest, a_part2, a_part3 = (sem(n) for n in (
                    "c_a_turned", "c_a_part1", "c_a_rest", "c_a_part2", "c_a_part3"))
                block = s4.enter_context(nc.Block())

                def each_step(*works):
                    for n in range(NQ + 4):
                        for work, lag in works:
                            if 0 <= n - lag < NQ:
                                work(n - lag)

                @block.sync
                def _(sp):
                    sp.dma_start(wo_sb[:, :, :], wo.rearrange("(t p) d -> p t d", p=P)).then_inc(wo_in, 16)
                    sp.dma_start(bo_sb[:, :], bo.rearrange("(a d) -> a d", a=1).to_broadcast([P, D])).then_inc(wo_in, 16)

                @block.gpsimd
                def _(pool):
                    def rows(n):
                        if n >= 2:
                            pool.wait_ge(turned, n - 1)
                        nc.gpsimd.tensor_tensor(la[:, n % 2, :, :], AT[:, four(n), :], over(ls, n), ALU.subtract).then_inc(normed, 1)

                    def t_third(n):
                        pool.wait_ge(t_part2, n + 1)
                        nc.gpsimd.tensor_tensor(at_p[:, 2, four(n), :], rest_t[:, n % 2, :, :], at_p[:, 1, four(n), :],
                                                ALU.subtract).then_inc(t_part3, 1)
                    each_step((rows, 0), (t_third, 3))

                @block.tensor
                def _(pe):
                    def turn(n):
                        pe.wait_ge(normed, n + 1)
                        if n >= 2:
                            pe.wait_ge(exped, n - 1)
                        for k in range(4):
                            last = nc.tensor.transpose(pLT[:, n % 2, k, :], la[:, n % 2, k, :], ident[:, :])
                        last.then_inc(turned, 1)

                    def turn_back(n):
                        pe.wait_ge(exped, n + 1)
                        if n >= 2:
                            pe.wait_ge(a_rest, n - 1)
                        for k in range(4):
                            last = nc.tensor.transpose(pA[:, n % 2, k, :], AT[:, 4 * n + k, :], ident[:, :])
                        last.then_inc(a_turned, 1)
                    each_step((turn, 0), (turn_back, 1))

                @block.scalar
                def _(act):
                    def exp(n):
                        act.wait_ge(maxed, n + 1)
                        for k in range(4):
                            m = 4 * n + k
                            last = nc.scalar.activation(AT[:, m, :], pLT[:, n % 2, k, :], ACT.Exp,
                                                        bias=nm2[:, m:m + 1], accum_out=tot[:, m:m + 1])
                        last.then_inc(exped, 1)

                    def t_first(n):
                        act.wait_ge(exped, n + 1)
                        nc.scalar.copy(at_p[:, 0, four(n), :], AT[:, four(n), :]).then_inc(t_part1, 1)

                    def a_second(n):
                        act.wait_ge(a_rest, n + 1)
                        nc.scalar.copy(a_p[:, 1, four(n), :], rest_a[:, n % 2, :, :]).then_inc(a_part2, 1)

                    def a_first(n):
                        act.wait_ge(a_turned, n + 1)
                        nc.scalar.copy(a_p[:, 0, four(n), :], pA[:, n % 2, :, :]).then_inc(a_part1, 1)
                    each_step((exp, 0), (a_second, 3), (a_first, 1), (t_first, 0))

                @block.vector
                def _(dve):
                    def maxima(n):
                        dve.wait_ge(turned, n + 1)
                        nc.vector.tensor_reduce(nm2[:, four(n)], pLT[:, n % 2, :, :], AX.X, ALU.max, negate=True).then_inc(maxed, 1)

                    def t_second(n):
                        dve.wait_ge(t_part1, n + 1)
                        if n >= 2:
                            dve.wait_ge(t_part3, n - 1)
                        nc.vector.tensor_tensor(rest_t[:, n % 2, :, :], AT[:, four(n), :], at_p[:, 0, four(n), :],
                                                ALU.subtract).then_inc(t_rest, 1)
                        dve.wait_ge(t_rest, n + 1)
                        nc.vector.tensor_copy(at_p[:, 1, four(n), :], rest_t[:, n % 2, :, :]).then_inc(t_part2, 1)

                    def a_remainder(n):
                        dve.wait_ge(a_part1, n + 1)
                        if n >= 2:
                            dve.wait_ge(a_part3, n - 1)
                        nc.vector.tensor_tensor(rest_a[:, n % 2, :, :], pA[:, n % 2, :, :], a_p[:, 0, four(n), :],
                                                ALU.subtract).then_inc(a_rest, 1)

                    def a_third(n):
                        dve.wait_ge(a_part2, n + 1)
                        nc.vector.tensor_tensor(a_p[:, 2, four(n), :], rest_a[:, n % 2, :, :], a_p[:, 1, four(n), :],
                                                ALU.subtract).then_inc(a_part3, 1)
                    each_step((maxima, 0), (a_third, 4), (a_remainder, 2), (t_second, 2))
            with ExitStack() as s5:
                NG, GM = 4, NM // 4
                pV = ps("c_pV", [P, 4, 512], F32, s5)
                r_sums, r_ready = sem("c_r_sums"), sem("c_r_ready")
                c_sums, c_ready = sem("c_c_sums"), sem("c_c_ready")
                step_done, first_done = sem("c_step"), sem("c_first")
                STEPS = 5 * 2 * NG
                block = s5.enter_context(nc.Block())

                @block.tensor
                def _(pe):
                    def products(g, mats, vec, done):
                        for k in range(GM):
                            m = GM * g + k
                            for n in range(3):
                                last = nc.tensor.matmul(pV[:, g, 4 * k:4 * k + 3], mats[:, n, m, :], vec[:, m, :],
                                                        start=n == 0, stop=n == 2)
                        last.then_inc(done, 1)
                    with pe.Fori(0, ITERS - 1) as it:
                        for g in range(NG):
                            pe.wait_ge(c_ready, NG * it + g + 1)
                            products(g, at_p, c_p, r_sums)
                        for g in range(NG):
                            pe.wait_ge(r_ready, NG * it + g + 1)
                            products(g, a_p, r_p, c_sums)

                @block.vector
                def _(dve):
                    def invert(it, no, g, sums, v32, v_p, ready):
                        s = slice(GM * g, GM * g + GM)
                        base = STEPS * it + 5 * no
                        dve.wait_ge(sums, NG * it + g + 1)
                        nc.vector.tensor_reduce(tot[:, s], pV[:, g, 0:4 * GM].rearrange("p (m n) -> p m n", n=4)[:, :, 0:3],
                                                AX.X, ALU.add).then_inc(step_done, 1)
                        dve.wait_ge(step_done, base + 1)
                        nc.vector.reciprocal(v32[:, s], tot[:, s]).then_inc(step_done, 1)
                        dve.wait_ge(step_done, base + 2)
                        nc.vector.tensor_copy(v_p[:, s, 0], v32[:, s]).then_inc(step_done, 1)
                        dve.wait_ge(step_done, base + 3)
                        nc.vector.tensor_tensor(left[:, s], v32[:, s], v_p[:, s, 0], ALU.subtract).then_inc(step_done, 1)
                        dve.wait_ge(step_done, base + 4)
                        nc.vector.tensor_copy(v_p[:, s, 1], left[:, s]).then_inc(step_done, 1)
                        dve.wait_ge(step_done, base + 5)
                        nc.vector.tensor_tensor(v_p[:, s, 2], left[:, s], v_p[:, s, 1], ALU.subtract).then_inc(ready, 1)
                    step = chain(dve, first_done)
                    step(nc.vector.reciprocal(c32[:, :], tot[:, :]))
                    step(nc.vector.tensor_copy(c_p[:, :, 0], c32[:, :]))
                    step(nc.vector.tensor_tensor(left[:, :], c32[:, :], c_p[:, :, 0], ALU.subtract))
                    step(nc.vector.tensor_copy(c_p[:, :, 1], left[:, :]))
                    nc.vector.tensor_tensor(c_p[:, :, 2], left[:, :], c_p[:, :, 1], ALU.subtract).then_inc(c_ready, NG)
                    with dve.Fori(0, ITERS - 1) as it:
                        for g in range(NG):
                            invert(it, g, g, r_sums, r32, r_p, r_ready)
                        for g in range(NG):
                            invert(it, NG + g, g, c_sums, c32, c_p, c_ready)

        with ExitStack() as s6:
            cv = sb("d_cv", [P, 2, D], F32, s6)
            o = sb("d_o", [P, 2, D], F32, s6)
            oT = sb("d_oT", [P, 2, DT, P], F32, s6)
            pO = ps("d_pO", [P, 2, D], F32, s6)
            pt = ps("d_pt", [P, 2, DT, P], F32, s6)
            pY = ps("d_pY", [P, 2, D], F32, s6)
            weighted, summed, scaled, turned = (sem(n) for n in ("d_weighted", "d_summed", "d_scaled", "d_turned"))
            turned_out, projected, added, biased = (sem(n) for n in ("d_tout", "d_proj", "d_added", "d_biased"))
            block = s6.enter_context(nc.Block())

            def by_parity(rows):
                return rows.rearrange("p (a u k) -> p u a k", a=SH // 2, u=2)

            def spread(scales, b):
                return scales[:, SH * b:SH * b + SH].rearrange("p (u a) -> p u a", u=2).unsqueeze(3).to_broadcast(
                    [P, 2, SH // 2, DK])

            @block.gpsimd
            def _(pool):
                pool.wait_ge(wo_in, 32)
                for b in range(B):
                    nc.gpsimd.tensor_tensor(x1[:, b, :], x1[:, b, :], bo_sb[:, :], ALU.add).then_inc(biased, 1)

            @block.vector
            def _(dve):
                def weight(b):
                    if b >= 2:
                        dve.wait_ge(summed, b - 1)
                    nc.vector.tensor_tensor(by_parity(cv[:, b % 2, :]), by_parity(v_sb[:, b, :]), spread(c32, b),
                                            ALU.mult).then_inc(weighted, 1)

                def add(b):
                    dve.wait_ge(projected, b + 1)
                    dve.wait_ge(biased, b + 1)
                    nc.vector.tensor_tensor(x1[:, b, :], pY[:, b % 2, :], x1[:, b, :], ALU.add).then_inc(added, 1)
                weight(0)
                for b in range(B):
                    if b + 1 < B:
                        weight(b + 1)
                    dve.wait_ge(summed, b + 1)
                    if b >= 2:
                        dve.wait_ge(turned, b - 1)
                    nc.vector.tensor_tensor(by_parity(o[:, b % 2, :]), by_parity(pO[:, b % 2, :]), spread(r32, b),
                                            ALU.mult).then_inc(scaled, 1)
                    if b:
                        add(b - 1)
                add(B - 1)

            @block.tensor
            def _(pe):
                def attend(b):
                    pe.wait_ge(weighted, b + 1)
                    if b >= 2:
                        pe.wait_ge(scaled, b - 1)
                    for h in range(SH):
                        last = nc.tensor.matmul(pO[:, b % 2, DK * h:DK * h + DK], AT[:, SH * b + 4 * (h % 2) + h // 2, :],
                                                cv[:, b % 2, DK * h:DK * h + DK], start=True, stop=True)
                    last.then_inc(summed, 1)
                attend(0)
                pe.wait_ge(wo_in, 32)
                for b in range(B):
                    if b + 1 < B:
                        attend(b + 1)
                    pe.wait_ge(scaled, b + 1)
                    if b >= 2:
                        pe.wait_ge(turned_out, b - 1)
                    for c in range(DT):
                        last = nc.tensor.transpose(pt[:, b % 2, c, :], o[:, b % 2, P * c:P * c + P], ident[:, :])
                    last.then_inc(turned, 1)
                    pe.wait_ge(turned_out, b + 1)
                    if b >= 2:
                        pe.wait_ge(added, b - 1)
                    for c in range(DT):
                        last = nc.tensor.matmul(pY[:, b % 2, :], oT[:, b % 2, c, :], wo_sb[:, c, :],
                                                start=c == 0, stop=c == DT - 1)
                    last.then_inc(projected, 1)

            @block.scalar
            def _(act):
                for b in range(B):
                    act.wait_ge(turned, b + 1)
                    if b >= 2:
                        act.wait_ge(projected, b - 1)
                    nc.scalar.copy(oT[:, b % 2, :, :], pt[:, b % 2, :, :]).then_inc(turned_out, 1)

E = 8
F = 2048
CAP = 161
CAPP = 162
OVER = CAP - P
FC = 4


def experts(nc, x2, wg, w1, b1, w2, b2, ident, buf, ybuf, out, used):
    es = ExitStack()
    with es:
        sb = lambda n, s, d, e=es: e.enter_context(nc.sbuf_tensor(n, s, d))
        ps = lambda n, s, d, e=es: e.enter_context(nc.psum_tensor(n, s, d))
        sem = lambda n: new_semaphore(nc, n, used)
        raw1 = sb("e_raw1", [P, 2, DT, 512], F32)
        raw2 = sb("e_raw2", [P, 2, 4, D], F32)
        w_in = [[sem(f"e_w{a}_in{n}") for n in range(2)] for a in (1, 2)]
        backs = [sem(f"h_back{t}") for t in range(B)]
        b1T = sb("e_b1T", [P, E * F // P], F32)
        b2T = sb("e_b2T", [P, E * DT], F32)
        slot = sb("e_slot", [P, B], U32)
        yslot = sb("e_yslot", [P, B], U32)
        weight = sb("e_weight", [P, B], F32)

        def w1_load(eng, e, c):
            eng.dma_start(raw1[:, c % 2, :, :], w1[e].rearrange("(t p) f -> p t f", p=P)[:, :, 512 * c:512 * c + 512]
                          ).then_inc(w_in[0][c % 2], 16)

        def w2_load(eng, e, c):
            eng.dma_start(raw2[:, c % 2, :, :], w2[e].rearrange("(c t p) d -> p c t d", p=P, c=FC)[:, c, :, :]
                          ).then_inc(w_in[1][c % 2], 16)

        with ExitStack() as s1:
            xn = sb("g_xn", [P, B, D], F32, s1)
            xT = sb("g_xT", [P, 2, DT, P], F32, s1)
            zero = sb("g_zero", [P, D], F32, s1)
            wg_sb = sb("g_wg", [P, DT, E], F32, s1)
            b1r = sb("g_b1", [P, P], F32, s1)
            b2r = sb("g_b2", [E * DT, P], F32, s1)
            stats = sb("g_stats", [P, B, 6], F32, s1)
            mv = sb("g_mv", [P, B, 2], F32, s1)
            veps = sb("g_veps", [P, B], F32, s1)
            std = sb("g_std", [P, B], F32, s1)
            rstd = sb("g_rstd", [P, B], F32, s1)
            before = sb("g_before", [P, P], F32, s1)
            ones = sb("g_ones", [P, P], F32, s1)
            e_no = sb("g_eno", [P, E], F32, s1)
            token = sb("g_token", [P, B], F32, s1)
            mx = sb("g_mx", [P, B], F32, s1)
            lm = sb("g_lm", [P, B, E], F32, s1)
            ex = sb("g_ex", [P, B, E], F32, s1)
            s_ = sb("g_s", [P, B], F32, s1)
            prob = sb("g_prob", [P, B], F32, s1)
            cand = sb("g_cand", [P, B, E], F32, s1)
            top = sb("g_top", [P, B], F32, s1)
            oh = sb("g_oh", [P, B, E], F32, s1)
            carry = sb("g_carry", [P, B, E], F32, s1)
            rk = sb("g_rk", [P, B, E], F32, s1)
            ro = sb("g_ro", [P, B, E], F32, s1)
            rank = sb("g_rank", [P, B], F32, s1)
            valid = sb("g_valid", [P, B], F32, s1)
            sl = sb("g_sl", [P, 4, B], F32, s1)
            pt = ps("g_pt", [P, 2, DT, P], F32, s1)
            pg = ps("g_pg", [P, B, E], F32, s1)
            pr = ps("g_pr", [P, B, E], F32, s1)
            pc = ps("g_pc", [P, B, E], F32, s1)
            pb = ps("g_pb", [P, P + E * DT], F32, s1)
            c_in, zeroed, zero_out = sem("g_c_in"), sem("g_zeroed"), sem("g_zero_out")
            step_done, var_ready, std_ready = sem("g_step"), sem("g_var"), sem("g_std")
            normed, turned, turned_out, gated = (sem(n) for n in ("g_normed", "g_turned", "g_tout", "g_gated"))
            shifted, exped, hot, counted = (sem(n) for n in ("g_shifted", "g_exped", "g_hot", "g_counted"))
            placed, sent, consts, b1_turned = (sem(n) for n in ("g_placed", "g_sent", "g_consts", "g_b1t"))
            pool_step = sem("g_pool")
            block = s1.enter_context(nc.Block())

            @block.sync
            def _(sp):
                sp.dma_start(b1r[:, :], b1.rearrange("e (t p) -> (e t) p", p=P)).then_inc(c_in, 16)
                sp.dma_start(b2r[:, :], b2.rearrange("e (t p) -> (e t) p", p=P)).then_inc(c_in, 16)
                sp.dma_start(wg_sb[:, :, :], wg.rearrange("(t p) e -> p t e", p=P)).then_inc(c_in, 16)
                sp.wait_ge(zeroed, 1)
                rows = E * CAP
                for r in range(0, rows, P):
                    n = min(P, rows - r)
                    sp.dma_start(buf[r:r + n, :], zero[0:n, :]).then_inc(zero_out, 16)
                for c in range(2):
                    w1_load(sp, 0, c)
                for c in range(2):
                    w2_load(sp, 0, c)
                sp.wait_ge(zero_out, 16 * -(-rows // P))
                sp.wait_ge(c_in, 48)

            @block.gpsimd
            def _(pool):
                step = chain(pool, pool_step)
                nc.gpsimd.memset(ones[:, :], 1.0).then_inc(consts, 1)
                pool.wait_ge(consts, 1)
                nc.gpsimd.affine_select(out=before[:, :], in_=ones[:, :], compare_op=ALU.is_gt, fill=0.0, base=0,
                                        pattern=[[1, P]], channel_multiplier=-1).then_inc(consts, 1)
                nc.gpsimd.iota(e_no[:, :], pattern=[[1, E]], base=-E, channel_multiplier=0,
                               allow_small_or_imprecise_dtypes=True).then_inc(consts, 1)
                nc.gpsimd.iota(token[:, :], pattern=[[P, B]], base=E * CAP, channel_multiplier=1,
                               allow_small_or_imprecise_dtypes=True).then_inc(consts, 1)
                pool.wait_ge(placed, 1)
                pool.wait_ge(zero_out, 16 * -(-(E * CAP) // P))
                for t in range(B):
                    nc.gpsimd.indirect_dma_start(buf[:, :], bass.IndirectOffsetOnAxis(ap=slot[:, t:t + 1], axis=0),
                                                 xn[:, t, :], None).then_inc(sent, 16)
                pool.wait_ge(sent, 16 * B)

            @block.vector
            def _(dve):
                step = chain(dve, step_done)
                nc.vector.memset(zero[:, :], 0.0).then_inc(zeroed, 1)
                for t in range(B):
                    norm_steps(nc, dve, step, x2, stats, mv, t)
                nc.vector.tensor_scalar_add(veps[:, :], mv[:, :, 1], EPS).then_inc(var_ready, 1)
                dve.wait_ge(std_ready, 1)
                step(nc.vector.reciprocal(rstd[:, :], std[:, :]))
                for t in range(B):
                    nc.vector.tensor_scalar(xn[:, t, :], x2[:, t, :], mv[:, t, 0:1], rstd[:, t:t + 1],
                                            ALU.subtract, ALU.mult).then_inc(normed, 1)
                over = lambda a: a[:, :].unsqueeze(2).to_broadcast([P, B, E])
                dve.wait_ge(gated, B)
                dve.wait_ge(consts, 4)
                step(nc.vector.tensor_reduce(mx[:, :], pg[:, :, :], AX.X, ALU.max))
                nc.vector.tensor_tensor(lm[:, :, :], pg[:, :, :], over(mx), ALU.subtract).then_inc(shifted, 1)
                dve.wait_ge(shifted, 1)
                step(nc.vector.tensor_scalar(cand[:, :, :], lm[:, :, :], 0.0, None, ALU.is_lt))
                step(nc.vector.scalar_tensor_tensor(out=cand[:, :, :], in0=cand[:, :, :], scalar=float(E),
                                                    in1=e_no[:, :].unsqueeze(1).to_broadcast([P, B, E]),
                                                    op0=ALU.mult, op1=ALU.add))
                step(nc.vector.tensor_reduce(top[:, :], cand[:, :, :], AX.X, ALU.min))
                nc.vector.tensor_tensor(oh[:, :, :], e_no[:, :].unsqueeze(1).to_broadcast([P, B, E]), over(top),
                                        ALU.is_equal).then_inc(hot, 1)
                dve.wait_ge(exped, 1)
                step(nc.vector.tensor_reduce(s_[:, :], ex[:, :, :], AX.X, ALU.add))
                step(nc.vector.reciprocal(prob[:, :], s_[:, :]))
                dve.wait_ge(counted, 1)
                step(nc.vector.memset(carry[:, 0, :], 0.0))
                for t in range(1, B):
                    step(nc.vector.tensor_tensor(carry[:, t, :], pc[:, t - 1, :], carry[:, t - 1, :], ALU.add))
                step(nc.vector.tensor_tensor(rk[:, :, :], pr[:, :, :], carry[:, :, :], ALU.add))
                step(nc.vector.tensor_tensor(ro[:, :, :], rk[:, :, :], oh[:, :, :], ALU.mult))
                step(nc.vector.tensor_reduce(rank[:, :], ro[:, :, :], AX.X, ALU.add))
                step(nc.vector.tensor_scalar(valid[:, :], rank[:, :], float(CAP), None, ALU.is_lt))
                step(nc.vector.tensor_scalar(sl[:, 0, :], top[:, :], float(E), float(CAP), ALU.add, ALU.mult))
                step(nc.vector.tensor_tensor(sl[:, 1, :], sl[:, 0, :], rank[:, :], ALU.add))
                step(nc.vector.tensor_tensor(sl[:, 2, :], sl[:, 1, :], token[:, :], ALU.subtract))
                step(nc.vector.tensor_tensor(sl[:, 3, :], sl[:, 2, :], valid[:, :], ALU.mult))
                step(nc.vector.tensor_tensor(sl[:, 0, :], sl[:, 3, :], token[:, :], ALU.add))
                step(nc.vector.tensor_copy(slot[:, :], sl[:, 0, :]))
                step(nc.vector.tensor_scalar(sl[:, 1, :], sl[:, 0, :], float(E * CAP - 1), None, ALU.min))
                step(nc.vector.tensor_copy(yslot[:, :], sl[:, 1, :]))
                nc.vector.tensor_tensor(weight[:, :], prob[:, :], valid[:, :], ALU.mult).then_inc(placed, 1)

            @block.scalar
            def _(act):
                act.wait_ge(var_ready, 1)
                nc.scalar.activation(std[:, :], veps[:, :], ACT.Sqrt).then_inc(std_ready, 1)
                for t in range(B):
                    act.wait_ge(turned, t + 1)
                    if t >= 2:
                        act.wait_ge(gated, t - 1)
                    nc.scalar.copy(xT[:, t % 2, :, :], pt[:, t % 2, :, :]).then_inc(turned_out, 1)
                act.wait_ge(b1_turned, 1)
                nc.scalar.copy(b1T[:, :], pb[:, 0:P]).then_inc(turned_out, 1)
                nc.scalar.copy(b2T[:, :], pb[:, P:P + E * DT]).then_inc(turned_out, 1)
                act.wait_ge(shifted, 1)
                nc.scalar.activation(ex[:, :, :], lm[:, :, :], ACT.Exp).then_inc(exped, 1)

            @block.tensor
            def _(pe):
                pe.wait_ge(c_in, 48)

                def gate(t):
                    pe.wait_ge(turned_out, t + 1)
                    for c in range(DT):
                        last = nc.tensor.matmul(pg[:, t, :], xT[:, t % 2, c, :], wg_sb[:, c, :],
                                                start=c == 0, stop=c == DT - 1)
                    last.then_inc(gated, 1)
                for t in range(B):
                    pe.wait_ge(normed, t + 1)
                    if t >= 2:
                        pe.wait_ge(turned_out, t - 1)
                    for c in range(DT):
                        last = nc.tensor.transpose(pt[:, t % 2, c, :], xn[:, t, P * c:P * c + P], ident[:, :])
                    last.then_inc(turned, 1)
                    if t:
                        gate(t - 1)
                gate(B - 1)
                nc.tensor.transpose(pb[:, 0:P], b1r[:, :], ident[:, :])
                nc.tensor.transpose(pb[:, P:P + E * DT], b2r[:, :], ident[0:E * DT, 0:E * DT]).then_inc(b1_turned, 1)
                pe.wait_ge(hot, 1)
                pe.wait_ge(consts, 2)
                flat = oh[:, :, :].rearrange("p b e -> p (b e)")
                nc.tensor.matmul(pr[:, :, :].rearrange("p b e -> p (b e)"), before[:, :], flat, start=True, stop=True)
                nc.tensor.matmul(pc[:, :, :].rearrange("p b e -> p (b e)"), ones[:, :], flat,
                                 start=True, stop=True).then_inc(counted, 1)

        with ExitStack() as s2:
            NF = F // P
            PAIRS = NF // 2
            eb = sb("f_eb", [P, 2, D], F32, s2)
            xe = sb("f_xe", [P, DT, 2, CAPP], F32R, s2)
            w1p = sb("f_w1", [P, 2, 2, DT, 512], F32R, s2)
            w2p = sb("f_w2", [P, FC, 2, 4, D], F32R, s2)
            mixed = sb("f_mixed", [P, 2, 2, CAPP], F32, s2)
            pre = sb("f_pre", [P, 2, 2, CAPP], F32, s2)
            h32 = sb("f_h32", [P, 2, 2, CAPP], F32, s2)
            hp = sb("f_h", [P, NF, 2, CAPP], F32R, s2)
            ymix = sb("f_ymix", [P, DT, CAPP], F32, s2)
            yT = sb("f_yT", [P, DT, CAPP], F32, s2)
            y = sb("f_y", [P, 2, D], F32, s2)
            ph = ps("f_ph", [P, 4, 512], F32, s2)
            py = ps("f_py", [P, DT, 512], F32, s2)
            eb_in, y_out = sem("f_eb_in"), sem("f_y_out")
            w_hi = [sem("f_w1_hi"), sem("f_w2_hi")]
            w_lo = [sem("f_w1_lo"), sem("f_w2_lo")]
            xt, x_hi, x_lo = sem("f_xt"), sem("f_x_hi"), sem("f_x_lo")
            up, up_mixed, up_sum = sem("f_up"), sem("f_up_mixed"), sem("f_up_sum")
            gelus, h_hi, h_lo = sem("f_gelus"), sem("f_h_hi"), sem("f_h_lo")
            down, y_mixed, y_sum = sem("f_down"), sem("f_y_mixed"), sem("f_y_sum")
            y_back, y_first, y_second = sem("f_y_back"), sem("f_y_first"), sem("f_y_second")
            padded = sem("f_padded")
            w2_late = sem("f_w2_late")
            block = s2.enter_context(nc.Block())

            def lo_ready(eng, e, c):
                if c < 2:
                    eng.wait_ge(w_lo[1], 2 * e + c + 1)
                else:
                    eng.wait_ge(w2_late, 2 * e + c - 1)

            def up_banks(n):
                return (ph, py)[n // 2 % 2][:, 2 * (n % 2):2 * (n % 2) + 2, :]

            def each_expert(eng, body):
                body(0, True, False)
                with eng.Fori(1, E - 1) as e:
                    body(e, False, False)
                body(E - 1, False, True)

            @block.sync
            def _(sp):
                def rows_load(e):
                    sp.dma_start(eb[:, 0, :], buf[bass.ds(e * CAP, P), :]).then_inc(eb_in, 16)
                    sp.dma_start(eb[0:OVER, 1, :], buf[bass.ds(e * CAP + P, OVER), :]).then_inc(eb_in, 16)

                def store(e):
                    sp.wait_ge(y_first, e + 1)
                    sp.dma_start(ybuf[bass.ds(e * CAP, P), :], y[:, 0, :]).then_inc(y_out, 16)
                    sp.wait_ge(y_second, e + 1)
                    sp.dma_start(ybuf[bass.ds(e * CAP + P, OVER), :], y[0:OVER, 1, :]).then_inc(y_out, 16)

                def body(e, first, final):
                    if not final:
                        sp.wait_ge(xt, e + 1)
                        rows_load(e + 1)
                    if not first:
                        store(e - 1)
                    if not final:
                        for c in range(2):
                            sp.wait_ge(w_lo[0], PAIRS * e + 2 * c + 6)
                            w1_load(sp, e + 1, c)
                        for c in range(2):
                            lo_ready(sp, e, c + 2)
                            w2_load(sp, e + 1, c)
                        for c in range(2):
                            sp.wait_ge(w_lo[0], PAIRS * e + PAIRS + 2 * c + 2)
                            w1_load(sp, e + 1, c + 2)
                        for c in range(2):
                            lo_ready(sp, e + 1, c)
                            w2_load(sp, e + 1, c + 2)
                rows_load(0)
                for c in range(2):
                    sp.wait_ge(w_lo[0], 2 * c + 2)
                    w1_load(sp, 0, c + 2)
                for c in range(2):
                    lo_ready(sp, 0, c)
                    w2_load(sp, 0, c + 2)
                each_expert(sp, body)
                store(E - 1)
                sp.wait_ge(y_out, 32 * E + 32)

            @block.tensor
            def _(pe):
                def product(out, hi, lo, rows, start, stop):
                    nc.tensor.matmul(out[:, 0:2 * CAPP], hi, rows.rearrange("p n s -> p (n s)"), start=start, stop=False)
                    return nc.tensor.matmul(out[:, CAPP:2 * CAPP], lo, rows[:, 0, :], start=False, stop=stop)

                def rows_turn(e):
                    pe.wait_ge(eb_in, 32 * e + 32)
                    for c in range(DT):
                        nc.tensor.transpose(ph[:, c, 0:P], eb[:, 0, P * c:P * c + P], ident[:, :])
                        last = nc.tensor.transpose(ph[:, c, P:CAP], eb[0:OVER, 1, P * c:P * c + P], ident[0:OVER, 0:OVER])
                    last.then_inc(xt, 1)

                def results_turn(e):
                    pe.wait_ge(y_sum, 2 * e + 2)
                    for c in range(DT):
                        nc.tensor.transpose(py[:, 2, P * c:P * c + P], yT[:, c, 0:P], ident[:, :])
                        last = nc.tensor.transpose(py[0:OVER, 3, P * c:P * c + P], yT[:, c, P:CAP], ident[:, :])
                    last.then_inc(y_back, 1)

                def body(e, first, final):
                    pe.wait_ge(x_lo, e + 1)
                    for n in range(PAIRS):
                        pe.wait_ge(w_lo[0], PAIRS * e + n + 1)
                        if n >= 4:
                            pe.wait_ge(up_sum, PAIRS * e + n - 3)
                        if n == 3 and not first:
                            pe.wait_ge(y_first, e)
                            pe.wait_ge(y_second, e)
                        for t in range(2):
                            f = 2 * n + t
                            for k in range(DT):
                                cols = slice(P * (f % 4), P * (f % 4) + P)
                                last = product(up_banks(n)[:, t, :], w1p[:, n // 2 % 2, 0, k, cols],
                                               w1p[:, n // 2 % 2, 1, k, cols], xe[:, k, :, :], k == 0, k == DT - 1)
                        last.then_inc(up, 1)
                        if n == 0 and not first:
                            results_turn(e - 1)
                    if not final:
                        pe.wait_ge(up_sum, PAIRS * e + PAIRS - 2)
                        rows_turn(e + 1)
                    for c in range(FC):
                        lo_ready(pe, e, c)
                        pe.wait_ge(h_lo, PAIRS * e + 2 * c + 4)
                        for d in range(DT):
                            if c == 0 and d % 2 == 0:
                                pe.wait_ge(up_sum, PAIRS * e + PAIRS - 1 + d // 2)
                            for k in range(4):
                                cols = slice(P * d, P * d + P)
                                last = product(py[:, d, :], w2p[:, c, 0, k, cols], w2p[:, c, 1, k, cols],
                                               hp[:, 4 * c + k, :, :], c + k == 0, c == FC - 1 and k == 3)
                        last.then_inc(down, 1)
                rows_turn(0)
                pe.wait_ge(padded, 1)
                each_expert(pe, body)
                results_turn(E - 1)

            @block.scalar
            def _(act):
                def split1(e, n, used):
                    c, cols = n // 2, slice(2 * P * (n % 2), 2 * P * (n % 2) + 2 * P)
                    act.wait_ge(w_in[0][c % 2], 16 * (2 * e + c // 2 + 1))
                    if used is not None:
                        act.wait_ge(up, used)
                    nc.scalar.copy(w1p[:, c % 2, 0, :, cols], raw1[:, c % 2, :, cols]).then_inc(w_hi[0], 1)

                def split2(e, c, used):
                    act.wait_ge(w_in[1][c % 2], 16 * (2 * e + c // 2 + 1))
                    if used is not None:
                        act.wait_ge(down, used)
                    nc.scalar.copy(w2p[:, c, 0, :, :], raw2[:, c % 2, :, :]).then_inc(w_hi[1], 1)

                def rows_hi(e):
                    act.wait_ge(xt, e + 1)
                    nc.scalar.copy(xe[:, :, 0, 0:CAP], ph[:, :, 0:CAP]).then_inc(x_hi, 1)

                def results_out(e):
                    act.wait_ge(y_back, e + 1)
                    act.wait_ge(y_out, 32 * e + 32)
                    nc.scalar.copy(y[:, 0, :], py[:, 2, :]).then_inc(y_first, 1)

                def body(e, first, final):
                    for n in range(PAIRS + 1):
                        if n < PAIRS:
                            act.wait_ge(up, PAIRS * e + n + 1)
                            nc.scalar.copy(mixed[:, n % 2, :, :], up_banks(n)[:, :, CAPP:2 * CAPP]).then_inc(up_mixed, 1)
                        if n == 0 and not first:
                            results_out(e - 1)
                        if n:
                            m = n - 1
                            act.wait_ge(up_sum, PAIRS * e + m + 1)
                            if m >= 2 or not first:
                                act.wait_ge(h_lo, PAIRS * e + m + 1)
                            for t in range(2):
                                last = nc.scalar.activation(h32[:, m % 2, t, :], pre[:, m % 2, t, :], ACT.Gelu,
                                                            bias=b1T[:, bass.ds(e * NF + 2 * m + t, 1)])
                            last.then_inc(gelus, 1)
                        if n < 4:
                            split1(e, n + 4, PAIRS * e + n + 1)
                        if n in (4, 6):
                            split2(e, n // 2, None)
                    if not final:
                        rows_hi(e + 1)
                        for n in range(4):
                            split1(e + 1, n, PAIRS * e + n + 5)
                        for c in range(2):
                            split2(e + 1, c, FC * e + c + 1)
                    act.wait_ge(down, FC * e + FC)
                    for d in range(DT):
                        last = nc.scalar.activation(ymix[:, d, :], py[:, d, CAPP:2 * CAPP], ACT.Identity,
                                                    bias=b2T[:, bass.ds(e * DT + d, 1)])
                        if d % 2:
                            last.then_inc(y_mixed, 1)
                rows_hi(0)
                for n in range(4):
                    split1(0, n, None)
                for c in range(2):
                    split2(0, c, None)
                each_expert(act, body)
                results_out(E - 1)

            @block.gpsimd
            def _(pool):
                def body(e, first, final):
                    for c in range(2, FC):
                        pool.wait_ge(w_hi[1], FC * e + c + 1)
                        nc.gpsimd.tensor_tensor(w2p[:, c, 1, :, :], raw2[:, c % 2, :, :],
                                                w2p[:, c, 0, :, :].bitcast(F32), ALU.subtract).then_inc(w2_late, 1)
                each_expert(pool, body)

            @block.vector
            def _(dve):
                def split1(e, n):
                    c, cols = n // 2, slice(2 * P * (n % 2), 2 * P * (n % 2) + 2 * P)
                    dve.wait_ge(w_hi[0], PAIRS * e + n + 1)
                    nc.vector.tensor_tensor(w1p[:, c % 2, 1, :, cols], raw1[:, c % 2, :, cols], w1p[:, c % 2, 0, :, cols].bitcast(F32),
                                            ALU.subtract).then_inc(w_lo[0], 1)

                def split2(e, c):
                    dve.wait_ge(w_hi[1], FC * e + c + 1)
                    nc.vector.tensor_tensor(w2p[:, c, 1, :, :], raw2[:, c % 2, :, :], w2p[:, c, 0, :, :].bitcast(F32),
                                            ALU.subtract).then_inc(w_lo[1], 1)

                def rows_lo(e):
                    dve.wait_ge(x_hi, e + 1)
                    nc.vector.tensor_tensor(xe[:, :, 1, 0:CAP], ph[:, :, 0:CAP], xe[:, :, 0, 0:CAP].bitcast(F32),
                                            ALU.subtract).then_inc(x_lo, 1)

                def results_out(e):
                    dve.wait_ge(y_back, e + 1)
                    dve.wait_ge(y_out, 32 * e + 32)
                    nc.vector.tensor_copy(y[0:OVER, 1, :], py[0:OVER, 3, :]).then_inc(y_second, 1)

                def body(e, first, final):
                    for n in range(PAIRS + 1):
                        if n < PAIRS:
                            dve.wait_ge(up_mixed, PAIRS * e + n + 1)
                            nc.vector.tensor_tensor(pre[:, n % 2, :, :], up_banks(n)[:, :, 0:CAPP], mixed[:, n % 2, :, :],
                                                    ALU.add).then_inc(up_sum, 1)
                        if n == 0 and not first:
                            results_out(e - 1)
                        if n:
                            m = n - 1
                            dve.wait_ge(gelus, PAIRS * e + m + 1)
                            nc.vector.tensor_copy(hp[:, 2 * m:2 * m + 2, 0, :], h32[:, m % 2, :, :]).then_inc(h_hi, 1)
                            dve.wait_ge(h_hi, PAIRS * e + m + 1)
                            nc.vector.tensor_tensor(hp[:, 2 * m:2 * m + 2, 1, :], h32[:, m % 2, :, :],
                                                    hp[:, 2 * m:2 * m + 2, 0, :].bitcast(F32), ALU.subtract).then_inc(h_lo, 1)
                        if n < 4:
                            split1(e, n + 4)
                    if not final:
                        rows_lo(e + 1)
                        for n in range(4):
                            split1(e + 1, n)
                        for c in range(2):
                            split2(e + 1, c)
                    for a in range(2):
                        dve.wait_ge(y_mixed, 2 * e + a + 1)
                        nc.vector.tensor_tensor(yT[:, 2 * a:2 * a + 2, :], py[:, 2 * a:2 * a + 2, 0:CAPP],
                                                ymix[:, 2 * a:2 * a + 2, :], ALU.add).then_inc(y_sum, 1)
                dve.sem_inc(y_out, 32)
                dve.sem_inc(h_lo, 2)
                nc.vector.memset(xe[:, :, :, CAP:CAPP].bitcast(F32), 0.0).then_inc(padded, 1)
                rows_lo(0)
                for n in range(4):
                    split1(0, n)
                for c in range(2):
                    split2(0, c)
                each_expert(dve, body)
                results_out(E - 1)

        with ExitStack() as s3:
            yg = sb("h_y", [P, B, D], F32, s3)
            o = sb("h_o", [P, B, D], F32, s3)
            done, out_done = sem("h_done"), sem("h_out")
            block = s3.enter_context(nc.Block())

            @block.gpsimd
            def _(pool):
                for t in range(B):
                    nc.gpsimd.indirect_dma_start(yg[:, t, :], None, ybuf[:, :],
                                                 bass.IndirectOffsetOnAxis(ap=yslot[:, t:t + 1], axis=0)).then_inc(backs[t], 16)
                for t in range(B):
                    pool.wait_ge(backs[t], 16)

            @block.vector
            def _(dve):
                for t in range(B):
                    dve.wait_ge(backs[t], 16)
                    nc.vector.scalar_tensor_tensor(out=o[:, t, :], in0=yg[:, t, :], scalar=weight[:, t:t + 1],
                                                   in1=x2[:, t, :], op0=ALU.mult, op1=ALU.add).then_inc(done, 1)

            @block.sync
            def _(sp):
                for t in range(B):
                    sp.wait_ge(done, t + 1)
                    sp.dma_start(out[t, :, :], o[:, t, :]).then_inc(out_done, 16)
                sp.wait_ge(out_done, 16 * B)


def perceiver(nc, x, ctx_1024, xWq, xbq, xWk, xbk, xWv, xbv, xWo, xbo, aWq, abq, aWk, abk, aWv, abv, aWo, abo,
              wg, W1, b1, W2, b2, out):
    scratch = lambda name, shape: nc.dram_tensor(name, shape, F32, kind="Internal").ap()
    wk_split = scratch("wk_split", [2, P, DT, XH * DK])
    wv_split = scratch("wv_split", [2, P, DT, XH * DK])
    q_split = scratch("q_split", [XH * DK, B, 2, P])
    o_parts = scratch("o_parts", [B, XH, P, P])
    row_scale = scratch("row_scale", [B, P, XH])
    buf = scratch("expert_rows", [E * CAP + TOK, D])
    ybuf = scratch("expert_results", [E * CAP, D])
    used = []
    with nc.sbuf_tensor("ident", [P, P], F32) as ident:
        prepare(nc, x, xWq, xbq, xWk, xWv, ident, wk_split, wv_split, q_split, used)
        cross_attention(nc, ctx_1024, wk_split, wv_split, q_split, xbk, ident, o_parts, row_scale, used)
        with nc.sbuf_tensor("x12", [P, B, D], F32) as x12:
            self_attention(nc, x, xWo, xbv, xbo, o_parts, row_scale, aWq, abq, aWk, abk, aWv, abv, aWo, abo, ident, x12, used)
            nc.clear_and_free_semaphores(used)
            nc.all_engine_barrier()
            used = []
            experts(nc, x12, wg, W1, b1, W2, b2, ident, buf, ybuf, out, used)


_INS = ["x", "ctx_1024", "L0_xattn_Wq", "L0_xattn_bq", "L0_xattn_Wk", "L0_xattn_bk", "L0_xattn_Wv", "L0_xattn_bv",
        "L0_xattn_Wo", "L0_xattn_bo", "L0_attn_Wq", "L0_attn_bq", "L0_attn_Wk", "L0_attn_bk", "L0_attn_Wv",
        "L0_attn_bv", "L0_attn_Wo", "L0_attn_bo", "L0_ffn_wg", "L0_ffn_W1", "L0_ffn_b1", "L0_ffn_W2", "L0_ffn_b2"]


def kernel(**inputs):
    import numpy as np
    import concourse.bacc as bacc
    from concourse.bass_utils import run_bass_kernel_spmd

    nc = bacc.Bacc("TRN2", target_bir_lowering=False, num_devices=1)
    arrays, args = {}, []
    for name in _INS:
        a = np.ascontiguousarray(inputs[name])
        arrays[f"in_{name}"] = a
        args.append(nc.dram_tensor(f"in_{name}", a.shape, mybir.dt.from_np(a.dtype), kind="ExternalInput").ap())
    out = nc.dram_tensor("out_0", (B, P, D), F32, kind="ExternalOutput").ap()
    perceiver(nc, *args, out)
    r = run_bass_kernel_spmd(nc, [arrays], core_ids=[0])
    return r.results[0]["out_0"]
```

```python
import concourse.bass as bass
from concourse import mybir
from contextlib import ExitStack

F32 = mybir.dt.float32
F32R = mybir.dt.float32r
I32 = mybir.dt.int32
U32 = mybir.dt.uint32
ALU = mybir.AluOpType
ACT = mybir.ActivationFunctionType
AX = mybir.AxisListType

P = 128
B = 8
D = 512
DT = D // P
TOK = B * P
S = 2048
ST = S // P
XH, DK = 16, 64
XG = 4
NCH = S // 512
EPS = 1e-5


def new_semaphore(nc, name, used):
    used.append(nc.alloc_semaphore(name))
    return used[-1]


def cross_attention(nc, ctx, wk_split, wv_split, q_split, bk, ident, o_parts, row_scale, used, batches=B):
    NS = 4
    PIECES = 16 * XG
    FIRST_CTX = 47
    PRO = ST + 16
    PER = PIECES + ST

    def fill_no(m, last=False):
        return m if last else m + 2 * min(max(m - FIRST_CTX + 1, 0), ST // 2)

    def ctx_no(u):
        return FIRST_CTX + 3 * (u // 2) + u % 2

    es = ExitStack()
    with es:
        sb = lambda n, s, d: es.enter_context(nc.sbuf_tensor(n, s, d))
        ps = lambda n, s, d: es.enter_context(nc.psum_tensor(n, s, d))
        sem = lambda n: new_semaphore(nc, n, used)
        stage = sb("ctx_stage", [P, NS, D], F32)
        ctx_hi = sb("ctxT_hi", [P, DT, S], F32R)
        ctx_lo = sb("ctxT_lo", [P, DT, S], F32R)
        wk = sb("wk_pairs", [P, 2, 2, DT, P], F32R)
        wv = sb("wv_group", [P, 2, DT, 256], F32R)
        keys = sb("keys", [P, XG, S], F32R)
        values = sb("values", [P, 2, ST, 4, 2 * DK], F32R)
        q = sb("q", [P, 4, 2, P], F32R)
        probs = sb("probs", [P, S], F32)
        probsT = sb("probsT", [P, 2, 4, 2, P], F32R)
        bk_sb = sb("bk", [DK, XH], F32)
        neg_max = sb("neg_max", [P, 2], F32)
        sums = sb("sums", [P, XH, NCH], F32)
        total = sb("total", [P, XH], F32)
        scale = sb("scale", [P, XH], F32)
        o_copy = sb("o_copy", [P, 2 * P], F32)
        o_half = sb("o_half", [P, 2, P], F32)
        pS = ps("scores", [P, S], F32)
        pJ = ps("fills", [P, 2, 512], F32)
        pT = ps("probsT_ps", [P, 4, P], F32)
        pO = ps("o_ps", [P, 512], F32)

        bias_in = sem("bias_in")
        ctx_in = [sem(f"ctx_in{n}") for n in range(NS)]
        wk_in = [sem("wk_in0"), sem("wk_in1")]
        wv_in = sem("wv_in")
        q_in = [sem(f"q_in{i}") for i in range(4)]
        o_out = [sem("o_out0"), sem("o_out1")]
        scale_out = sem("scale_out")
        filled = sem("filled")
        fill_hi = sem("fill_hi")
        fill_lo = sem("fill_lo")
        scored = sem("scored")
        maxed = sem("maxed")
        exped = sem("exped")
        transposed = sem("transposed")
        pt_hi = sem("pt_hi")
        pt_lo = sem("pt_lo")
        weighed = sem("weighed")
        o_copied = sem("o_copied")
        o_added = sem("o_added")
        totalled = sem("totalled")
        scaled = sem("scaled")

        block = es.enter_context(nc.Block())

        def turned_bank(alone, j):
            return pJ[:, 0, :].rearrange("p (k t) -> p k t", k=4) if alone and j % 2 else pT[:, :, :]

        def q_load(sp, b, g, i):
            for u in range(2):
                sp.dma_start(q[64 * u:64 * u + 64, i, :, :].bitcast(F32),
                             q_split[bass.ds((4 * g + i) * DK, DK), b, :, :]).then_inc(q_in[i], 16)

        def wv_load(sp, g):
            for n in range(2):
                sp.dma_start(wv[:, n, :, :].bitcast(F32), wv_split[n, :, :, 256 * g:256 * g + 256]).then_inc(wv_in, 16)

        def wk_load(sp, g, p):
            c = 256 * g + 128 * p
            for n in range(2):
                sp.dma_start(wk[:, p, n, :, :].bitcast(F32), wk_split[n, :, :, c:c + P]).then_inc(wk_in[p], 16)

        def ctx_load(sp, b, u):
            sp.dma_start(stage[:, u % NS, :], ctx[b, P * u:P * u + P, :]).then_inc(ctx_in[u % NS], 16)

        @block.sync
        def _(sp):
            def batch(b, last):
                if not last:
                    for u in range(NS):
                        ctx_load(sp, b + 1, u)
                for g in range(XG):
                    more = not (last and g == XG - 1)
                    for i in range(4):
                        h = 4 * g + i
                        for j in range(4):
                            k = 16 * g + 4 * i + j - FIRST_CTX
                            if not last and 0 <= k < (ST - NS) // 2:
                                sp.wait_ge(filled, PRO + PER * b + ctx_no(2 * k + 1) + 1)
                                ctx_load(sp, b + 1, 2 * k + NS)
                                ctx_load(sp, b + 1, 2 * k + NS + 1)
                            if j == 1 and h > 0:
                                o_store(b, h - 1)
                            if j == 1 and more:
                                sp.wait_ge(scored, 16 * b + h + 1)
                                q_load(sp, b + 1 if g == 3 else b, (g + 1) % XG, i)
                        if i and not (last and g >= 2):
                            sp.wait_ge(filled, PRO + PER * b + fill_no(16 * g + 4 * i + 3) + 1)
                            if i == 1:
                                wv_load(sp, (g + 2) % XG)
                            else:
                                wk_load(sp, (g + 2) % XG, i - 2)
                o_store(b, XH - 1)
                sp.wait_ge(scaled, 16 * b + 16)
                with nc.allow_non_contiguous_dma(reason="one number per token and head"):
                    sp.dma_start(row_scale[b, :, :], scale[:, :]).then_inc(scale_out, 16)

            def o_store(b, h):
                sp.wait_ge(o_added, 16 * b + h + 2)
                sp.dma_start(o_parts[b, h, :, :], o_half[:, h % 2, :]).then_inc(o_out[h % 2], 16)

            with nc.allow_non_contiguous_dma(reason="the bias, once"):
                sp.dma_start(bk_sb[:, :], bk.rearrange("h k -> k h")).then_inc(bias_in, 16)
            for u in range(NS):
                ctx_load(sp, 0, u)
            for u in range(NS, ST):
                sp.wait_ge(filled, u - NS + 1)
                ctx_load(sp, 0, u)
                if u == NS + 1:
                    wv_load(sp, 0)
            wk_load(sp, 0, 0)
            for i in range(4):
                q_load(sp, 0, 0, i)
            wk_load(sp, 0, 1)
            sp.wait_ge(filled, ST + 8)
            wv_load(sp, 1)
            sp.wait_ge(filled, ST + 12)
            wk_load(sp, 1, 0)
            sp.wait_ge(filled, ST + 16)
            wk_load(sp, 1, 1)
            if batches > 1:
                with sp.Fori(0, batches - 1) as b:
                    batch(b, False)
            batch(batches - 1, True)
            for n in range(2):
                sp.wait_ge(o_out[n], 16 * 8 * batches + 16)
            sp.wait_ge(scale_out, 16 * batches + 16)

        @block.tensor
        def _(pe):
            def ctx_fill(no, b, u):
                pe.wait_ge(ctx_in[u % NS], 16 * (ST // NS * b + u // NS + 1))
                pe.wait_ge(fill_lo, no - 1)
                for t in range(DT):
                    last = nc.tensor.transpose(pJ[:, bank[0], P * t:P * t + P],
                                               stage[:, u % NS, P * t:P * t + P], ident[:, :])
                last.then_inc(filled, 1)

            def v_fill(seq, j, i):
                for k in range(2):
                    s = P * (2 * (4 * i + j) + k)
                    for t in range(DT):
                        for n, (c, w) in enumerate(((ctx_hi, 0), (ctx_lo, 0), (ctx_hi, 1))):
                            last = nc.tensor.matmul(pJ[:, bank[0], 256 * k:256 * k + 256], c[:, t, s:s + P],
                                                    wv[:, w, t, :], start=t + n == 0, stop=t == DT - 1 and n == 2)
                last.then_inc(filled, 1)

            def k_fill(p, j):
                for t in range(DT):
                    for n, (w, c) in enumerate(((0, ctx_hi), (0, ctx_lo), (1, ctx_hi))):
                        last = nc.tensor.matmul(pJ[:, bank[0], :], wk[:, p, w, t, :], c[:, t, 512 * j:512 * j + 512],
                                                start=t + n == 0, stop=t == DT - 1 and n == 2)
                last.then_inc(filled, 1)

            bank = [0]

            def fill(no, seq, i, j):
                if j == 0 and i == 0:
                    pe.wait_ge(wv_in, 32 * seq + 32)
                if j == 0 and i >= 2:
                    pe.wait_ge(wk_in[i - 2], 32 * seq + 32)
                pe.wait_ge(fill_lo, no - 1)
                if i < 2:
                    v_fill(seq, j, i)
                else:
                    k_fill(i - 2, j)

            def score(b, h, last=False):
                g, i = h // 4, h % 4
                pe.wait_ge(q_in[i], 128 * b + 32 * (g + 1))
                pe.wait_ge(fill_lo, PER * b + (28 + 4 * (i // 2) if g == 0 else
                                               PRO + fill_no(16 * g - 16 + 11 + 4 * (i // 2), last) + 1))
                if h or not first[0]:
                    pe.wait_ge(exped, 64 * b + 4 * h)
                for c in range(NCH):
                    for n in range(2):
                        last = nc.tensor.matmul(pS[:, 512 * c:512 * c + 512], q[:, i, n, :],
                                                keys[:, i, 512 * c:512 * c + 512], start=n == 0, stop=n == 1)
                last.then_inc(scored, 1)

            def transpose(b, h, j, alone):
                pe.wait_ge(exped, 64 * b + 4 * h + j + 1)
                if alone and 4 * h + j > 16 * (XG - 1):
                    pe.wait_ge(pt_lo, 64 * b + 4 * h + j - 1)
                elif h or j:
                    pe.wait_ge(pt_lo, 64 * b + 4 * h + j)
                for k in range(4):
                    last = nc.tensor.transpose(turned_bank(alone, j)[:, k, :], probs[:, P * (4 * j + k):P * (4 * j + k) + P], ident[:, :])
                last.then_inc(transposed, 1)

            def weigh(b, h, j):
                g, i = h // 4, h % 4
                pe.wait_ge(pt_lo, 64 * b + 4 * h + j + 1)
                if j == 0:
                    pe.wait_ge(o_copied, 16 * b + h + 1)
                    pe.wait_ge(fill_lo, PER * b + (24 if g == 0 else PRO + fill_no(16 * g - 16 + 7) + 1))
                for k in range(4):
                    s = 4 * j + k
                    last = nc.tensor.matmul(pO[:, 0:2 * P], values[:, g % 2, s, i, :],
                                            probsT[:, j % 2, k, :, :].rearrange("p n t -> p (n t)"),
                                            start=s == 0, stop=s == ST - 1)
                last.then_inc(weighed, 1)

            first = [True]

            def batch(b, last):
                for g in range(XG):
                    more = not (last and g == XG - 1)
                    if not more:
                        pe.wait_ge(fill_lo, PRO + PER * b + fill_no(16 * g - 1, last) + 1)
                    for i in range(4):
                        h = 4 * g + i
                        for j in range(4):
                            m = 16 * g + 4 * i + j
                            k = m - FIRST_CTX
                            turn = not last and 0 <= k < ST // 2
                            if turn:
                                bank[0] = ctx_no(2 * k) % 2
                                ctx_fill(PRO + PER * b + ctx_no(2 * k), b + 1, 2 * k)
                            if not more:
                                transpose(b, h, j, True)
                            if j:
                                weigh(b, h, j - 1)
                            elif h:
                                weigh(b, h - 1, 3)
                            if more:
                                transpose(b, h, j, False)
                            if j == (1 if more else 0) and (more or i < 3):
                                score(b, h + 1, last)
                            if turn:
                                bank[0] = ctx_no(2 * k + 1) % 2
                                ctx_fill(PRO + PER * b + ctx_no(2 * k + 1), b + 1, 2 * k + 1)
                            if more:
                                bank[0] = fill_no(m) % 2
                                fill(PRO + PER * b + fill_no(m, last), 4 * b + g + 1, i, j)
                weigh(b, XH - 1, 3)

            for u in range(ST):
                bank[0] = u % 2
                if u >= 2:
                    ctx_fill(u, 0, u)
                else:
                    pe.wait_ge(ctx_in[u], 16)
                    for t in range(DT):
                        last = nc.tensor.transpose(pJ[:, u, P * t:P * t + P], stage[:, u, P * t:P * t + P], ident[:, :])
                    last.then_inc(filled, 1)
            for m in range(16):
                if m == 14:
                    score(0, 0)
                    first[0] = False
                bank[0] = m % 2
                fill(ST + m, 0, m // 4, m % 4)
            if batches > 1:
                with pe.Fori(0, batches - 1) as b:
                    batch(b, False)
            batch(batches - 1, True)

        @block.scalar
        def _(act):
            def fill_hi_ctx(no, bk_, u):
                act.wait_ge(filled, no + 1)
                nc.scalar.copy(ctx_hi[:, :, P * u:P * u + P],
                               pJ[:, bk_, :].rearrange("p (t s) -> p t s", t=DT)).then_inc(fill_hi, 1)

            def fill_hi_vk(no, bk_, g, i, j):
                act.wait_ge(filled, no + 1)
                if i < 2:
                    n = 2 * (4 * i + j)
                    nc.scalar.copy(values[:, g % 2, n:n + 2, :, 0:DK],
                                   pJ[:, bk_, :].rearrange("p (s h k) -> p s h k", s=2, h=4)).then_inc(fill_hi, 1)
                    return
                for a in range(2):
                    x = 2 * (i - 2) + a
                    last = nc.scalar.activation(keys[0:DK, x, 512 * j:512 * j + 512], pJ[DK * a:DK * a + DK, bk_, :],
                                                ACT.Identity, bias=bk_sb[:, 4 * g + x:4 * g + x + 1])
                last.then_inc(fill_hi, 1)

            def exp(b, h, c):
                act.wait_ge(maxed, 16 * b + h + 1)
                if h:
                    act.wait_ge(transposed, 64 * b + 4 * (h - 1) + c + 1)
                nc.scalar.activation(probs[:, 512 * c:512 * c + 512], pS[:, 512 * c:512 * c + 512], ACT.Exp,
                                     bias=neg_max[:, h % 2:h % 2 + 1],
                                     accum_out=sums[:, h % XH, c:c + 1]).then_inc(exped, 1)

            def copy_o(b, h):
                act.wait_ge(weighed, 64 * b + 4 * h + 4)
                act.wait_ge(o_added, 16 * b + h + 1)
                nc.scalar.copy(o_copy[:, :], pO[:, 0:2 * P]).then_inc(o_copied, 1)

            def batch(b, last):
                for g in range(XG):
                    more = not (last and g == XG - 1)
                    for i in range(4):
                        h = 4 * g + i
                        for j in range(4):
                            m = 16 * g + 4 * i + j
                            k = m - FIRST_CTX
                            turn = not last and 0 <= k < ST // 2
                            if turn:
                                fill_hi_ctx(PRO + PER * b + ctx_no(2 * k), ctx_no(2 * k) % 2, 2 * k)
                            act.wait_ge(transposed, 64 * b + 4 * h + j + 1)
                            if h or j > 1:
                                act.wait_ge(weighed, 64 * b + 4 * h + j - 1)
                            nc.scalar.copy(probsT[:, j % 2, :, 0, :], turned_bank(not more, j)).then_inc(pt_hi, 1)
                            if j == 0 and h:
                                copy_o(b, h - 1)
                            if turn:
                                fill_hi_ctx(PRO + PER * b + ctx_no(2 * k + 1), ctx_no(2 * k + 1) % 2, 2 * k + 1)
                            if more or i < 3:
                                for c in ((), (), (0, 1), (2, 3))[j] if more else ((), (0, 1), (2,), (3,))[j]:
                                    exp(b, h + 1, c)
                            if more:
                                if g and i < 2 and j == 0:
                                    act.wait_ge(weighed, 64 * b + 16 * g)
                                if i >= 2 and j == 0:
                                    act.wait_ge(scored, 16 * b + 4 * g + 2 * (i - 2) + 2)
                                fill_hi_vk(PRO + PER * b + fill_no(m, last), fill_no(m) % 2, (g + 1) % XG, i, j)
                copy_o(b, XH - 1)

            act.sem_inc(o_copied, 1)
            act.wait_ge(bias_in, 16)
            for u in range(ST):
                fill_hi_ctx(u, u % 2, u)
            for m in range(16):
                fill_hi_vk(ST + m, m % 2, 0, m // 4, m % 4)
                if m == 14:
                    for c in range(NCH):
                        exp(0, 0, c)
            if batches > 1:
                with act.Fori(0, batches - 1) as b:
                    batch(b, False)
            batch(batches - 1, True)

        @block.vector
        def _(dve):
            def fill_lo_ctx(no, bk_, u):
                dve.wait_ge(fill_hi, no + 1)
                nc.vector.tensor_tensor(ctx_lo[:, :, P * u:P * u + P],
                                        pJ[:, bk_, :].rearrange("p (t s) -> p t s", t=DT),
                                        ctx_hi[:, :, P * u:P * u + P].bitcast(F32), ALU.subtract).then_inc(fill_lo, 1)

            def fill_lo_vk(no, bk_, g, i, j):
                dve.wait_ge(fill_hi, no + 1)
                if i < 2:
                    n = 2 * (4 * i + j)
                    nc.vector.tensor_tensor(values[:, g % 2, n:n + 2, :, DK:2 * DK],
                                            pJ[:, bk_, :].rearrange("p (s h k) -> p s h k", s=2, h=4),
                                            values[:, g % 2, n:n + 2, :, 0:DK].bitcast(F32),
                                            ALU.subtract).then_inc(fill_lo, 1)
                    return
                for a in range(2):
                    x = 2 * (i - 2) + a
                    last = nc.vector.scalar_tensor_tensor(
                        out=keys[DK:P, x, 512 * j:512 * j + 512], in0=pJ[DK * a:DK * a + DK, bk_, :],
                        scalar=bk_sb[:, 4 * g + x:4 * g + x + 1],
                        in1=keys[0:DK, x, 512 * j:512 * j + 512].bitcast(F32), op0=ALU.add, op1=ALU.subtract)
                last.then_inc(fill_lo, 1)

            def maxima(b, h):
                dve.wait_ge(scored, 16 * b + h + 1)
                nc.vector.tensor_reduce(neg_max[:, h % 2:h % 2 + 1], pS[:, :], AX.X, ALU.max,
                                        negate=True).then_inc(maxed, 1)

            def add_o(b, h):
                dve.wait_ge(o_copied, 16 * b + h + 2)
                dve.wait_ge(o_out[h % 2], 128 * b + 16 * (h // 2) + 16)
                nc.vector.tensor_tensor(o_half[:, h % 2, :], o_copy[:, 0:P], o_copy[:, P:2 * P],
                                        ALU.add).then_inc(o_added, 1)

            def row_sum(b, h):
                dve.wait_ge(exped, 64 * b + 4 * h + 4)
                nc.vector.tensor_reduce(total[:, h:h + 1], sums[:, h, :], AX.X, ALU.add).then_inc(totalled, 1)
                dve.wait_ge(totalled, 16 * b + h + 1)
                if h == 0:
                    dve.wait_ge(scale_out, 16 * b + 16)
                nc.vector.reciprocal(scale[:, h:h + 1], total[:, h:h + 1]).then_inc(scaled, 1)

            def batch(b, last):
                for g in range(XG):
                    more = not (last and g == XG - 1)
                    for i in range(4):
                        h = 4 * g + i
                        for j in range(4):
                            m = 16 * g + 4 * i + j
                            k = m - FIRST_CTX
                            turn = not last and 0 <= k < ST // 2
                            if turn:
                                fill_lo_ctx(PRO + PER * b + ctx_no(2 * k), ctx_no(2 * k) % 2, 2 * k)
                            dve.wait_ge(pt_hi, 64 * b + 4 * h + j + 1)
                            nc.vector.tensor_tensor(probsT[:, j % 2, :, 1, :], turned_bank(not more, j),
                                                    probsT[:, j % 2, :, 0, :].bitcast(F32),
                                                    ALU.subtract).then_inc(pt_lo, 1)
                            if turn:
                                fill_lo_ctx(PRO + PER * b + ctx_no(2 * k + 1), ctx_no(2 * k + 1) % 2, 2 * k + 1)
                            if j == 0 and h:
                                add_o(b, h - 1)
                            if j == 0:
                                row_sum(b, h)
                            if j == (1 if more else 0) and (more or i < 3):
                                maxima(b, h + 1)
                            if more:
                                fill_lo_vk(PRO + PER * b + fill_no(m, last), fill_no(m) % 2, (g + 1) % XG, i, j)
                add_o(b, XH - 1)

            dve.sem_inc(o_added, 1)
            dve.sem_inc(o_out[0], 16)
            dve.sem_inc(o_out[1], 16)
            dve.sem_inc(scale_out, 16)
            dve.wait_ge(bias_in, 16)
            for u in range(ST):
                fill_lo_ctx(u, u % 2, u)
            for m in range(16):
                if m == 14:
                    maxima(0, 0)
                fill_lo_vk(ST + m, m % 2, 0, m // 4, m % 4)
            if batches > 1:
                with dve.Fori(0, batches - 1) as b:
                    batch(b, False)
            batch(batches - 1, True)


def chain(eng, done):
    count = [0]

    def step(ins):
        count[0] += 1
        ins.then_inc(done, 1)
        eng.wait_ge(done, count[0])
    return step


def norm_steps(nc, dve, step, x, stats, mv, t):
    step(nc.vector.bn_stats(stats[:, t, :], x[:, t, :]))
    step(nc.vector.bn_aggr(mv[:, t, :], stats[:, t, :]))


def prepare(nc, x, wq, bq, wk, wv, ident, wk_split, wv_split, q_split, used):
    es = ExitStack()
    with es:
        sb = lambda n, s, d: es.enter_context(nc.sbuf_tensor(n, s, d))
        ps = lambda n, s, d: es.enter_context(nc.psum_tensor(n, s, d))
        sem = lambda n: new_semaphore(nc, n, used)
        WX = XH * DK
        xs = sb("p_x", [P, B, D], F32)
        xn = sb("p_xn", [P, 2, D], F32)
        xT = sb("p_xT", [P, 2, DT, TOK], F32R)
        raw = sb("p_raw", [P, 2, DT, WX], F32)
        wq_p = sb("p_wqp", [P, 2, DT, WX], F32R)
        w_p = sb("p_wp", [P, 2, 2, DT, WX], F32R)
        bq_sb = sb("p_bq", [P, XH // 2], F32)
        bq8 = sb("p_bq8", [P, XH // 2], F32)
        stats = sb("p_stats", [P, B, 6], F32)
        mv = sb("p_mv", [P, B, 2], F32)
        veps = sb("p_veps", [P, B], F32)
        std = sb("p_std", [P, B], F32)
        rstd = sb("p_rstd", [P, B], F32)
        q32 = sb("p_q32", [P, 2, 512], F32)
        qb = sb("p_qb", [P, 4, 4, 2, P], F32R)
        pt = ps("p_pt", [P, 2, 512], F32)
        pq = ps("p_pq", [P, 4, 512], F32)

        x_in = [sem("p_x_in0"), sem("p_x_in1")]
        wq_in, bq_in = sem("p_wq_in"), sem("p_bq_in")
        w_in = [sem("p_w_in0"), sem("p_w_in1")]
        w_out = sem("p_w_out")
        q_out = [sem(f"p_q_out{n}") for n in range(4)]
        made = sem("p_made")
        step_done = sem("p_step")
        var_ready, std_ready = sem("p_var"), sem("p_std_ready")
        normed = sem("p_normed")
        turned = sem("p_turned")
        x_hi, x_lo = sem("p_x_hi"), sem("p_x_lo")
        wq_hi, wq_lo = sem("p_wq_hi"), sem("p_wq_lo")
        bias_ready = sem("p_bias8")
        q_done = sem("p_qdone")
        q_copied = sem("p_qcopied")
        q_hi, q_parts = sem("p_qhi"), sem("p_qparts")
        w_hi, w_lo = sem("p_whi"), sem("p_wlo")
        block = es.enter_context(nc.Block())

        @block.sync
        def _(sp):
            for hf in range(2):
                sp.dma_start(xs[:, 4 * hf:4 * hf + 4, :], x[4 * hf:4 * hf + 4].rearrange("b p d -> p b d")).then_inc(x_in[hf], 16)
            with nc.allow_non_contiguous_dma(reason="the bias, once"):
                sp.dma_start(bq_sb[:, :], bq.rearrange("(a u) k -> (u k) a", u=2)).then_inc(bq_in, 16)
            sp.dma_start(raw[:, 0, :, :], wk.rearrange("(t p) h k -> p t (h k)", p=P)).then_inc(w_in[0], 16)
            sp.dma_start(raw[:, 1, :, :], wq.rearrange("(t p) h k -> p t (h k)", p=P)).then_inc(wq_in, 16)
            for part, ready in enumerate((w_hi, w_lo)):
                sp.wait_ge(ready, 2)
                sp.dma_start(wk_split[part], w_p[:, 0, part, :, :].bitcast(F32)).then_inc(w_out, 16)
            sp.dma_start(raw[:, 0, :, :], wv.rearrange("(t p) h k -> p t (h k)", p=P)).then_inc(w_in[1], 16)
            for n in range(16):
                half, pair = n // 8, n % 8
                sp.wait_ge(q_parts, n + 1)
                sp.dma_start(q_split[P * pair:P * pair + P, 4 * half:4 * half + 4, :, :],
                             qb[:, n % 4, :, :, :].bitcast(F32)).then_inc(q_out[n % 4], 16)
            sp.wait_ge(w_out, 64)
            for n in range(4):
                sp.wait_ge(q_out[n], 16 * 4)

        @block.gpsimd
        def _(pool):
            nc.gpsimd.memset(ident[:, :], 0.0).then_inc(made, 1)
            pool.wait_ge(made, 1)
            nc.gpsimd.affine_select(out=ident[:, :], in_=ident[:, :], compare_op=ALU.not_equal, fill=1.0,
                                    base=0, pattern=[[-1, P]], channel_multiplier=1).then_inc(made, 1)

        @block.vector
        def _(dve):
            step = chain(dve, step_done)

            def halves(t):
                return slice(4 * t, 4 * t + 4)

            def normalise(t):
                if t >= 2:
                    dve.wait_ge(turned, t - 1)
                nc.vector.tensor_scalar(xn[:, t % 2, :], xs[:, t, :], mv[:, t, 0:1], rstd[:, t:t + 1],
                                        ALU.subtract, ALU.mult).then_inc(normed, 1)

            def lo(t):
                dve.wait_ge(x_hi, t + 1)
                nc.vector.tensor_tensor(xT[:, 1, :, P * t:P * t + P], pt[:, t % 2, :].rearrange("p (c s) -> p c s", c=DT),
                                        xT[:, 0, :, P * t:P * t + P].bitcast(F32), ALU.subtract).then_inc(x_lo, 1)

            def weights_lo(c):
                dve.wait_ge(wq_hi, c + 1)
                cols = slice(512 * c, 512 * c + 512)
                nc.vector.tensor_tensor(wq_p[:, 1, :, cols], raw[:, 1, :, cols], wq_p[:, 0, :, cols].bitcast(F32),
                                        ALU.subtract).then_inc(wq_lo, 1)

            def other_lo(n):
                k, cols = n // 2, slice(512 * (n % 2), 512 * (n % 2) + 512)
                dve.wait_ge(w_hi, n + 1)
                nc.vector.tensor_tensor(w_p[:, k, 1, :, cols], raw[:, 0, :, cols],
                                        w_p[:, k, 0, :, cols].bitcast(F32), ALU.subtract).then_inc(w_lo, 1)
            for hf in range(2):
                dve.wait_ge(x_in[hf], 16)
                for t in range(4):
                    norm_steps(nc, dve, step, xs, stats, mv, 4 * hf + t)
                nc.vector.tensor_scalar_add(veps[:, halves(hf)], mv[:, halves(hf), 1], EPS).then_inc(var_ready, 1)
            for hf in range(2):
                dve.wait_ge(std_ready, hf + 1)
                step(nc.vector.reciprocal(rstd[:, halves(hf)], std[:, halves(hf)]))
            normalise(0)
            normalise(1)
            other_lo(0)
            other_lo(1)
            for t in range(B):
                lo(t)
                if t + 2 < B:
                    normalise(t + 2)
                if t == 2:
                    weights_lo(0)
                if t == 3:
                    dve.wait_ge(bq_in, 16)
                    nc.vector.tensor_scalar(bq8[:, :], bq_sb[:, :], DK ** -0.5, None, ALU.mult).then_inc(bias_ready, 1)
                    weights_lo(1)
            for n in range(16):
                if n in (4, 5):
                    other_lo(n - 2)
                dve.wait_ge(q_copied, n + 1)
                if n >= 4:
                    dve.wait_ge(q_out[n % 4], 16 * (n // 4))
                q4 = q32[:, n % 2, :].rearrange("p (b t) -> p b t", b=4)
                nc.vector.tensor_copy(qb[:, n % 4, :, 0, :], q4).then_inc(q_hi, 1)
                dve.wait_ge(q_hi, n + 1)
                nc.vector.tensor_tensor(qb[:, n % 4, :, 1, :], q4, qb[:, n % 4, :, 0, :].bitcast(F32),
                                        ALU.subtract).then_inc(q_parts, 1)

        @block.scalar
        def _(act):
            def hi(t):
                act.wait_ge(turned, t + 1)
                nc.scalar.copy(xT[:, 0, :, P * t:P * t + P], pt[:, t % 2, :].rearrange("p (c s) -> p c s", c=DT)).then_inc(x_hi, 1)

            def weights_hi(c):
                act.wait_ge(wq_in, 16)
                cols = slice(512 * c, 512 * c + 512)
                nc.scalar.copy(wq_p[:, 0, :, cols], raw[:, 1, :, cols]).then_inc(wq_hi, 1)

            def other_hi(n):
                k, cols = n // 2, slice(512 * (n % 2), 512 * (n % 2) + 512)
                act.wait_ge(w_in[k], 16)
                if k:
                    act.wait_ge(w_lo, 2)
                nc.scalar.copy(w_p[:, k, 0, :, cols], raw[:, 0, :, cols]).then_inc(w_hi, 1)
            for hf in range(2):
                act.wait_ge(var_ready, hf + 1)
                nc.scalar.activation(std[:, 4 * hf:4 * hf + 4], veps[:, 4 * hf:4 * hf + 4], ACT.Sqrt).then_inc(std_ready, 1)
            other_hi(0)
            other_hi(1)
            for t in range(4):
                hi(t)
                if t >= 2:
                    weights_hi(t - 2)
            hi(4)
            for n in range(16):
                if n < 3:
                    hi(5 + n)
                if n in (4, 5):
                    other_hi(n - 2)
                if n == 7:
                    act.wait_ge(w_lo, 4)
                    for part in range(2):
                        act.dma_start(wv_split[part], w_p[:, 1, part, :, :].bitcast(F32)).then_inc(w_out, 16)
                if n == 0:
                    act.wait_ge(bias_ready, 1)
                act.wait_ge(q_done, n + 1)
                if n >= 2:
                    act.wait_ge(q_parts, n - 1)
                nc.scalar.activation(q32[:, n % 2, :], pq[:, n % 4, :], ACT.Identity,
                                     bias=bq8[:, n % 8:n % 8 + 1], scale=DK ** -0.5).then_inc(q_copied, 1)

        @block.tensor
        def _(pe):
            def x_turn(t):
                pe.wait_ge(normed, t + 1)
                if t >= 2:
                    pe.wait_ge(x_lo, t - 1)
                for c in range(DT):
                    last = nc.tensor.transpose(pt[:, t % 2, P * c:P * c + P], xn[:, t % 2, P * c:P * c + P], ident[:, :])
                last.then_inc(turned, 1)
            pe.wait_ge(made, 2)
            for t in range(6):
                x_turn(t)
            for n in range(16):
                half, pair = n // 8, n % 8
                pe.wait_ge(wq_lo, pair // 4 + 1)
                pe.wait_ge(x_lo, 4 * half + 4)
                if n >= 4:
                    pe.wait_ge(q_copied, n - 3)
                for t in range(DT):
                    for k, (w, c) in enumerate(((0, 0), (0, 1), (1, 0))):
                        last = nc.tensor.matmul(pq[:, n % 4, :], wq_p[:, w, t, P * pair:P * pair + P],
                                                xT[:, c, t, 512 * half:512 * half + 512],
                                                start=t + k == 0, stop=t == DT - 1 and k == 2)
                last.then_inc(q_done, 1)
                if n < 2:
                    x_turn(6 + n)

SH = 8
NM = B * SH
ITERS = 20


def self_attention(nc, x, xo, x_bv, x_bo, o_parts, row_scale, wq, bq, wk, bk, wv, bv, wo, bo, ident, x1, mv_out, used):
    es = ExitStack()
    with es:
        sb = lambda n, s, d, e=es: e.enter_context(nc.sbuf_tensor(n, s, d))
        ps = lambda n, s, d, e=es: e.enter_context(nc.psum_tensor(n, s, d))
        sem = lambda n: new_semaphore(nc, n, used)
        BF16 = mybir.dt.bfloat16
        v_sb = sb("s_v", [P, B, D], F32)
        AT = sb("s_AT", [P, NM, P], F32)
        s_ = sb("s_rowsum", [P, NM], F32)
        ls = sb("s_ls", [P, NM], F32)
        NQ = NM // 4

        def four(n):
            return bass.ds(4 * n, 4)

        def over(t, n):
            return t[:, four(n)].unsqueeze(2).to_broadcast([P, 4, P])
        half = ExitStack()
        w_p = sb("s_wp", [P, 3, 2, DT, D], F32R, half)
        q_sb = sb("s_q", [P, DT, TOK], F32, half)
        k_sb = sb("s_k", [P, DT, TOK], F32, half)
        bqk = sb("s_bqk", [P, 2, DT], F32, half)
        bq8 = sb("s_bq8", [P, DT], F32, half)
        bvb = sb("s_bv", [P, D], F32, half)
        mv = sb("s_mv", [P, B, 2], F32, half)
        rstd = sb("s_rstd", [P, B], F32, half)
        with half:
            with ExitStack() as s1:
                xo_sb = sb("a_xo", [P, XH // 2, D], F32, s1)
                ua = sb("a_ua", [P, 2, 2, XH // 2, P], F32, s1)
                us = sb("a_us", [P, XH // 2, P], F32, s1)
                oT = sb("a_oT", [P, 2, XH // 2, P], F32, s1)
                rs = sb("a_rs", [P, B, XH], F32, s1)
                rsx = sb("a_rsx", [P, XH // 2, P], F32, s1)
                xbo = sb("a_xbo", [P, D], F32, s1)
                xbv = sb("a_xbv", [P, XH // 2], F32, s1)
                w_raw = sb("a_w", [P, DT, D], F32, s1)
                stats = sb("a_stats", [P, B, 6], F32, s1)
                veps = sb("a_veps", [P, B], F32, s1)
                std = sb("a_std", [P, B], F32, s1)
                pR = ps("a_pR", [P, 2, 2, 4, P], F32, s1)
                pY = ps("a_pY", [P, 2, D], F32, s1)
                pB = ps("a_pB", [P, D], F32, s1)
                xs_in, xo_in, rs_in, c_in = (sem(n) for n in ("a_xs_in", "a_xo_in", "a_rs_in", "a_c_in"))
                w_in, w_hi, w_lo = sem("a_w_in"), sem("a_w_hi"), sem("a_w_lo")
                u_in = [sem("a_u_in0"), sem("a_u_in1")]
                widened, spread, added, merged = sem("a_widened"), sem("a_spread"), sem("a_added"), sem("a_merged")
                bias_made, bias_ready = sem("a_bias_made"), sem("a_bias_ready")
                projected, xb_done = sem("a_projected"), sem("a_xb")
                step_done, var_ready, std_ready = sem("a_step"), sem("a_var"), sem("a_std")
                x1_done = sem("a_x1")
                block = s1.enter_context(nc.Block())

                @block.sync
                def _(sp):
                    def u_load(b):
                        for n in range(2):
                            for u in range(2):
                                sp.dma_start(ua[DK * u:DK * u + DK, b % 2, n, :, :],
                                             o_parts[b].rearrange("(a u) k t -> u k a t", u=2)[u, DK * n:DK * n + DK, :, :]
                                             ).then_inc(u_in[b % 2], 16)
                    sp.dma_start(rs[:, :, :], row_scale.rearrange("b t h -> t b h")).then_inc(rs_in, 16)
                    u_load(0)
                    sp.dma_start(xo_sb[:, :, :], xo.rearrange("(a u) k d -> (u k) a d", u=2)).then_inc(xo_in, 16)
                    with nc.allow_non_contiguous_dma(reason="biases, once"):
                        sp.dma_start(xbv[:, :], x_bv.rearrange("(a u) k -> (u k) a", u=2)).then_inc(xo_in, 16)
                        sp.dma_start(bqk[:, 0, :], bq.rearrange("(t p) -> p t", p=P)).then_inc(c_in, 16)
                        sp.dma_start(bqk[:, 1, :], bk.rearrange("(t p) -> p t", p=P)).then_inc(c_in, 16)
                    for out, src in ((xbo, x_bo), (bvb, bv)):
                        sp.dma_start(out[:, :], src.rearrange("(a d) -> a d", a=1).to_broadcast([P, D])).then_inc(c_in, 16)
                    u_load(1)
                    sp.dma_start(x1[:, :, :], x.rearrange("b p d -> p b d")).then_inc(xs_in, 16)
                    for b in range(2, B):
                        sp.wait_ge(added, b - 1)
                        u_load(b)
                        if b % 2 == 0:
                            n = b // 2 - 1
                            if n:
                                sp.wait_ge(w_lo, n)
                            sp.dma_start(w_raw[:, :, :], (wq, wk, wv)[n].rearrange("(t p) d -> p t d", p=P)).then_inc(w_in, 16)
                    sp.wait_ge(w_in, 48)

                @block.tensor
                def _(pe):
                    def spread_scales(b):
                        pe.wait_ge(widened, b + 1)
                        if b >= 2:
                            pe.wait_ge(merged, b - 1)
                        for a in range(XH // 2):
                            last = nc.tensor.transpose(pR[:, b % 2, a // 4, a % 4, :], rsx[:, a, :], ident[:, :])
                        last.then_inc(spread, 1)
                    spread_scales(0)
                    pe.wait_ge(xo_in, 32)
                    for a in range(XH // 2):
                        last = nc.tensor.matmul(pB[:, :], xbv[:, a:a + 1].to_broadcast([P, P]), xo_sb[:, a, :],
                                                start=a == 0, stop=a == XH // 2 - 1)
                    last.then_inc(bias_made, 1)
                    for b in range(B):
                        if b + 1 < B:
                            spread_scales(b + 1)
                        pe.wait_ge(merged, b + 1)
                        if b >= 2:
                            pe.wait_ge(x1_done, b - 1)
                        for a in range(XH // 2):
                            last = nc.tensor.matmul(pY[:, b % 2, :], oT[:, b % 2, a, :], xo_sb[:, a, :],
                                                    start=a == 0, stop=a == XH // 2 - 1)
                        last.then_inc(projected, 1)

                @block.gpsimd
                def _(pool):
                    for b in range(B):
                        pool.wait_ge(u_in[b % 2], 64 * (b // 2 + 1))
                        if b:
                            pool.wait_ge(merged, b)
                        nc.gpsimd.tensor_tensor(us[:, :, :], ua[:, b % 2, 0, :, :], ua[:, b % 2, 1, :, :],
                                                ALU.add).then_inc(added, 1)
                        if b == 0:
                            pool.wait_ge(bias_ready, 1)
                            pool.wait_ge(xs_in, 16)
                        nc.gpsimd.tensor_tensor(x1[:, b, :], x1[:, b, :], xbo[:, :], ALU.add).then_inc(xb_done, 1)
                        if b in (3, 5, 7):
                            n = b // 2 - 1
                            pool.wait_ge(w_hi, n + 1)
                            nc.gpsimd.tensor_tensor(w_p[:, n, 1, :, :], w_raw[:, :, :], w_p[:, n, 0, :, :].bitcast(F32),
                                                    ALU.subtract).then_inc(w_lo, 1)

                @block.vector
                def _(dve):
                    step = chain(dve, step_done)

                    def residual(b):
                        dve.wait_ge(projected, b + 1)
                        dve.wait_ge(xb_done, b + 1)
                        nc.vector.tensor_tensor(x1[:, b, :], pY[:, b % 2, :], x1[:, b, :], ALU.add).then_inc(x1_done, 1)
                        dve.wait_ge(x1_done, b + 1)
                        norm_steps(nc, dve, step, x1, stats, mv, b)
                    for b in range(B):
                        dve.wait_ge(added, b + 1)
                        dve.wait_ge(spread, b + 1)
                        if b >= 2:
                            dve.wait_ge(projected, b - 1)
                        nc.vector.tensor_tensor(oT[:, b % 2, :, :], us[:, :, :],
                                                pR[:, b % 2, :, :, :].rearrange("p a b t -> p (a b) t"), ALU.mult).then_inc(merged, 1)
                        if b == 0:
                            dve.wait_ge(c_in, 64)
                            dve.wait_ge(bias_made, 1)
                            nc.vector.tensor_tensor(xbo[:, :], pB[:, :], xbo[:, :], ALU.add).then_inc(bias_ready, 1)
                        else:
                            residual(b - 1)
                    residual(B - 1)
                    nc.vector.tensor_scalar_add(veps[:, :], mv[:, :, 1], EPS).then_inc(var_ready, 1)
                    step(nc.vector.tensor_scalar(bq8[:, :], bqk[:, 0, :], DK ** -0.5, None, ALU.mult))
                    dve.wait_ge(std_ready, 1)
                    step(nc.vector.reciprocal(rstd[:, :], std[:, :]))

                @block.scalar
                def _(act):
                    act.wait_ge(rs_in, 16)
                    for b in range(B):
                        if b:
                            act.wait_ge(spread, b)
                        nc.scalar.copy(rsx[:, :, :].rearrange("p a (u k) -> p (a u) k", u=2),
                                       rs[:, b, :].unsqueeze(2).to_broadcast([P, XH, DK])).then_inc(widened, 1)
                        if b in (3, 5, 7):
                            n = b // 2 - 1
                            act.wait_ge(w_in, 16 * n + 16)
                            nc.scalar.copy(w_p[:, n, 0, :, :], w_raw[:, :, :]).then_inc(w_hi, 1)
                    act.wait_ge(var_ready, 1)
                    nc.scalar.activation(std[:, :], veps[:, :], ACT.Sqrt).then_inc(std_ready, 1)

            with ExitStack() as s2:
                lm = AT
                xn = sb("b_xn", [P, 2, D], F32, s2)
                xT = sb("b_xT", [P, 2, DT, TOK], F32R, s2)
                ex = sb("b_ex", [P, 2, 4, P], F32, s2)
                nm = sb("b_nm", [P, NM], F32, s2)
                pt = ps("b_pt", [P, 2, DT, P], F32, s2)
                pw = ps("b_pw", [P, 2, 512], F32, s2)
                pL = ps("b_pL", [P, 2, 4, P], F32, s2)
                normed, x_turned, x_hi, x_lo = (sem(n) for n in ("b_normed_x", "b_x_turned", "b_x_hi", "b_x_lo"))
                made, qk_out, v_out = sem("b_made"), sem("b_qk_out"), sem("b_v_out")
                logits, shifted, exped, summed = (sem(n) for n in ("b_logits", "b_shifted", "b_exped", "b_summed"))
                logged = sem("b_logged")
                step_done = sem("b_step")
                block = s2.enter_context(nc.Block())

                @block.tensor
                def _(pe):
                    def x_turn(t):
                        pe.wait_ge(normed, t + 1)
                        if t >= 2:
                            pe.wait_ge(x_lo, t - 1)
                        for c in range(DT):
                            last = nc.tensor.transpose(pt[:, t % 2, c, :], xn[:, t % 2, P * c:P * c + P], ident[:, :])
                        last.then_inc(x_turned, 1)

                    def queries_keys(n):
                        hf, s, a = n // 8, n // 4 % 2, n % 4
                        pe.wait_ge(x_lo, 4 * hf + 4)
                        if n >= 2:
                            pe.wait_ge(qk_out, n - 1)
                        for t in range(DT):
                            for k, (w, c) in enumerate(((0, 0), (0, 1), (1, 0))):
                                last = nc.tensor.matmul(pw[:, n % 2, :], w_p[:, s, w, t, P * a:P * a + P],
                                                        xT[:, c, t, 512 * hf:512 * hf + 512],
                                                        start=t + k == 0, stop=t == DT - 1 and k == 2)
                        last.then_inc(made, 1)

                    def values(b):
                        if b >= 2:
                            pe.wait_ge(v_out, b - 1)
                        else:
                            pe.wait_ge(qk_out, 15 + b)
                        for t in range(DT):
                            for k, (c, w) in enumerate(((0, 0), (1, 0), (0, 1))):
                                last = nc.tensor.matmul(pw[:, b % 2, :], xT[:, c, t, P * b:P * b + P], w_p[:, 2, w, t, :],
                                                        start=t + k == 0, stop=t == DT - 1 and k == 2)
                        last.then_inc(made, 1)

                    def score(n):
                        b = n // 2
                        pe.wait_ge(qk_out, 8 * (b // 4) + 8)
                        if n >= 2:
                            pe.wait_ge(shifted, n - 1)
                        for k in range(4):
                            h = 2 * k + n % 2
                            r = slice(DK * (h % 2), DK * (h % 2) + DK)
                            last = nc.tensor.matmul(pL[:, n % 2, k, :], q_sb[r, h // 2, P * b:P * b + P],
                                                    k_sb[r, h // 2, P * b:P * b + P], start=True, stop=True)
                        last.then_inc(logits, 1)

                    for t in range(4):
                        x_turn(t)
                    for n in range(8):
                        queries_keys(n)
                        if n < 4:
                            x_turn(4 + n)
                    for n in range(8):
                        queries_keys(8 + n)
                        score(n)
                    for n in range(8):
                        values(n)
                        score(8 + n)
                @block.scalar
                def _(act):
                    def hi(t):
                        act.wait_ge(x_turned, t + 1)
                        nc.scalar.copy(xT[:, 0, :, P * t:P * t + P], pt[:, t % 2, :, :]).then_inc(x_hi, 1)

                    def queries_keys(n):
                        hf, s, a = n // 8, n // 4 % 2, n % 4
                        act.wait_ge(made, n + 1)
                        nc.scalar.activation((q_sb, k_sb)[s][:, a, 512 * hf:512 * hf + 512], pw[:, n % 2, :], ACT.Identity,
                                             bias=bq8[:, a:a + 1] if s == 0 else bqk[:, 1, a:a + 1],
                                             scale=DK ** -0.5 if s == 0 else 1.0).then_inc(qk_out, 1)

                    def exp(n):
                        act.wait_ge(shifted, n + 1)
                        if n >= 2:
                            act.wait_ge(summed, n - 1)
                        nc.scalar.activation(ex[:, n % 2, :, :], lm[:, four(n), :], ACT.Exp).then_inc(exped, 1)
                    for t in range(4):
                        hi(t)
                    for n in range(8):
                        queries_keys(n)
                        if n < 4:
                            hi(4 + n)
                    for n in range(8):
                        queries_keys(8 + n)
                        if n:
                            exp(n - 1)
                    for n in range(7, NQ):
                        exp(n)
                    act.wait_ge(summed, NQ)
                    nc.scalar.activation(ls[:, :], s_[:, :], ACT.Ln).then_inc(logged, 1)

                @block.vector
                def _(dve):
                    step = chain(dve, step_done)

                    def first(n):
                        dve.wait_ge(logits, n + 1)
                        step(nc.vector.tensor_reduce(nm[:, four(n)], pL[:, n % 2, :, :], AX.X, ALU.max, negate=True))
                        nc.vector.tensor_tensor(lm[:, four(n), :], pL[:, n % 2, :, :], over(nm, n), ALU.add).then_inc(shifted, 1)

                    def sums(n):
                        dve.wait_ge(exped, n + 1)
                        nc.vector.tensor_reduce(s_[:, four(n)], ex[:, n % 2, :, :], AX.X, ALU.add).then_inc(summed, 1)

                    def normalise(t):
                        if t >= 2:
                            dve.wait_ge(x_turned, t - 1)
                        nc.vector.tensor_scalar(xn[:, t % 2, :], x1[:, t, :], mv[:, t, 0:1], rstd[:, t:t + 1],
                                                ALU.subtract, ALU.mult).then_inc(normed, 1)

                    def lo(t):
                        dve.wait_ge(x_hi, t + 1)
                        nc.vector.tensor_tensor(xT[:, 1, :, P * t:P * t + P], pt[:, t % 2, :, :],
                                                xT[:, 0, :, P * t:P * t + P].bitcast(F32), ALU.subtract).then_inc(x_lo, 1)

                    def values(b):
                        dve.wait_ge(made, 16 + b + 1)
                        nc.vector.tensor_tensor(v_sb[:, b, :], pw[:, b % 2, :], bvb[:, :], ALU.add).then_inc(v_out, 1)
                    normalise(0)
                    normalise(1)
                    for t in range(B):
                        if t + 2 < B:
                            normalise(t + 2)
                        lo(t)
                    for n in range(NQ):
                        if n >= 8:
                            values(n - 8)
                        first(n)
                        if n:
                            sums(n - 1)
                    sums(NQ - 1)

        bo_sb = sb("s_bo", [P, D], F32)
        wo_sb = sb("s_wo", [P, DT, D], F32)
        wo_p = sb("s_wop", [P, 2, DT, D], F32R)
        wo_in, wo_hi, wo_lo = sem("s_wo_in"), sem("s_wo_hi"), sem("s_wo_lo")
        r32 = sb("s_r32", [P, NM], F32)
        c32 = sb("s_c32", [P, NM], F32)
        with ExitStack() as s3:
            at_p = sb("c_atp", [P, 3, NM, P], BF16, s3)
            a_p = sb("c_ap", [P, 3, NM, P], BF16, s3)
            r_p = sb("c_rp", [P, NM, 3], BF16, s3)
            c_p = sb("c_cp", [P, NM, 3], BF16, s3)
            tot = sb("c_tot", [P, NM], F32, s3)
            left = sb("c_left", [P, NM], F32, s3)
            with ExitStack() as s4:
                la = sb("c_la", [P, 2, 4, P], F32, s4)
                rest_t = sb("c_rest_t", [P, 2, 4, P], F32, s4)
                rest_a = sb("c_rest_a", [P, 2, 4, P], F32, s4)
                nm2 = sb("c_nm2", [P, NM], F32, s4)
                pLT = ps("c_pLT", [P, 2, 4, P], F32, s4)
                pA = ps("c_pA", [P, 2, 4, P], F32, s4)
                normed, turned, maxed, exped = (sem(n) for n in ("c_normed", "c_turned", "c_maxed", "c_exped"))
                t_part1, t_rest, t_part2, t_part3 = (sem(n) for n in ("c_t_part1", "c_t_rest", "c_t_part2", "c_t_part3"))
                a_turned, a_part1, a_rest, a_part2, a_part3 = (sem(n) for n in (
                    "c_a_turned", "c_a_part1", "c_a_rest", "c_a_part2", "c_a_part3"))
                block = s4.enter_context(nc.Block())

                def each_step(eng, *works, looped=True):
                    def step(n):
                        for work, lag in works:
                            if 0 <= n - lag < NQ:
                                work(n - lag, (n - lag) % 2, n - lag >= 2)
                    if not looped:
                        for n in range(NQ + 4):
                            step(n)
                        return
                    for n in range(4):
                        step(n)
                    with eng.Fori(0, (NQ - 4) // 2) as it:
                        for p in range(2):
                            for work, lag in works:
                                work(2 * it + (4 + p - lag), (4 + p - lag) % 2, True)
                    for n in range(NQ, NQ + 4):
                        step(n)

                @block.sync
                def _(sp):
                    sp.dma_start(wo_sb[:, :, :], wo.rearrange("(t p) d -> p t d", p=P)).then_inc(wo_in, 16)
                    sp.dma_start(bo_sb[:, :], bo.rearrange("(a d) -> a d", a=1).to_broadcast([P, D])).then_inc(wo_in, 16)

                @block.gpsimd
                def _(pool):
                    def rows(n, buf, reused):
                        if reused:
                            pool.wait_ge(turned, n - 1)
                        nc.gpsimd.tensor_tensor(la[:, buf, :, :], AT[:, four(n), :], over(ls, n), ALU.subtract).then_inc(normed, 1)

                    def t_third(n, buf, reused):
                        pool.wait_ge(t_part2, n + 1)
                        nc.gpsimd.tensor_tensor(at_p[:, 2, four(n), :], rest_t[:, buf, :, :], at_p[:, 1, four(n), :],
                                                ALU.subtract).then_inc(t_part3, 1)
                    each_step(pool, (rows, 0), (t_third, 3))

                @block.tensor
                def _(pe):
                    def turn(n, buf, reused):
                        pe.wait_ge(normed, n + 1)
                        if reused:
                            pe.wait_ge(exped, n - 1)
                        for k in range(4):
                            last = nc.tensor.transpose(pLT[:, buf, k, :], la[:, buf, k, :], ident[:, :])
                        last.then_inc(turned, 1)

                    def turn_back(n, buf, reused):
                        pe.wait_ge(exped, n + 1)
                        if reused:
                            pe.wait_ge(a_rest, n - 1)
                        for k in range(4):
                            last = nc.tensor.transpose(pA[:, buf, k, :], AT[:, 4 * n + k, :], ident[:, :])
                        last.then_inc(a_turned, 1)
                    each_step(pe, (turn, 0), (turn_back, 1), looped=False)

                @block.scalar
                def _(act):
                    def exp(n, buf, reused):
                        act.wait_ge(maxed, n + 1)
                        for k in range(4):
                            m = bass.ds(4 * n + k, 1)
                            last = nc.scalar.activation(AT[:, m, :], pLT[:, buf, k:k + 1, :], ACT.Exp,
                                                        bias=nm2[:, m], accum_out=tot[:, m])
                        last.then_inc(exped, 1)

                    def t_first(n, buf, reused):
                        act.wait_ge(exped, n + 1)
                        nc.scalar.copy(at_p[:, 0, four(n), :], AT[:, four(n), :]).then_inc(t_part1, 1)

                    def a_second(n, buf, reused):
                        act.wait_ge(a_rest, n + 1)
                        nc.scalar.copy(a_p[:, 1, four(n), :], rest_a[:, buf, :, :]).then_inc(a_part2, 1)

                    def a_first(n, buf, reused):
                        act.wait_ge(a_turned, n + 1)
                        nc.scalar.copy(a_p[:, 0, four(n), :], pA[:, buf, :, :]).then_inc(a_part1, 1)
                    each_step(act, (exp, 0), (a_second, 3), (a_first, 1), (t_first, 0))

                @block.vector
                def _(dve):
                    def maxima(n, buf, reused):
                        dve.wait_ge(turned, n + 1)
                        nc.vector.tensor_reduce(nm2[:, four(n)], pLT[:, buf, :, :], AX.X, ALU.max, negate=True).then_inc(maxed, 1)

                    def t_second(n, buf, reused):
                        dve.wait_ge(t_part1, n + 1)
                        if reused:
                            dve.wait_ge(t_part3, n - 1)
                        nc.vector.tensor_tensor(rest_t[:, buf, :, :], AT[:, four(n), :], at_p[:, 0, four(n), :],
                                                ALU.subtract).then_inc(t_rest, 1)
                        dve.wait_ge(t_rest, n + 1)
                        nc.vector.tensor_copy(at_p[:, 1, four(n), :], rest_t[:, buf, :, :]).then_inc(t_part2, 1)

                    def a_remainder(n, buf, reused):
                        dve.wait_ge(a_part1, n + 1)
                        if reused:
                            dve.wait_ge(a_part3, n - 1)
                        nc.vector.tensor_tensor(rest_a[:, buf, :, :], pA[:, buf, :, :], a_p[:, 0, four(n), :],
                                                ALU.subtract).then_inc(a_rest, 1)

                    def a_third(n, buf, reused):
                        dve.wait_ge(a_part2, n + 1)
                        nc.vector.tensor_tensor(a_p[:, 2, four(n), :], rest_a[:, buf, :, :], a_p[:, 1, four(n), :],
                                                ALU.subtract).then_inc(a_part3, 1)
                    each_step(dve, (maxima, 0), (a_third, 4), (a_remainder, 2), (t_second, 2))
            with ExitStack() as s5:
                NG, GM = 4, NM // 4
                pV = ps("c_pV", [P, 4, 512], F32, s5)
                r_sums, r_ready = sem("c_r_sums"), sem("c_r_ready")
                c_sums, c_ready = sem("c_c_sums"), sem("c_c_ready")
                step_done, first_done = sem("c_step"), sem("c_first")
                STEPS = 5 * 2 * NG
                block = s5.enter_context(nc.Block())

                @block.tensor
                def _(pe):
                    def products(g, mats, vec, done):
                        for k in range(GM):
                            m = GM * g + k
                            for n in range(3):
                                last = nc.tensor.matmul(pV[:, g, 4 * k:4 * k + 3], mats[:, n, m, :], vec[:, m, :],
                                                        start=n == 0, stop=n == 2)
                        last.then_inc(done, 1)
                    with pe.Fori(0, ITERS - 1) as it:
                        for g in range(NG):
                            pe.wait_ge(c_ready, NG * it + g + 1)
                            products(g, at_p, c_p, r_sums)
                        for g in range(NG):
                            pe.wait_ge(r_ready, NG * it + g + 1)
                            products(g, a_p, r_p, c_sums)

                @block.scalar
                def _(act):
                    act.wait_ge(wo_in, 32)
                    nc.scalar.copy(wo_p[:, 0, :, :], wo_sb[:, :, :]).then_inc(wo_hi, 1)

                @block.gpsimd
                def _(pool):
                    pool.wait_ge(wo_hi, 1)
                    nc.gpsimd.tensor_tensor(wo_p[:, 1, :, :], wo_sb[:, :, :], wo_p[:, 0, :, :].bitcast(F32),
                                            ALU.subtract).then_inc(wo_lo, 1)

                @block.vector
                def _(dve):
                    def invert(it, no, g, sums, v32, v_p, ready):
                        s = slice(GM * g, GM * g + GM)
                        base = STEPS * it + 5 * no
                        dve.wait_ge(sums, NG * it + g + 1)
                        nc.vector.tensor_reduce(tot[:, s], pV[:, g, 0:4 * GM].rearrange("p (m n) -> p m n", n=4)[:, :, 0:3],
                                                AX.X, ALU.add).then_inc(step_done, 1)
                        dve.wait_ge(step_done, base + 1)
                        nc.vector.reciprocal(v32[:, s], tot[:, s]).then_inc(step_done, 1)
                        dve.wait_ge(step_done, base + 2)
                        nc.vector.tensor_copy(v_p[:, s, 0], v32[:, s]).then_inc(step_done, 1)
                        dve.wait_ge(step_done, base + 3)
                        nc.vector.tensor_tensor(left[:, s], v32[:, s], v_p[:, s, 0], ALU.subtract).then_inc(step_done, 1)
                        dve.wait_ge(step_done, base + 4)
                        nc.vector.tensor_copy(v_p[:, s, 1], left[:, s]).then_inc(step_done, 1)
                        dve.wait_ge(step_done, base + 5)
                        nc.vector.tensor_tensor(v_p[:, s, 2], left[:, s], v_p[:, s, 1], ALU.subtract).then_inc(ready, 1)
                    step = chain(dve, first_done)
                    step(nc.vector.reciprocal(c32[:, :], tot[:, :]))
                    step(nc.vector.tensor_copy(c_p[:, :, 0], c32[:, :]))
                    step(nc.vector.tensor_tensor(left[:, :], c32[:, :], c_p[:, :, 0], ALU.subtract))
                    step(nc.vector.tensor_copy(c_p[:, :, 1], left[:, :]))
                    nc.vector.tensor_tensor(c_p[:, :, 2], left[:, :], c_p[:, :, 1], ALU.subtract).then_inc(c_ready, NG)
                    with dve.Fori(0, ITERS - 1) as it:
                        for g in range(NG):
                            invert(it, g, g, r_sums, r32, r_p, r_ready)
                        for g in range(NG):
                            invert(it, NG + g, g, c_sums, c32, c_p, c_ready)

        with ExitStack() as s6:
            cv = sb("d_cv", [P, 2, D], F32, s6)
            stats = sb("d_stats", [P, B, 6], F32, s6)
            step_done = sem("d_step")
            o = sb("d_o", [P, 2, D], F32, s6)
            oT = sb("d_oT", [P, 2, 2, DT, P], F32R, s6)
            pO = ps("d_pO", [P, 2, D], F32, s6)
            pt = ps("d_pt", [P, 2, DT, P], F32, s6)
            pY = ps("d_pY", [P, 2, D], F32, s6)
            weighted, summed, scaled, turned = (sem(n) for n in ("d_weighted", "d_summed", "d_scaled", "d_turned"))
            o_hi, o_lo = sem("d_o_hi"), sem("d_o_lo")
            projected, added, biased = (sem(n) for n in ("d_proj", "d_added", "d_biased"))
            block = s6.enter_context(nc.Block())

            def by_parity(rows):
                return rows.rearrange("p (a u k) -> p u a k", a=SH // 2, u=2)

            def spread(scales, b):
                return scales[:, SH * b:SH * b + SH].rearrange("p (u a) -> p u a", u=2).unsqueeze(3).to_broadcast(
                    [P, 2, SH // 2, DK])

            @block.gpsimd
            def _(pool):
                pool.wait_ge(wo_in, 32)
                for b in range(B):
                    nc.gpsimd.tensor_tensor(x1[:, b, :], x1[:, b, :], bo_sb[:, :], ALU.add).then_inc(biased, 1)

            @block.vector
            def _(dve):
                def weight(b):
                    if b >= 2:
                        dve.wait_ge(summed, b - 1)
                    nc.vector.tensor_tensor(by_parity(cv[:, b % 2, :]), by_parity(v_sb[:, b, :]), spread(c32, b),
                                            ALU.mult).then_inc(weighted, 1)

                def add(b):
                    dve.wait_ge(projected, b + 1)
                    dve.wait_ge(biased, b + 1)
                    nc.vector.tensor_tensor(x1[:, b, :], pY[:, b % 2, :], x1[:, b, :], ALU.add).then_inc(added, 1)
                    dve.wait_ge(added, b + 1)
                    norm_steps(nc, dve, step, x1, stats, mv_out, b)
                step = chain(dve, step_done)
                weight(0)
                for b in range(B):
                    if b + 1 < B:
                        weight(b + 1)
                    dve.wait_ge(summed, b + 1)
                    if b >= 2:
                        dve.wait_ge(turned, b - 1)
                    nc.vector.tensor_tensor(by_parity(o[:, b % 2, :]), by_parity(pO[:, b % 2, :]), spread(r32, b),
                                            ALU.mult).then_inc(scaled, 1)
                    if b >= 2:
                        add(b - 2)
                    dve.wait_ge(o_hi, b + 1)
                    nc.vector.tensor_tensor(oT[:, b % 2, 1, :, :], pt[:, b % 2, :, :], oT[:, b % 2, 0, :, :].bitcast(F32),
                                            ALU.subtract).then_inc(o_lo, 1)
                add(B - 2)
                add(B - 1)

            @block.tensor
            def _(pe):
                def attend(b):
                    pe.wait_ge(weighted, b + 1)
                    if b >= 2:
                        pe.wait_ge(scaled, b - 1)
                    for h in range(SH):
                        last = nc.tensor.matmul(pO[:, b % 2, DK * h:DK * h + DK], AT[:, SH * b + 4 * (h % 2) + h // 2, :],
                                                cv[:, b % 2, DK * h:DK * h + DK], start=True, stop=True)
                    last.then_inc(summed, 1)

                def project(b):
                    pe.wait_ge(o_lo, b + 1)
                    if b >= 2:
                        pe.wait_ge(added, b - 1)
                    for c in range(DT):
                        for k, (m, w) in enumerate(((0, 0), (0, 1), (1, 0))):
                            last = nc.tensor.matmul(pY[:, b % 2, :], oT[:, b % 2, m, c, :], wo_p[:, w, c, :],
                                                    start=c + k == 0, stop=c == DT - 1 and k == 2)
                    last.then_inc(projected, 1)
                attend(0)
                pe.wait_ge(wo_lo, 1)
                for b in range(B):
                    if b + 1 < B:
                        attend(b + 1)
                    pe.wait_ge(scaled, b + 1)
                    if b >= 2:
                        pe.wait_ge(o_lo, b - 1)
                    for c in range(DT):
                        last = nc.tensor.transpose(pt[:, b % 2, c, :], o[:, b % 2, P * c:P * c + P], ident[:, :])
                    last.then_inc(turned, 1)
                    if b:
                        project(b - 1)
                project(B - 1)

            @block.scalar
            def _(act):
                for b in range(B):
                    act.wait_ge(turned, b + 1)
                    if b >= 2:
                        act.wait_ge(projected, b - 1)
                    nc.scalar.copy(oT[:, b % 2, 0, :, :], pt[:, b % 2, :, :]).then_inc(o_hi, 1)

E = 8
F = 2048
CAP = 161
CAPP = 162
OVER = CAP - P
FC = 4


def experts(nc, x2, mv, wg, w1, b1, w2, b2, ident, buf, ybuf, out, used):
    es = ExitStack()
    with es:
        sb = lambda n, s, d, e=es: e.enter_context(nc.sbuf_tensor(n, s, d))
        ps = lambda n, s, d, e=es: e.enter_context(nc.psum_tensor(n, s, d))
        sem = lambda n: new_semaphore(nc, n, used)
        raw1 = sb("e_raw1", [P, 2, DT, 512], F32)
        raw2 = sb("e_raw2", [P, 2, 4, D], F32)
        w_in = [[sem(f"e_w{a}_in{n}") for n in range(2)] for a in (1, 2)]
        backs = [sem(f"h_back{t}") for t in range(B)]
        w1p = sb("e_w1", [P, 2, 2, DT, 512], F32R)
        w2p = sb("e_w2", [P, FC, 2, 4, D], F32R)
        w_hi = [sem("e_w1_hi"), sem("e_w2_hi")]
        w_lo = [sem("e_w1_lo"), sem("e_w2_lo")]
        b1T = sb("e_b1T", [P, E * F // P], F32)
        b2T = sb("e_b2T", [P, E * DT], F32)
        slot = sb("e_slot", [P, B], U32)
        yslot = sb("e_yslot", [P, B], U32)
        weight = sb("e_weight", [P, B], F32)

        def w1_load(eng, e, c):
            eng.dma_start(raw1[:, c % 2, :, :], w1[e].rearrange("(t p) f -> p t f", p=P)[:, :, 512 * c:512 * c + 512]
                          ).then_inc(w_in[0][c % 2], 16)

        def w2_load(eng, e, c):
            eng.dma_start(raw2[:, c % 2, :, :], w2[e].rearrange("(c t p) d -> p c t d", p=P, c=FC)[:, c, :, :]
                          ).then_inc(w_in[1][c % 2], 16)

        NF = F // P
        PAIRS = NF // 2

        def split1_hi(act, e, n):
            c, cols = n // 2, slice(2 * P * (n % 2), 2 * P * (n % 2) + 2 * P)
            act.wait_ge(w_in[0][c % 2], 16 * (2 * e + c // 2 + 1))
            nc.scalar.copy(w1p[:, c % 2, 0, :, cols], raw1[:, c % 2, :, cols]).then_inc(w_hi[0], 1)

        def split2_hi(act, e, c):
            act.wait_ge(w_in[1][c % 2], 16 * (2 * e + c // 2 + 1))
            nc.scalar.copy(w2p[:, c, 0, :, :], raw2[:, c % 2, :, :]).then_inc(w_hi[1], 1)

        def split1_lo(dve, e, n):
            c, cols = n // 2, slice(2 * P * (n % 2), 2 * P * (n % 2) + 2 * P)
            dve.wait_ge(w_hi[0], PAIRS * e + n + 1)
            nc.vector.tensor_tensor(w1p[:, c % 2, 1, :, cols], raw1[:, c % 2, :, cols], w1p[:, c % 2, 0, :, cols].bitcast(F32),
                                    ALU.subtract).then_inc(w_lo[0], 1)

        def split2_lo(dve, e, c):
            dve.wait_ge(w_hi[1], FC * e + c + 1)
            nc.vector.tensor_tensor(w2p[:, c, 1, :, :], raw2[:, c % 2, :, :], w2p[:, c, 0, :, :].bitcast(F32),
                                    ALU.subtract).then_inc(w_lo[1], 1)

        with ExitStack() as s1:
            xn = sb("g_xn", [P, B, D], F32, s1)
            xT = sb("g_xT", [P, 2, DT, P], F32, s1)
            zero = sb("g_zero", [P, D], F32, s1)
            wg_sb = sb("g_wg", [P, DT, E], F32, s1)
            b1r = sb("g_b1", [P, P], F32, s1)
            b2r = sb("g_b2", [E * DT, P], F32, s1)
            veps = sb("g_veps", [P, B], F32, s1)
            std = sb("g_std", [P, B], F32, s1)
            rstd = sb("g_rstd", [P, B], F32, s1)
            before = sb("g_before", [P, P], F32, s1)
            ones = sb("g_ones", [P, P], F32, s1)
            e_no = sb("g_eno", [P, E], F32, s1)
            token = sb("g_token", [P, B], F32, s1)
            mx = sb("g_mx", [P, B], F32, s1)
            lm = sb("g_lm", [P, B, E], F32, s1)
            ex = sb("g_ex", [P, B, E], F32, s1)
            s_ = sb("g_s", [P, B], F32, s1)
            prob = sb("g_prob", [P, B], F32, s1)
            cand = sb("g_cand", [P, B, E], F32, s1)
            top = sb("g_top", [P, B], F32, s1)
            oh = sb("g_oh", [P, B, E], F32, s1)
            carry = sb("g_carry", [P, B, E], F32, s1)
            rk = sb("g_rk", [P, B, E], F32, s1)
            ro = sb("g_ro", [P, B, E], F32, s1)
            rank = sb("g_rank", [P, B], F32, s1)
            valid = sb("g_valid", [P, B], F32, s1)
            sl = sb("g_sl", [P, 4, B], F32, s1)
            pt = ps("g_pt", [P, 2, DT, P], F32, s1)
            pg = ps("g_pg", [P, B, E], F32, s1)
            pr = ps("g_pr", [P, B, E], F32, s1)
            pc = ps("g_pc", [P, B, E], F32, s1)
            pb = ps("g_pb", [P, P + E * DT], F32, s1)
            c_in, zeroed, zero_out = sem("g_c_in"), sem("g_zeroed"), sem("g_zero_out")
            step_done, var_ready, std_ready = sem("g_step"), sem("g_var"), sem("g_std")
            normed, turned, turned_out, gated = (sem(n) for n in ("g_normed", "g_turned", "g_tout", "g_gated"))
            shifted, exped, hot, counted = (sem(n) for n in ("g_shifted", "g_exped", "g_hot", "g_counted"))
            placed, sent, consts, b1_turned = (sem(n) for n in ("g_placed", "g_sent", "g_consts", "g_b1t"))
            block = s1.enter_context(nc.Block())

            @block.sync
            def _(sp):
                sp.dma_start(b1r[:, :], b1.rearrange("e (t p) -> (e t) p", p=P)).then_inc(c_in, 16)
                sp.dma_start(b2r[:, :], b2.rearrange("e (t p) -> (e t) p", p=P)).then_inc(c_in, 16)
                sp.dma_start(wg_sb[:, :, :], wg.rearrange("(t p) e -> p t e", p=P)).then_inc(c_in, 16)
                for c in range(2):
                    w1_load(sp, 0, c)
                for c in range(2):
                    w2_load(sp, 0, c)
                sp.wait_ge(zeroed, 1)
                rows = E * CAP
                for r in range(0, rows, P):
                    n = min(P, rows - r)
                    sp.dma_start(buf[r:r + n, :], zero[0:n, :]).then_inc(zero_out, 16)
                sp.wait_ge(zero_out, 16 * -(-rows // P))
                sp.wait_ge(c_in, 48)

            @block.gpsimd
            def _(pool):
                nc.gpsimd.memset(ones[:, :], 1.0).then_inc(consts, 1)
                pool.wait_ge(consts, 1)
                nc.gpsimd.affine_select(out=before[:, :], in_=ones[:, :], compare_op=ALU.is_gt, fill=0.0, base=0,
                                        pattern=[[1, P]], channel_multiplier=-1).then_inc(consts, 1)
                nc.gpsimd.iota(e_no[:, :], pattern=[[1, E]], base=-E, channel_multiplier=0,
                               allow_small_or_imprecise_dtypes=True).then_inc(consts, 1)
                nc.gpsimd.iota(token[:, :], pattern=[[P, B]], base=E * CAP, channel_multiplier=1,
                               allow_small_or_imprecise_dtypes=True).then_inc(consts, 1)
                pool.wait_ge(placed, 1)
                pool.wait_ge(zero_out, 16 * -(-(E * CAP) // P))
                for t in range(B):
                    nc.gpsimd.indirect_dma_start(buf[:, :], bass.IndirectOffsetOnAxis(ap=slot[:, t:t + 1], axis=0),
                                                 xn[:, t, :], None).then_inc(sent, 16)
                pool.wait_ge(sent, 16 * B)

            @block.vector
            def _(dve):
                step = chain(dve, step_done)
                nc.vector.memset(zero[:, :], 0.0).then_inc(zeroed, 1)
                nc.vector.tensor_scalar_add(veps[:, :], mv[:, :, 1], EPS).then_inc(var_ready, 1)
                dve.wait_ge(std_ready, 1)
                step(nc.vector.reciprocal(rstd[:, :], std[:, :]))
                for t in range(B):
                    nc.vector.tensor_scalar(xn[:, t, :], x2[:, t, :], mv[:, t, 0:1], rstd[:, t:t + 1],
                                            ALU.subtract, ALU.mult).then_inc(normed, 1)
                for n in range(4):
                    split1_lo(dve, 0, n)
                over = lambda a: a[:, :].unsqueeze(2).to_broadcast([P, B, E])
                dve.wait_ge(gated, B)
                dve.wait_ge(consts, 4)
                step(nc.vector.tensor_reduce(mx[:, :], pg[:, :, :], AX.X, ALU.max))
                nc.vector.tensor_tensor(lm[:, :, :], pg[:, :, :], over(mx), ALU.subtract).then_inc(shifted, 1)
                dve.wait_ge(shifted, 1)
                step(nc.vector.tensor_scalar(cand[:, :, :], lm[:, :, :], 0.0, None, ALU.is_lt))
                step(nc.vector.scalar_tensor_tensor(out=cand[:, :, :], in0=cand[:, :, :], scalar=float(E),
                                                    in1=e_no[:, :].unsqueeze(1).to_broadcast([P, B, E]),
                                                    op0=ALU.mult, op1=ALU.add))
                step(nc.vector.tensor_reduce(top[:, :], cand[:, :, :], AX.X, ALU.min))
                nc.vector.tensor_tensor(oh[:, :, :], e_no[:, :].unsqueeze(1).to_broadcast([P, B, E]), over(top),
                                        ALU.is_equal).then_inc(hot, 1)
                dve.wait_ge(counted, 1)
                step(nc.vector.memset(carry[:, 0, :], 0.0))
                for t in range(1, B):
                    step(nc.vector.tensor_tensor(carry[:, t, :], pc[:, t - 1, :], carry[:, t - 1, :], ALU.add))
                step(nc.vector.tensor_tensor(rk[:, :, :], pr[:, :, :], carry[:, :, :], ALU.add))
                step(nc.vector.tensor_tensor(ro[:, :, :], rk[:, :, :], oh[:, :, :], ALU.mult))
                step(nc.vector.tensor_reduce(rank[:, :], ro[:, :, :], AX.X, ALU.add))
                step(nc.vector.tensor_scalar(valid[:, :], rank[:, :], float(CAP), None, ALU.is_lt))
                step(nc.vector.tensor_scalar(sl[:, 0, :], top[:, :], float(E), float(CAP), ALU.add, ALU.mult))
                step(nc.vector.tensor_tensor(sl[:, 1, :], sl[:, 0, :], rank[:, :], ALU.add))
                step(nc.vector.tensor_tensor(sl[:, 2, :], sl[:, 1, :], token[:, :], ALU.subtract))
                step(nc.vector.tensor_tensor(sl[:, 3, :], sl[:, 2, :], valid[:, :], ALU.mult))
                step(nc.vector.tensor_tensor(sl[:, 0, :], sl[:, 3, :], token[:, :], ALU.add))
                nc.vector.tensor_copy(slot[:, :], sl[:, 0, :]).then_inc(placed, 1)
                dve.wait_ge(exped, 1)
                step(nc.vector.tensor_reduce(s_[:, :], ex[:, :, :], AX.X, ALU.add))
                step(nc.vector.reciprocal(prob[:, :], s_[:, :]))
                step(nc.vector.tensor_scalar(sl[:, 1, :], sl[:, 0, :], float(E * CAP - 1), None, ALU.min))
                step(nc.vector.tensor_copy(yslot[:, :], sl[:, 1, :]))
                step(nc.vector.tensor_tensor(weight[:, :], prob[:, :], valid[:, :], ALU.mult))
                for c in range(2):
                    split2_lo(dve, 0, c)

            @block.scalar
            def _(act):
                act.wait_ge(var_ready, 1)
                nc.scalar.activation(std[:, :], veps[:, :], ACT.Sqrt).then_inc(std_ready, 1)
                for t in range(B):
                    act.wait_ge(turned, t + 1)
                    if t >= 2:
                        act.wait_ge(gated, t - 1)
                    nc.scalar.copy(xT[:, t % 2, :, :], pt[:, t % 2, :, :]).then_inc(turned_out, 1)
                    if 2 <= t < 6:
                        split1_hi(act, 0, t - 2)
                    if t >= 6:
                        split2_hi(act, 0, t - 6)
                act.wait_ge(b1_turned, 1)
                nc.scalar.copy(b1T[:, :], pb[:, 0:P]).then_inc(turned_out, 1)
                nc.scalar.copy(b2T[:, :], pb[:, P:P + E * DT]).then_inc(turned_out, 1)
                act.wait_ge(shifted, 1)
                nc.scalar.activation(ex[:, :, :], lm[:, :, :], ACT.Exp).then_inc(exped, 1)

            @block.tensor
            def _(pe):
                pe.wait_ge(c_in, 48)

                def gate(t):
                    pe.wait_ge(turned_out, t + 1)
                    for c in range(DT):
                        last = nc.tensor.matmul(pg[:, t, :], xT[:, t % 2, c, :], wg_sb[:, c, :],
                                                start=c == 0, stop=c == DT - 1)
                    last.then_inc(gated, 1)
                for t in range(B):
                    pe.wait_ge(normed, t + 1)
                    if t >= 2:
                        pe.wait_ge(turned_out, t - 1)
                    for c in range(DT):
                        last = nc.tensor.transpose(pt[:, t % 2, c, :], xn[:, t, P * c:P * c + P], ident[:, :])
                    last.then_inc(turned, 1)
                    if t:
                        gate(t - 1)
                gate(B - 1)
                nc.tensor.transpose(pb[:, 0:P], b1r[:, :], ident[:, :])
                nc.tensor.transpose(pb[:, P:P + E * DT], b2r[:, :], ident[0:E * DT, 0:E * DT]).then_inc(b1_turned, 1)
                pe.wait_ge(hot, 1)
                pe.wait_ge(consts, 2)
                flat = oh[:, :, :].rearrange("p b e -> p (b e)")
                nc.tensor.matmul(pr[:, :, :].rearrange("p b e -> p (b e)"), before[:, :], flat, start=True, stop=True)
                nc.tensor.matmul(pc[:, :, :].rearrange("p b e -> p (b e)"), ones[:, :], flat,
                                 start=True, stop=True).then_inc(counted, 1)

        with ExitStack() as s2:
            eb = sb("f_eb", [P, 2, D], F32, s2)
            xe = sb("f_xe", [P, DT, 2, CAPP], F32R, s2)
            mixed = sb("f_mixed", [P, 2, 2, CAPP], F32, s2)
            pre = sb("f_pre", [P, 2, 2, CAPP], F32, s2)
            h32 = sb("f_h32", [P, 2, 2, CAPP], F32, s2)
            hp = sb("f_h", [P, NF, 2, CAPP], F32R, s2)
            ymix = sb("f_ymix", [P, DT, CAPP], F32, s2)
            yT = sb("f_yT", [P, DT, CAPP], F32, s2)
            y = sb("f_y", [P, 2, D], F32, s2)
            ph = ps("f_ph", [P, 4, 512], F32, s2)
            py = ps("f_py", [P, DT, 512], F32, s2)
            eb_in, y_out = sem("f_eb_in"), sem("f_y_out")
            xt, x_hi, x_lo = sem("f_xt"), sem("f_x_hi"), sem("f_x_lo")
            up, up_mixed, up_sum = sem("f_up"), sem("f_up_mixed"), sem("f_up_sum")
            gelus, h_hi, h_lo = sem("f_gelus"), sem("f_h_hi"), sem("f_h_lo")
            down, y_mixed, y_sum = sem("f_down"), sem("f_y_mixed"), sem("f_y_sum")
            y_back, y_first, y_second = sem("f_y_back"), sem("f_y_first"), sem("f_y_second")
            padded = sem("f_padded")
            w2_late = sem("f_w2_late")
            block = s2.enter_context(nc.Block())

            def lo_ready(eng, e, c):
                if c < 2:
                    eng.wait_ge(w_lo[1], 2 * e + c + 1)
                else:
                    eng.wait_ge(w2_late, 2 * e + c - 1)

            def up_banks(n):
                return (ph, py)[n // 2 % 2][:, 2 * (n % 2):2 * (n % 2) + 2, :]

            def each_expert(eng, body):
                body(0, True, False)
                with eng.Fori(1, E - 1) as e:
                    body(e, False, False)
                body(E - 1, False, True)

            @block.sync
            def _(sp):
                def rows_load(e):
                    sp.dma_start(eb[:, 0, :], buf[bass.ds(e * CAP, P), :]).then_inc(eb_in, 16)
                    sp.dma_start(eb[0:OVER, 1, :], buf[bass.ds(e * CAP + P, OVER), :]).then_inc(eb_in, 16)

                def store(e):
                    sp.wait_ge(y_first, e + 1)
                    sp.dma_start(ybuf[bass.ds(e * CAP, P), :], y[:, 0, :]).then_inc(y_out, 16)
                    sp.wait_ge(y_second, e + 1)
                    sp.dma_start(ybuf[bass.ds(e * CAP + P, OVER), :], y[0:OVER, 1, :]).then_inc(y_out, 16)

                def body(e, first, final):
                    if not final:
                        sp.wait_ge(xt, e + 1)
                        rows_load(e + 1)
                    if not first:
                        store(e - 1)
                    if not final:
                        for c in range(2):
                            sp.wait_ge(w_lo[0], PAIRS * e + 2 * c + 6)
                            w1_load(sp, e + 1, c)
                        for c in range(2):
                            lo_ready(sp, e, c + 2)
                            w2_load(sp, e + 1, c)
                        for c in range(2):
                            sp.wait_ge(w_lo[0], PAIRS * e + PAIRS + 2 * c + 2)
                            w1_load(sp, e + 1, c + 2)
                        for c in range(2):
                            lo_ready(sp, e + 1, c)
                            w2_load(sp, e + 1, c + 2)
                rows_load(0)
                for c in range(2):
                    sp.wait_ge(w_lo[0], 2 * c + 2)
                    w1_load(sp, 0, c + 2)
                for c in range(2):
                    sp.wait_ge(w_lo[1], c + 1)
                    w2_load(sp, 0, c + 2)
                each_expert(sp, body)
                store(E - 1)
                sp.wait_ge(y_out, 32 * E + 32)

            @block.tensor
            def _(pe):
                def product(out, hi, lo, rows, start, stop):
                    nc.tensor.matmul(out[:, 0:2 * CAPP], hi, rows.rearrange("p n s -> p (n s)"), start=start, stop=False)
                    return nc.tensor.matmul(out[:, CAPP:2 * CAPP], lo, rows[:, 0, :], start=False, stop=stop)

                def rows_turn(e):
                    pe.wait_ge(eb_in, 32 * e + 32)
                    for c in range(DT):
                        nc.tensor.transpose(ph[:, c, 0:P], eb[:, 0, P * c:P * c + P], ident[:, :])
                        last = nc.tensor.transpose(ph[:, c, P:CAP], eb[0:OVER, 1, P * c:P * c + P], ident[0:OVER, 0:OVER])
                    last.then_inc(xt, 1)

                def results_turn(e):
                    pe.wait_ge(y_sum, 2 * e + 2)
                    for c in range(DT):
                        nc.tensor.transpose(py[:, 2, P * c:P * c + P], yT[:, c, 0:P], ident[:, :])
                        last = nc.tensor.transpose(py[0:OVER, 3, P * c:P * c + P], yT[:, c, P:CAP], ident[:, :])
                    last.then_inc(y_back, 1)

                def body(e, first, final):
                    pe.wait_ge(x_lo, e + 1)
                    for n in range(PAIRS):
                        pe.wait_ge(w_lo[0], PAIRS * e + n + 1)
                        if n >= 4:
                            pe.wait_ge(up_sum, PAIRS * e + n - 3)
                        if n == 3 and not first:
                            pe.wait_ge(y_first, e)
                            pe.wait_ge(y_second, e)
                        for t in range(2):
                            f = 2 * n + t
                            for k in range(DT):
                                cols = slice(P * (f % 4), P * (f % 4) + P)
                                last = product(up_banks(n)[:, t, :], w1p[:, n // 2 % 2, 0, k, cols],
                                               w1p[:, n // 2 % 2, 1, k, cols], xe[:, k, :, :], k == 0, k == DT - 1)
                        last.then_inc(up, 1)
                        if n == 0 and not first:
                            results_turn(e - 1)
                    if not final:
                        pe.wait_ge(up_sum, PAIRS * e + PAIRS - 2)
                        rows_turn(e + 1)
                    for c in range(FC):
                        lo_ready(pe, e, c)
                        pe.wait_ge(h_lo, PAIRS * e + 2 * c + 4)
                        for d in range(DT):
                            if c == 0 and d % 2 == 0:
                                pe.wait_ge(up_sum, PAIRS * e + PAIRS - 1 + d // 2)
                            for k in range(4):
                                cols = slice(P * d, P * d + P)
                                last = product(py[:, d, :], w2p[:, c, 0, k, cols], w2p[:, c, 1, k, cols],
                                               hp[:, 4 * c + k, :, :], c + k == 0, c == FC - 1 and k == 3)
                        last.then_inc(down, 1)
                rows_turn(0)
                pe.wait_ge(padded, 1)
                each_expert(pe, body)
                results_turn(E - 1)

            @block.scalar
            def _(act):
                def rows_hi(e):
                    act.wait_ge(xt, e + 1)
                    nc.scalar.copy(xe[:, :, 0, 0:CAP], ph[:, :, 0:CAP]).then_inc(x_hi, 1)

                def results_out(e):
                    act.wait_ge(y_back, e + 1)
                    act.wait_ge(y_out, 32 * e + 32)
                    nc.scalar.copy(y[:, 0, :], py[:, 2, :]).then_inc(y_first, 1)

                def body(e, first, final):
                    for n in range(PAIRS + 1):
                        if n < PAIRS:
                            act.wait_ge(up, PAIRS * e + n + 1)
                            nc.scalar.copy(mixed[:, n % 2, :, :], up_banks(n)[:, :, CAPP:2 * CAPP]).then_inc(up_mixed, 1)
                        if n == 0 and not first:
                            results_out(e - 1)
                        if n:
                            m = n - 1
                            act.wait_ge(up_sum, PAIRS * e + m + 1)
                            if m >= 2 or not first:
                                act.wait_ge(h_lo, PAIRS * e + m + 1)
                            for t in range(2):
                                last = nc.scalar.activation(h32[:, m % 2, t, :], pre[:, m % 2, t, :], ACT.Gelu,
                                                            bias=b1T[:, bass.ds(e * NF + 2 * m + t, 1)])
                            last.then_inc(gelus, 1)
                        if n < 4:
                            split1_hi(act, e, n + 4)
                        if n in (4, 6):
                            split2_hi(act, e, n // 2)
                    if not final:
                        rows_hi(e + 1)
                        for n in range(4):
                            split1_hi(act, e + 1, n)
                        for c in range(2):
                            act.wait_ge(down, FC * e + c + 1)
                            split2_hi(act, e + 1, c)
                    act.wait_ge(down, FC * e + FC)
                    for d in range(DT):
                        last = nc.scalar.activation(ymix[:, d, :], py[:, d, CAPP:2 * CAPP], ACT.Identity,
                                                    bias=b2T[:, bass.ds(e * DT + d, 1)])
                        if d % 2:
                            last.then_inc(y_mixed, 1)
                rows_hi(0)
                each_expert(act, body)
                results_out(E - 1)

            @block.gpsimd
            def _(pool):
                def body(e, first, final):
                    for c in range(2, FC):
                        pool.wait_ge(w_hi[1], FC * e + c + 1)
                        nc.gpsimd.tensor_tensor(w2p[:, c, 1, :, :], raw2[:, c % 2, :, :],
                                                w2p[:, c, 0, :, :].bitcast(F32), ALU.subtract).then_inc(w2_late, 1)
                each_expert(pool, body)

            @block.vector
            def _(dve):
                def rows_lo(e):
                    dve.wait_ge(x_hi, e + 1)
                    nc.vector.tensor_tensor(xe[:, :, 1, 0:CAP], ph[:, :, 0:CAP], xe[:, :, 0, 0:CAP].bitcast(F32),
                                            ALU.subtract).then_inc(x_lo, 1)

                def results_out(e):
                    dve.wait_ge(y_back, e + 1)
                    dve.wait_ge(y_out, 32 * e + 32)
                    nc.vector.tensor_copy(y[0:OVER, 1, :], py[0:OVER, 3, :]).then_inc(y_second, 1)

                def body(e, first, final):
                    for n in range(PAIRS + 1):
                        if n < PAIRS:
                            dve.wait_ge(up_mixed, PAIRS * e + n + 1)
                            nc.vector.tensor_tensor(pre[:, n % 2, :, :], up_banks(n)[:, :, 0:CAPP], mixed[:, n % 2, :, :],
                                                    ALU.add).then_inc(up_sum, 1)
                        if n == 0 and not first:
                            results_out(e - 1)
                        if n:
                            m = n - 1
                            dve.wait_ge(gelus, PAIRS * e + m + 1)
                            nc.vector.tensor_copy(hp[:, 2 * m:2 * m + 2, 0, :], h32[:, m % 2, :, :]).then_inc(h_hi, 1)
                            dve.wait_ge(h_hi, PAIRS * e + m + 1)
                            nc.vector.tensor_tensor(hp[:, 2 * m:2 * m + 2, 1, :], h32[:, m % 2, :, :],
                                                    hp[:, 2 * m:2 * m + 2, 0, :].bitcast(F32), ALU.subtract).then_inc(h_lo, 1)
                        if n < 4:
                            split1_lo(dve, e, n + 4)
                    if not final:
                        rows_lo(e + 1)
                        for n in range(4):
                            split1_lo(dve, e + 1, n)
                        for c in range(2):
                            split2_lo(dve, e + 1, c)
                    for a in range(2):
                        dve.wait_ge(y_mixed, 2 * e + a + 1)
                        nc.vector.tensor_tensor(yT[:, 2 * a:2 * a + 2, :], py[:, 2 * a:2 * a + 2, 0:CAPP],
                                                ymix[:, 2 * a:2 * a + 2, :], ALU.add).then_inc(y_sum, 1)
                dve.sem_inc(y_out, 32)
                dve.sem_inc(h_lo, 2)
                nc.vector.memset(xe[:, :, :, CAP:CAPP].bitcast(F32), 0.0).then_inc(padded, 1)
                rows_lo(0)
                each_expert(dve, body)
                results_out(E - 1)

        with ExitStack() as s3:
            yg = sb("h_y", [P, B, D], F32, s3)
            o = sb("h_o", [P, B, D], F32, s3)
            done, out_done = sem("h_done"), sem("h_out")
            block = s3.enter_context(nc.Block())

            @block.gpsimd
            def _(pool):
                for t in range(B):
                    nc.gpsimd.indirect_dma_start(yg[:, t, :], None, ybuf[:, :],
                                                 bass.IndirectOffsetOnAxis(ap=yslot[:, t:t + 1], axis=0)).then_inc(backs[t], 16)
                for t in range(B):
                    pool.wait_ge(backs[t], 16)

            @block.vector
            def _(dve):
                for t in range(B):
                    dve.wait_ge(backs[t], 16)
                    nc.vector.scalar_tensor_tensor(out=o[:, t, :], in0=yg[:, t, :], scalar=weight[:, t:t + 1],
                                                   in1=x2[:, t, :], op0=ALU.mult, op1=ALU.add).then_inc(done, 1)

            @block.sync
            def _(sp):
                for t in range(B):
                    sp.wait_ge(done, t + 1)
                    sp.dma_start(out[t, :, :], o[:, t, :]).then_inc(out_done, 16)
                sp.wait_ge(out_done, 16 * B)


def perceiver(nc, x, ctx_1024, xWq, xbq, xWk, xbk, xWv, xbv, xWo, xbo, aWq, abq, aWk, abk, aWv, abv, aWo, abo,
              wg, W1, b1, W2, b2, out):
    scratch = lambda name, shape: nc.dram_tensor(name, shape, F32, kind="Internal").ap()
    wk_split = scratch("wk_split", [2, P, DT, XH * DK])
    wv_split = scratch("wv_split", [2, P, DT, XH * DK])
    q_split = scratch("q_split", [XH * DK, B, 2, P])
    o_parts = scratch("o_parts", [B, XH, P, P])
    row_scale = scratch("row_scale", [B, P, XH])
    buf = scratch("expert_rows", [E * CAP + TOK, D])
    ybuf = scratch("expert_results", [E * CAP, D])
    used = []
    with nc.sbuf_tensor("ident", [P, P], F32) as ident:
        prepare(nc, x, xWq, xbq, xWk, xWv, ident, wk_split, wv_split, q_split, used)
        cross_attention(nc, ctx_1024, wk_split, wv_split, q_split, xbk, ident, o_parts, row_scale, used)
        with nc.sbuf_tensor("x12", [P, B, D], F32) as x12, nc.sbuf_tensor("x2_mv", [P, B, 2], F32) as mv:
            self_attention(nc, x, xWo, xbv, xbo, o_parts, row_scale, aWq, abq, aWk, abk, aWv, abv, aWo, abo, ident, x12, mv, used)
            nc.clear_and_free_semaphores(used)
            nc.all_engine_barrier()
            used = []
            experts(nc, x12, mv, wg, W1, b1, W2, b2, ident, buf, ybuf, out, used)


_INS = ["x", "ctx_1024", "L0_xattn_Wq", "L0_xattn_bq", "L0_xattn_Wk", "L0_xattn_bk", "L0_xattn_Wv", "L0_xattn_bv",
        "L0_xattn_Wo", "L0_xattn_bo", "L0_attn_Wq", "L0_attn_bq", "L0_attn_Wk", "L0_attn_bk", "L0_attn_Wv",
        "L0_attn_bv", "L0_attn_Wo", "L0_attn_bo", "L0_ffn_wg", "L0_ffn_W1", "L0_ffn_b1", "L0_ffn_W2", "L0_ffn_b2"]


def kernel(**inputs):
    import numpy as np
    import concourse.bacc as bacc
    from concourse.bass_utils import run_bass_kernel_spmd

    nc = bacc.Bacc("TRN2", target_bir_lowering=False, num_devices=1)
    arrays, args = {}, []
    for name in _INS:
        a = np.ascontiguousarray(inputs[name])
        arrays[f"in_{name}"] = a
        args.append(nc.dram_tensor(f"in_{name}", a.shape, mybir.dt.from_np(a.dtype), kind="ExternalInput").ap())
    out = nc.dram_tensor("out_0", (B, P, D), F32, kind="ExternalOutput").ap()
    perceiver(nc, *args, out)
    r = run_bass_kernel_spmd(nc, [arrays], core_ids=[0])
    return r.results[0]["out_0"]
```
